# Optimizing a Trainium2 kernel written in Bass

```python
import numpy as np
import jax
import jax.numpy as jnp

def _softmax(x, axis=-1):
    return jax.nn.softmax(x, axis=axis)

def _gelu(x):
    return jax.nn.gelu(x, approximate=True)

def _silu(x):
    return jax.nn.silu(x)

def _sigmoid(x):
    return jax.nn.sigmoid(x)

def _layernorm(x, axis=-1, eps=1e-05):
    m = jnp.mean(x, axis=axis, keepdims=True)
    v = jnp.var(x, axis=axis, keepdims=True)
    return (x - m) / jnp.sqrt(v + eps)

def _scatter_add(tgt, idx, src, axis=0):
    return tgt.at[idx].add(src)

def _segment_sum(src, seg, n):
    return jax.ops.segment_sum(src, seg, n)
kernel_name = 'mk_hybrid_d1_jaxref_r4_6f4303'

def setup_inputs(seed: int=0):
    np.random.seed(seed)
    _w = jnp.asarray

    def _L0_attn_a_setup():
        import jax, jax.numpy as jnp
        import numpy as np
        B, S, DIM = (4, 1024, 256)
        ERR_CLIP = 5.0
        GRAD_CLIP = 1.0
        INIT_STD = 0.02

        def _silu_deriv(x):
            s = jax.nn.sigmoid(x)
            return s * (1.0 + x * (1.0 - s))

        def _forward(x, Wk, Wv, Wq, Wout, W0, W1, Wg_decay, bg_decay, Wg_lr, bg_lr, Wg_mom, bg_mom):
            k = x @ Wk.T
            v = x @ Wv.T
            q = x @ Wq.T
            alpha = jax.nn.sigmoid(jnp.mean(x @ Wg_decay.T + bg_decay))
            lr = jax.nn.sigmoid(jnp.mean(x @ Wg_lr.T + bg_lr))
            eta = jax.nn.sigmoid(jnp.mean(x @ Wg_mom.T + bg_mom))
            W0d = jax.lax.stop_gradient(W0)
            W1d = jax.lax.stop_gradient(W1)
            pre1 = k @ W0d.T
            a1 = jax.nn.silu(pre1)
            pred = a1 @ W1d.T
            scale = 2.0 / float(S)
            err = jnp.clip(pred - v, -ERR_CLIP, ERR_CLIP)
            d2 = scale * err
            g1 = jnp.clip(jnp.einsum('bsd,bse->de', d2, a1), -GRAD_CLIP, GRAD_CLIP)
            d1 = d2 @ W1d * _silu_deriv(pre1)
            g0 = jnp.clip(jnp.einsum('bsd,bse->de', d1, k), -GRAD_CLIP, GRAD_CLIP)
            m0 = eta * jnp.zeros_like(W0) - lr * g0
            m1 = eta * jnp.zeros_like(W1) - lr * g1
            W0n = (1.0 - alpha) * W0 + m0
            W1n = (1.0 - alpha) * W1 + m1
            h = jax.nn.silu(q @ W0n.T) @ W1n.T
            return h @ Wout.T
        key = jax.random.key(seed)
        ks = jax.random.split(key, 10)
        fan = 1.0 / np.sqrt(DIM)
        return {'x': jax.random.normal(ks[0], (B, S, DIM), jnp.float32), 'Wk': jax.random.normal(ks[1], (DIM, DIM), jnp.float32) * INIT_STD, 'Wv': jax.random.normal(ks[2], (DIM, DIM), jnp.float32) * INIT_STD, 'Wq': jax.random.normal(ks[3], (DIM, DIM), jnp.float32) * INIT_STD, 'Wout': jax.random.normal(ks[4], (DIM, DIM), jnp.float32) * INIT_STD, 'W0': jax.random.normal(ks[5], (DIM, DIM), jnp.float32) * fan, 'W1': jax.random.normal(ks[6], (DIM, DIM), jnp.float32) * fan, 'Wg_decay': jax.random.normal(ks[7], (1, DIM), jnp.float32) * INIT_STD, 'bg_decay': jnp.full((1,), -4.0, jnp.float32), 'Wg_lr': jax.random.normal(ks[8], (1, DIM), jnp.float32) * INIT_STD, 'bg_lr': jnp.zeros((1,), jnp.float32), 'Wg_mom': jax.random.normal(ks[9], (1, DIM), jnp.float32) * INIT_STD, 'bg_mom': jnp.zeros((1,), jnp.float32)}
    _L0_attn_a_in = _L0_attn_a_setup()

    def _L0_attn_b_setup():
        import math
        import jax, jax.numpy as jnp
        import numpy as np
        D_MODEL = 256
        N_HEADS = 16
        D_K = D_MODEL // N_HEADS
        D_C = 64
        B, S = (2, 512)
        key = jax.random.key(seed)
        ks = jax.random.split(key, 7)
        sd = lambda fan_in: 1.0 / math.sqrt(fan_in)
        return {'x': jax.random.normal(ks[0], (B, S, D_MODEL), dtype=jnp.float32), 'W_dq': jax.random.uniform(ks[1], (D_MODEL, D_C), minval=-sd(D_MODEL), maxval=sd(D_MODEL), dtype=jnp.float32), 'W_uq': jax.random.uniform(ks[2], (D_C, N_HEADS * D_K), minval=-sd(D_C), maxval=sd(D_C), dtype=jnp.float32), 'W_dkv': jax.random.uniform(ks[3], (D_MODEL, D_C), minval=-sd(D_MODEL), maxval=sd(D_MODEL), dtype=jnp.float32), 'W_uk': jax.random.uniform(ks[4], (D_C, N_HEADS * D_K), minval=-sd(D_C), maxval=sd(D_C), dtype=jnp.float32), 'W_uv': jax.random.uniform(ks[5], (D_C, N_HEADS * D_K), minval=-sd(D_C), maxval=sd(D_C), dtype=jnp.float32), 'W_o': jax.random.uniform(ks[6], (N_HEADS * D_K, D_MODEL), minval=-sd(N_HEADS * D_K), maxval=sd(N_HEADS * D_K), dtype=jnp.float32)}
    _L0_attn_b_in = _L0_attn_b_setup()

    def _L0_ffn_setup():
        import jax, jax.numpy as jnp
        import numpy as np
        TOPK = 8
        BN_EPS = 1e-05
        key = jax.random.key(seed)
        ks = jax.random.split(key, 5)
        b, n, d = (2, 256, 256)
        h, nk, kd = (8, 64, 128)
        ne = nk * nk
        scale = 0.02
        return {'inputs': jax.random.normal(ks[0], (b, n, d), jnp.float32), 'gamma': jnp.ones((d,), jnp.float32), 'beta': jnp.zeros((d,), jnp.float32), 'w_q': jax.random.normal(ks[1], (2 * h * kd, d), jnp.float32) * scale, 'keys': jax.random.normal(ks[2], (h, nk, 2, kd), jnp.float32) * scale, 'key_in': jax.random.normal(ks[3], (ne, d), jnp.float32) * scale, 'key_out': jax.random.normal(ks[4], (ne, d), jnp.float32) * scale}
    _L0_ffn_in = _L0_ffn_setup()
    _d = {'L0_attn_a_x': _L0_attn_a_in['x'], 'L0_attn_a_Wk': _L0_attn_a_in['Wk'], 'L0_attn_a_Wv': _L0_attn_a_in['Wv'], 'L0_attn_a_Wq': _L0_attn_a_in['Wq'], 'L0_attn_a_Wout': _L0_attn_a_in['Wout'], 'L0_attn_a_W0': _L0_attn_a_in['W0'], 'L0_attn_a_W1': _L0_attn_a_in['W1'], 'L0_attn_a_Wg_decay': _L0_attn_a_in['Wg_decay'], 'L0_attn_a_bg_decay': _L0_attn_a_in['bg_decay'], 'L0_attn_a_Wg_lr': _L0_attn_a_in['Wg_lr'], 'L0_attn_a_bg_lr': _L0_attn_a_in['bg_lr'], 'L0_attn_a_Wg_mom': _L0_attn_a_in['Wg_mom'], 'L0_attn_a_bg_mom': _L0_attn_a_in['bg_mom'], 'L0_attn_b_W_dq': _L0_attn_b_in['W_dq'], 'L0_attn_b_W_uq': _L0_attn_b_in['W_uq'], 'L0_attn_b_W_dkv': _L0_attn_b_in['W_dkv'], 'L0_attn_b_W_uk': _L0_attn_b_in['W_uk'], 'L0_attn_b_W_uv': _L0_attn_b_in['W_uv'], 'L0_attn_b_W_o': _L0_attn_b_in['W_o'], 'L0_ffn_gamma': _L0_ffn_in['gamma'], 'L0_ffn_beta': _L0_ffn_in['beta'], 'L0_ffn_w_q': _L0_ffn_in['w_q'], 'L0_ffn_keys': _L0_ffn_in['keys'], 'L0_ffn_key_in': _L0_ffn_in['key_in'], 'L0_ffn_key_out': _L0_ffn_in['key_out']}
    _x0 = _d['L0_attn_a_x']
    _d['L0_attn_a_x'] = jax.random.normal(jax.random.fold_in(jax.random.key(seed), 1), (2, 2048, 256), dtype=_x0.dtype)
    del _x0
    return _d

def reference(L0_attn_a_x, L0_attn_a_Wk, L0_attn_a_Wv, L0_attn_a_Wq, L0_attn_a_Wout, L0_attn_a_W0, L0_attn_a_W1, L0_attn_a_Wg_decay, L0_attn_a_bg_decay, L0_attn_a_Wg_lr, L0_attn_a_bg_lr, L0_attn_a_Wg_mom, L0_attn_a_bg_mom, L0_attn_b_W_dq, L0_attn_b_W_uq, L0_attn_b_W_dkv, L0_attn_b_W_uk, L0_attn_b_W_uv, L0_attn_b_W_o, L0_ffn_gamma, L0_ffn_beta, L0_ffn_w_q, L0_ffn_keys, L0_ffn_key_in, L0_ffn_key_out):

    def _L0_attn_a_ref(x, Wk, Wv, Wq, Wout, W0, W1, Wg_decay, bg_decay, Wg_lr, bg_lr, Wg_mom, bg_mom):
        import jax, jax.numpy as jnp
        import numpy as np
        B, S, DIM = (4, 1024, 256)
        ERR_CLIP = 5.0
        GRAD_CLIP = 1.0
        INIT_STD = 0.02

        def _silu_deriv(x):
            s = jax.nn.sigmoid(x)
            return s * (1.0 + x * (1.0 - s))

        def _forward(x, Wk, Wv, Wq, Wout, W0, W1, Wg_decay, bg_decay, Wg_lr, bg_lr, Wg_mom, bg_mom):
            k = x @ Wk.T
            v = x @ Wv.T
            q = x @ Wq.T
            alpha = jax.nn.sigmoid(jnp.mean(x @ Wg_decay.T + bg_decay))
            lr = jax.nn.sigmoid(jnp.mean(x @ Wg_lr.T + bg_lr))
            eta = jax.nn.sigmoid(jnp.mean(x @ Wg_mom.T + bg_mom))
            W0d = jax.lax.stop_gradient(W0)
            W1d = jax.lax.stop_gradient(W1)
            pre1 = k @ W0d.T
            a1 = jax.nn.silu(pre1)
            pred = a1 @ W1d.T
            scale = 2.0 / float(S)
            err = jnp.clip(pred - v, -ERR_CLIP, ERR_CLIP)
            d2 = scale * err
            g1 = jnp.clip(jnp.einsum('bsd,bse->de', d2, a1), -GRAD_CLIP, GRAD_CLIP)
            d1 = d2 @ W1d * _silu_deriv(pre1)
            g0 = jnp.clip(jnp.einsum('bsd,bse->de', d1, k), -GRAD_CLIP, GRAD_CLIP)
            m0 = eta * jnp.zeros_like(W0) - lr * g0
            m1 = eta * jnp.zeros_like(W1) - lr * g1
            W0n = (1.0 - alpha) * W0 + m0
            W1n = (1.0 - alpha) * W1 + m1
            h = jax.nn.silu(q @ W0n.T) @ W1n.T
            return h @ Wout.T
        return _forward(x, Wk, Wv, Wq, Wout, W0, W1, Wg_decay, bg_decay, Wg_lr, bg_lr, Wg_mom, bg_mom)

    def _L0_attn_b_ref(x, W_dq, W_uq, W_dkv, W_uk, W_uv, W_o):
        import math
        import jax, jax.numpy as jnp
        import numpy as np
        D_MODEL = 256
        N_HEADS = 16
        D_K = D_MODEL // N_HEADS
        D_C = 64
        B, S = (2, 512)
        Bx, Sx, _ = x.shape
        c_q = x @ W_dq
        Q = (c_q @ W_uq).reshape(Bx, Sx, N_HEADS, D_K)
        c_kv = x @ W_dkv
        K = (c_kv @ W_uk).reshape(Bx, Sx, N_HEADS, D_K)
        V = (c_kv @ W_uv).reshape(Bx, Sx, N_HEADS, D_K)
        scores = jnp.einsum('bqhd,bkhd->bhqk', Q, K) / math.sqrt(D_K)
        causal = jnp.tril(jnp.ones((Sx, Sx), dtype=bool))
        scores = jnp.where(causal, scores, -jnp.inf)
        attn = jax.nn.softmax(scores, axis=-1)
        out = jnp.einsum('bhqk,bkhd->bqhd', attn, V).reshape(Bx, Sx, N_HEADS * D_K)
        return out @ W_o

    def _L0_ffn_ref(inputs, gamma, beta, w_q, keys, key_in, key_out):
        import jax, jax.numpy as jnp
        import numpy as np
        TOPK = 8
        BN_EPS = 1e-05
        b, n, d = inputs.shape
        h, nk, _, kd = keys.shape
        k = TOPK
        x = inputs.reshape(b * n, d)
        mu = jnp.mean(x, axis=0)
        var = jnp.mean(jnp.square(x - mu), axis=0)
        xn = (x - mu) * jax.lax.rsqrt(var + BN_EPS) * gamma + beta
        q = (xn @ w_q.T).reshape(b, n, 2, h, kd).transpose(2, 0, 1, 3, 4)
        sim = jnp.einsum('pbnhd,hkpd->pbnhk', q, keys)
        s, i = jax.lax.top_k(sim, k)
        sx, sy = (s[0], s[1])
        ix, iy = (i[0], i[1])
        all_scores = (sx[..., :, None] + sy[..., None, :]).reshape(b, n, h, k * k)
        all_idx = (ix[..., :, None] * nk + iy[..., None, :]).reshape(b, n, h, k * k)
        scores, pk = jax.lax.top_k(all_scores, k)
        idx = jnp.take_along_axis(all_idx, pk, axis=-1)
        w_down = key_in[idx]
        w_up = key_out[idx]
        o = jnp.einsum('bnd,bnhkd->bnhk', inputs, w_down)
        o = jax.nn.gelu(o, approximate=False) * jax.nn.softmax(scores, axis=-1)
        return jnp.einsum('bnhk,bnhkd->bnd', o, w_up)
    x = L0_attn_a_x
    x = x + _L0_attn_a_ref(_layernorm(x, axis=-1), L0_attn_a_Wk, L0_attn_a_Wv, L0_attn_a_Wq, L0_attn_a_Wout, L0_attn_a_W0, L0_attn_a_W1, L0_attn_a_Wg_decay, L0_attn_a_bg_decay, L0_attn_a_Wg_lr, L0_attn_a_bg_lr, L0_attn_a_Wg_mom, L0_attn_a_bg_mom)
    x = x + _L0_ffn_ref(_layernorm(x, axis=-1), L0_ffn_gamma, L0_ffn_beta, L0_ffn_w_q, L0_ffn_keys, L0_ffn_key_in, L0_ffn_key_out)
    x = x + _L0_attn_b_ref(_layernorm(x, axis=-1), L0_attn_b_W_dq, L0_attn_b_W_uq, L0_attn_b_W_dkv, L0_attn_b_W_uk, L0_attn_b_W_uv, L0_attn_b_W_o)
    x = x + _L0_ffn_ref(_layernorm(x, axis=-1), L0_ffn_gamma, L0_ffn_beta, L0_ffn_w_q, L0_ffn_keys, L0_ffn_key_in, L0_ffn_key_out)
    return x

_drawn_inputs = setup_inputs


def setup_inputs(seed=0):
    import zlib

    import numpy as np

    out = dict(_drawn_inputs(seed))
    spreads = {'L0_ffn_gamma': (1.0, 0.6), 'L0_ffn_beta': (0.0, 0.8)}
    factors = {'L0_attn_a_Wg_decay': 200.0,
     'L0_attn_a_Wg_lr': 8.0,
     'L0_attn_b_W_dq': 8.0,
     'L0_attn_b_W_uq': 8.0,
     'L0_attn_b_W_dkv': 4.65,
     'L0_attn_b_W_uk': 8.0,
     'L0_attn_b_W_uv': 4.589,
     'L0_attn_b_W_o': 4.653,
     'L0_ffn_w_q': 8.0,
     'L0_ffn_keys': 8.0,
     'L0_ffn_key_in': 8.0,
     'L0_ffn_key_out': 8.0}
    for name, (base, spread) in spreads.items():
        noise = np.random.default_rng([zlib.crc32(name.encode()), seed]).standard_normal(out[name].shape)
        drawn = base * np.exp(spread * noise) if base else spread * noise
        out[name] = jnp.asarray(drawn.astype(out[name].dtype))
    for name, factor in factors.items():
        out[name] = (out[name] * factor).astype(out[name].dtype)
    return out
```

```python
from contextlib import ExitStack

import concourse.bass as bass
from concourse import mybir

F32, F16, BF16 = mybir.dt.float32, mybir.dt.float16, mybir.dt.bfloat16
U16 = mybir.dt.uint16
ALU, ACT, AX = mybir.AluOpType, mybir.ActivationFunctionType, mybir.AxisListType

P = 128
D = 256
DH = D // P
BATCH, SEQ = 2, 2048
T = BATCH * SEQ
BLK = 512
BT = BLK // P
NBLK = T // BLK
CH = 256
NCH = T // CH
LN_EPS = 1e-5


class Chain:

    def __init__(self, eng, sem, base=0):
        self.eng, self.sem, self.base, self.n = eng, sem, base, 0

    def mark(self, ins):
        self.n += 1
        return ins.then_inc(self.sem, 1)

    def wait(self):
        self.eng.wait_ge(self.sem, self.base + self.n)

    def link(self, ins):
        self.mark(ins)
        self.wait()


def layer_norm_rows(nc, dve, chain, x, y, stats, mv, var_eps, rstd, tmp, gate, var_ready, root_ready, n_root):
    for t in range(BT):
        chain.mark(nc.vector.bn_stats(stats[:, t, :], x[:, t, :]))
    chain.wait()
    nc.vector.memset(gate[:], 0.0)
    for t in range(BT):
        chain.mark(nc.vector.bn_aggr(mv[:, t, :], stats[:, t, :]))
    chain.wait()
    nc.vector.tensor_scalar_add(var_eps[:], mv[:, :, 1], LN_EPS).then_inc(var_ready, 1)
    dve.wait_ge(root_ready, n_root)
    newton_reciprocal(nc, chain, rstd, rstd, var_eps, tmp)
    for t in range(BT):
        last = nc.vector.tensor_scalar(y[:, t, :], x[:, t, :], mv[:, t, 0:1], rstd[:, t:t + 1],
                                       ALU.subtract, ALU.mult)
    return last


def newton_reciprocal(nc, chain, out, root, var_eps, tmp):
    chain.link(nc.vector.reciprocal(out[:], root[:]))
    chain.link(nc.vector.tensor_tensor(tmp[:], out[:], out[:], ALU.mult))
    chain.link(nc.vector.tensor_tensor(tmp[:], tmp[:], var_eps[:], ALU.mult))
    chain.link(nc.vector.tensor_scalar(tmp[:], tmp[:], -0.5, 1.5, ALU.mult, ALU.add))
    chain.link(nc.vector.tensor_tensor(out[:], out[:], tmp[:], ALU.mult))


LN_LINKS = BT + BT + 5


def layer_norm_pass(nc, sem, tag, x_dram, xt_dram, ident_dram, feature_stats, xln_dram=None, prefetch=None):
    with ExitStack() as ctx:
        def sb(name, shape, dt=F32):
            return ctx.enter_context(nc.sbuf_tensor(tag + name, shape, dt))

        ident = sb("ident", [P, P])
        xin = [sb(f"xin{u}", [P, BT, D]) for u in range(2)]
        xln = [sb(f"xln{u}", [P, BT, D]) for u in range(2)]
        xt = [sb(f"xt{u}", [P, DH, BLK]) for u in range(2)]
        ln_stats, mv, gate = sb("ln_stats", [P, BT, 6]), sb("mv", [P, BT, 2]), sb("gate", [P, 1])
        var_eps, rstd, ln_tmp = sb("var_eps", [P, BT]), sb("rstd", [P, BT]), sb("ln_tmp", [P, BT])
        pxt = [ctx.enter_context(nc.psum_tensor(f"{tag}pxt{u}", [P, DH, BLK], F32)) for u in range(2)]

        ident_loaded = sem(tag + "ident_loaded")
        x_loaded = [sem(f"{tag}x_loaded{u}") for u in range(2)]
        xln_ready = [sem(f"{tag}xln_ready{u}") for u in range(2)]
        xln_stored = [sem(f"{tag}xln_stored{u}") for u in range(2)]
        xt_ready = [sem(f"{tag}xt_ready{u}") for u in range(2)]
        counted = [sem(f"{tag}counted{u}") for u in range(2)]
        xt_copied = [sem(f"{tag}xt_copied{u}") for u in range(2)]
        xt_stored = [sem(f"{tag}xt_stored{u}") for u in range(2)]
        var_ready, root_ready, steps = sem(tag + "var_ready"), sem(tag + "root_ready"), sem(tag + "ln_steps")
        rows = x_dram.rearrange("(n p) d -> p n d", p=P)
        n_it = NBLK // 2
        block = ctx.enter_context(nc.Block())

        @block.sync
        def _(sp):
            sp.dma_start(ident[:], ident_dram).then_inc(ident_loaded, 16)
            with sp.Fori(0, n_it) as i:
                for u in range(2):
                    sp.wait_ge(xln_ready[u], i)
                    sp.dma_start(xin[u][:], rows[:, bass.ds((i * 2 + u) * BT, BT), :]).then_inc(x_loaded[u], 16)
            if prefetch is not None:
                prefetch(sp)

        @block.gpsimd
        def _(pool):
            with pool.Fori(0, n_it) as i:
                for u in range(2):
                    if xln_dram is not None:
                        pool.wait_ge(xln_ready[u], i + 1)
                        pool.dma_start(xln_dram.rearrange("(n p) d -> p n d", p=P)[:, bass.ds((i * 2 + u) * BT, BT), :],
                                       xln[u][:]).then_inc(xln_stored[u], 16)
                    pool.wait_ge(xt_copied[u], i + 1)
                    for k in range(BLK // CH):
                        pool.dma_start(xt_dram[bass.ds((i * 2 + u) * (BLK // CH) + k, 1), :, :, :].rearrange("c p h t -> (c p) h t"),
                                       xt[u][:, :, k * CH:(k + 1) * CH]).then_inc(xt_stored[u], 16)
            for u in range(2):
                pool.wait_ge(xt_stored[u], 16 * n_it * (BLK // CH))
                if xln_dram is not None:
                    pool.wait_ge(xln_stored[u], 16 * n_it)

        @block.tensor
        def _(pe):
            pe.wait_ge(ident_loaded, 16)
            with pe.Fori(0, n_it) as i:
                for u in range(2):
                    pe.wait_ge(xln_ready[u], i + 1)
                    pe.wait_ge(xt_copied[u], i)
                    for t in range(BT):
                        for dh in range(DH):
                            last = nc.tensor.transpose(pxt[u][:, dh, t * P:(t + 1) * P],
                                                       xln[u][:, t, dh * P:(dh + 1) * P], ident[:])
                    last.then_inc(xt_ready[u], 1)

        @block.scalar
        def _(act):
            with act.Fori(0, n_it) as i:
                for u in range(2):
                    act.wait_ge(var_ready, i * 2 + u + 1)
                    nc.scalar.activation(rstd[:], var_eps[:], ACT.Sqrt).then_inc(root_ready, 1)
                    act.wait_ge(xt_ready[u], i + 1)
                    act.wait_ge(xt_stored[u], i * 16 * (BLK // CH))
                    act.wait_ge(counted[u], i)
                    nc.scalar.copy(xt[u][:], pxt[u][:]).then_inc(xt_copied[u], 1)

        @block.vector
        def _(dve):
            with dve.Fori(0, n_it) as i:
                for u in range(2):
                    chain = Chain(dve, steps, (i * 2 + u) * LN_LINKS)
                    dve.wait_ge(x_loaded[u], i * 16 + 16)
                    dve.wait_ge(xt_ready[u], i)
                    if xln_dram is not None:
                        dve.wait_ge(xln_stored[u], i * 16)
                    layer_norm_rows(nc, dve, chain, xin[u], xln[u], ln_stats, mv, var_eps, rstd, ln_tmp, gate,
                                    var_ready, root_ready, i * 2 + u + 1).then_inc(xln_ready[u], 1)
                    assert chain.n == LN_LINKS
                    dve.wait_ge(xt_copied[u], i + 1)
                    for dh in range(DH):
                        last = nc.vector.bn_stats(feature_stats[:, dh, bass.ds(i * 2 + u, 1), :], xt[u][:, dh, :])
                    last.then_inc(counted[u], 1)


NH, NK, KD, TOPK = 8, 64, 128, 8
NE = NK * NK
NSUB = 2 * NH * NK
HK = NH * TOPK
BN_EPS = 1e-5
NX = NE // P
PS = 16
NS = P // PS
PB = 8
NG = P // PB
P_SCALE = 4096.0


def product_key_prepare(nc, sem, ident_dram, w_q, keys, key_in, wct_dram, kin_dram):
    with ExitStack() as ctx:
        def sb(name, shape, dt=F32):
            return ctx.enter_context(nc.sbuf_tensor(name, shape, dt))

        ident = sb("pp_ident", [P, P])
        kin = sb("pp_kin", [P, NX, D])
        kin_t = sb("pp_kin_t", [P, DH, NE])
        wq = sb("pp_wq", [P, 2 * NH, D])
        keyrows = sb("pp_keyrows", [P, NH, KD])
        keys_t = sb("pp_keys_t", [P, NH, NK, 2])
        wct = sb("pp_wct", [P, DH, NSUB])
        pt = [ctx.enter_context(nc.psum_tensor(f"pp_pt{i}", [P, 4, P], F32)) for i in range(2)]
        pw = [ctx.enter_context(nc.psum_tensor(f"pp_pw{i}", [P, 512], F32)) for i in range(4)]

        ident_zero, ident_ready = sem("pp_ident_zero"), sem("pp_ident_ready")
        kin_loaded, small_loaded = sem("pp_kin_loaded"), sem("pp_small_loaded")
        transposed, copied = sem("pp_transposed"), sem("pp_copied")
        product_ready, product_copied = sem("pp_product_ready"), sem("pp_product_copied")
        stored = sem("pp_stored")
        n_keyt, n_kint = NH // 4, DH * NX // 4
        block = ctx.enter_context(nc.Block())

        @block.gpsimd
        def _(pool):
            nc.gpsimd.memset(ident[:], 0.0).then_inc(ident_zero, 1)
            pool.wait_ge(ident_zero, 1)
            nc.gpsimd.affine_select(out=ident[:], in_=ident[:], compare_op=ALU.not_equal, fill=1.0, base=0,
                                    pattern=[[-1, P]], channel_multiplier=1).then_inc(ident_ready, 1)

        @block.sync
        def _(sp):
            sp.dma_start(keyrows[:], keys.rearrange("h k s d -> (k s) h d")).then_inc(small_loaded, 16)
            sp.dma_start(wq[:], w_q.rearrange("(b k) d -> k b d", k=P)).then_inc(small_loaded, 16)
            sp.dma_start(kin[:], key_in.rearrange("(x y) d -> y x d", y=P)).then_inc(kin_loaded, 16)
            sp.wait_ge(ident_ready, 1)
            sp.dma_start(ident_dram, ident[:]).then_inc(stored, 16)
            sp.wait_ge(product_copied, 4)
            sp.dma_start(wct_dram, wct[:]).then_inc(stored, 16)
            sp.wait_ge(copied, n_keyt + n_kint)
            sp.dma_start(kin_dram, kin_t[:]).then_inc(stored, 16)
            sp.wait_ge(stored, 48)

        @block.tensor
        def _(pe):
            pe.wait_ge(ident_ready, 1)
            pe.wait_ge(small_loaded, 32)
            for g in range(n_keyt):
                for j in range(4):
                    last = nc.tensor.transpose(pt[g % 2][:, j, :], keyrows[:, 4 * g + j, :], ident[:])
                last.then_inc(transposed, 1)
            pe.wait_ge(copied, n_keyt)
            for dh in range(DH):
                for side in range(2):
                    for h in range(NH):
                        last = nc.tensor.matmul(pw[2 * dh + side][:, h * NK:(h + 1) * NK],
                                                wq[:, side * NH + h, dh * P:(dh + 1) * P],
                                                keys_t[:, h, :, side], start=True, stop=True)
                    last.then_inc(product_ready, 1)
            pe.wait_ge(kin_loaded, 16)
            for g in range(n_kint):
                pe.wait_ge(copied, n_keyt + g - 1)
                dh, x0 = g // (NX // 4), 4 * (g % (NX // 4))
                for j in range(4):
                    last = nc.tensor.transpose(pt[g % 2][:, j, :], kin[:, x0 + j, dh * P:(dh + 1) * P], ident[:])
                last.then_inc(transposed, 1)

        @block.vector
        def _(dve):
            for g in range(n_keyt):
                dve.wait_ge(transposed, g + 1)
                nc.vector.tensor_copy(keys_t[:, 4 * g:4 * g + 4, :, :].rearrange("p h k s -> p (h k s)"),
                                      pt[g % 2][:].rearrange("p h k -> p (h k)")).then_inc(copied, 1)
            for g in range(n_kint):
                dve.wait_ge(transposed, n_keyt + g + 1)
                dh, x0 = g // (NX // 4), 4 * (g % (NX // 4))
                nc.vector.tensor_copy(kin_t[:, dh, x0 * P:(x0 + 4) * P],
                                      pt[g % 2][:].rearrange("p h k -> p (h k)")).then_inc(copied, 1)

        @block.scalar
        def _(act):
            for g in range(4):
                act.wait_ge(product_ready, g + 1)
                nc.scalar.copy(wct[:, g // 2, (g % 2) * 512:(g % 2 + 1) * 512], pw[g][:]).then_inc(product_copied, 1)


def product_key_memory(nc, sem, tag, x_dram, y_dram, xt_dram, ident_dram, wct_dram, kin_dram, key_out, gamma, beta):
    with ExitStack() as ctx:
        def sb(name, shape, dt=F32):
            return ctx.enter_context(nc.sbuf_tensor(tag + name, shape, dt))

        wct = sb("wct", [P, DH, NSUB])
        kin_t = sb("kin_t", [P, DH, NE])
        kout = sb("kout", [P, NX, D])
        scale = sb("scale", [P, DH])
        shift = sb("shift", [P, DH])
        weights_loaded = sem(tag + "weights_loaded")

        def load_weights(sp):
            sp.dma_start(wct[:], wct_dram).then_inc(weights_loaded, 16)
            sp.dma_start(kin_t[:], kin_dram).then_inc(weights_loaded, 16)
            sp.dma_start(kout[:], key_out.rearrange("(x y) d -> y x d", y=P)).then_inc(weights_loaded, 16)

        with ExitStack() as first:
            def fb(name, shape, dt=F32):
                return first.enter_context(nc.sbuf_tensor(tag + name, shape, dt))

            bn_st, bn_mv = fb("bn_st", [P, DH, NBLK, 6]), fb("bn_mv", [P, DH, 2])
            bn_var, bn_tmp, gb = fb("bn_var", [P, DH]), fb("bn_tmp", [P, DH]), fb("gb", [P, 2, DH])
            layer_norm_pass(nc, sem, tag + "ln_", x_dram, xt_dram, ident_dram, bn_st, prefetch=load_weights)

            gb_loaded, bn_steps = sem(tag + "gb_loaded"), sem(tag + "bn_steps")
            bn_var_ready, bn_root_ready = sem(tag + "bn_var_ready"), sem(tag + "bn_root_ready")
            block = first.enter_context(nc.Block())

            @block.sync
            def _(sp):
                with nc.allow_non_contiguous_dma(reason="512 scalars"):
                    sp.dma_start(gb[:, 0, :], gamma.rearrange("(h p) -> p h", p=P)).then_inc(gb_loaded, 16)
                    sp.dma_start(gb[:, 1, :], beta.rearrange("(h p) -> p h", p=P)).then_inc(gb_loaded, 16)

            @block.scalar
            def _(act):
                act.wait_ge(bn_var_ready, 1)
                nc.scalar.activation(scale[:], bn_var[:], ACT.Sqrt).then_inc(bn_root_ready, 1)

            @block.vector
            def _(dve):
                chain = Chain(dve, bn_steps)
                for dh in range(DH):
                    chain.mark(nc.vector.bn_aggr(bn_mv[:, dh, :], bn_st[:, dh, :, :].rearrange("p b s -> p (b s)")))
                chain.wait()
                nc.vector.tensor_scalar_add(bn_var[:], bn_mv[:, :, 1], BN_EPS).then_inc(bn_var_ready, 1)
                dve.wait_ge(bn_root_ready, 1)
                newton_reciprocal(nc, chain, scale, scale, bn_var, bn_tmp)
                dve.wait_ge(gb_loaded, 32)
                chain.link(nc.vector.tensor_tensor(scale[:], scale[:], gb[:, 0, :], ALU.mult))
                chain.link(nc.vector.tensor_tensor(bn_tmp[:], bn_mv[:, :, 0], scale[:], ALU.mult))
                chain.link(nc.vector.tensor_tensor(shift[:], gb[:, 1, :], bn_tmp[:], ALU.subtract))

        routed_experts(nc, sem, tag, x_dram, y_dram, xt_dram, ident_dram, wct, kin_t, kout, scale, shift,
                       weights_loaded)


def routed_experts(nc, sem, tag, x_dram, y_dram, xt_dram, ident_dram, wct, kin_t, kout, scale, shift, weights_loaded):
    with ExitStack() as ctx:
        def sb(name, shape, dt=F32):
            return ctx.enter_context(nc.sbuf_tensor(tag + name, shape, dt))

        def pb(name, shape):
            return ctx.enter_context(nc.psum_tensor(tag + name, shape, F32))

        ident = sb("ident2", [P, P])
        hidden = sb("hidden", [P, NX, CH])
        xt_in = sb("xt_in", [P, DH, CH])
        xt = sb("xtc", [P, DH, CH])
        xn = sb("xn", [P, DH, CH])
        sim = sb("sim", [P, 2, NSUB])
        top = sb("top", [P, 2, 2, NH, TOPK])
        top_key = sb("top_key", [P, 2, 2, NH, TOPK], U16)
        cand = sb("cand", [P, 2, NH, TOPK, TOPK])
        picked = cand[:].rearrange("p u h a b -> p (u h a b)").bitcast(F16).rearrange(
            "p (s g a k) -> p s g a k", s=2, g=2 * NH, a=TOPK)
        best = sb("best", [P, 2, NH, TOPK])
        best_at = sb("best_at", [P, 2 * NH * TOPK], U16)
        rank = sb("rank", [P, 2, 2 * NH, TOPK], U16)
        key = sb("key", [P, 2, 2 * HK])
        key_u = sb("key_u", [P, 2 * HK], U16)
        key_bit = sb("key_bit", [P, 2 * HK], U16)
        key_half = sb("key_half", [P, 2 * HK], U16)
        total = sb("total", [P, 2 * NH])
        expo = sb("expo", [P, 2 * NH, TOPK])
        picks = sb("picks", [P, 3, 2 * HK])
        xq, yq = sb("xq", [P, P], F16), sb("yq", [P, P], F16)
        p_hi, p_lo = sb("p_hi", [P, P], F16), sb("p_lo", [P, P], F16)
        rank_iota = sb("rank_iota", [P, TOPK, TOPK], U16)
        y_iota = sb("y_iota", [P, P, PS], F16)
        tile_base = sb("tile_base", [P, 1])
        y_hot = sb("y_hot", [P, NS, P, PS], F16)
        x_hot = [sb(f"x_hot{i}", [P, 2 * NX, PS], F16) for i in range(2)]
        x_hi = sb("x_hi", [P, NS, 2 * NX, PS], F16)
        x_lo = sb("x_lo", [P, NS, 2 * NX, PS], F16)
        xres = sb("xres", [P, 2, D])
        junk = sb("junk", [P, 8])

        p_sim = pb("p_sim", [P, NSUB])
        p_route = [pb(f"p_route{i}", [P, PB, 2 * NX]) for i in range(2)]
        p_hid = [pb(f"p_hid{i}", [P, 2, CH]) for i in range(2)]
        p_out = pb("p_out", [P, 2, D])
        p_picks = pb("p_picks", [P, 3, P])

        consts_loaded, iota_ready = sem(tag + "consts_loaded"), sem(tag + "iota_ready")
        xt_loaded, xn_ready, xt_copied = sem(tag + "xt2_loaded"), sem(tag + "xn_ready"), sem(tag + "xt2_copied")
        sim_ready, sim_copied = sem(tag + "sim_ready"), sem(tag + "sim_copied")
        best_ready, exp_ready = sem(tag + "best_ready"), sem(tag + "exp_ready")
        picks_ready, picks_turned, picks_copied = sem(tag + "picks_ready"), sem(tag + "picks_turned"), sem(tag + "picks_copied")
        p_lo_ready, hot_ready = sem(tag + "p_lo_ready"), sem(tag + "hot_ready")
        route_ready, routed = sem(tag + "route_ready"), sem(tag + "routed")
        hid_ready, gelu_ready = sem(tag + "hid_ready"), sem(tag + "gelu_ready")
        out_ready, x_loaded, y_ready, y_stored = sem(tag + "out_ready"), sem(tag + "xres_loaded"), sem(tag + "y_ready"), sem(tag + "y_stored")
        steps, base_ready = sem(tag + "steps"), sem(tag + "base_ready")

        def above(eng, s, value):
            if not isinstance(value, int) or value > 0:
                eng.wait_ge(s, value)

        block = ctx.enter_context(nc.Block())

        @block.gpsimd
        def _(pool):
            nc.gpsimd.iota(rank_iota[:], pattern=[[1, TOPK], [0, TOPK]], base=0, channel_multiplier=0,
                           allow_small_or_imprecise_dtypes=True).then_inc(iota_ready, 1)
            nc.gpsimd.iota(y_iota[:], pattern=[[1, P], [0, PS]], base=0, channel_multiplier=0,
                           allow_small_or_imprecise_dtypes=True).then_inc(iota_ready, 1)

        xt_view = xt_dram
        x_view = x_dram.rearrange("(n p) d -> p n d", p=P)
        y_view = y_dram.rearrange("(n p) d -> p n d", p=P)

        @block.sync
        def _(sp):
            def load_xt(c):
                above(sp, xt_copied, c)
                sp.dma_start(xt_in[:], xt_view[bass.ds(c, 1), :, :, :].rearrange("c p h t -> (c p) h t")).then_inc(xt_loaded, 16)

            def chunk(c, last=False):
                above(sp, y_stored, c * 16)
                sp.dma_start(xres[:], x_view[:, bass.ds(c * 2, 2), :]).then_inc(x_loaded, 16)
                if not last:
                    load_xt(c + 1)
                sp.wait_ge(y_ready, c + 1)
                sp.dma_start(y_view[:, bass.ds(c * 2, 2), :], xres[:]).then_inc(y_stored, 16)

            sp.dma_start(ident[:], ident_dram).then_inc(consts_loaded, 16)
            load_xt(0)
            with sp.Fori(0, NCH - 1) as c:
                chunk(c)
            chunk(NCH - 1, True)
            sp.wait_ge(y_stored, 16 * NCH)

        @block.tensor
        def _(pe):
            def sub_scores(c, u):
                if u == 0:
                    pe.wait_ge(xn_ready, c + 1)
                above(pe, sim_copied, 2 * c + u)
                for cb in range(NSUB // 512):
                    for dh in range(DH):
                        last = nc.tensor.matmul(p_sim[:, cb * 512:(cb + 1) * 512], xn[:, dh, u * P:(u + 1) * P],
                                                wct[:, dh, cb * 512:(cb + 1) * 512], start=dh == 0, stop=dh == DH - 1)
                last.then_inc(sim_ready, 1)

            def turn_picks(c):
                pe.wait_ge(picks_ready, c + 1)
                above(pe, p_lo_ready, c)
                for k in range(3):
                    last = nc.tensor.transpose(p_picks[:, k, :], picks[:, k, :], ident[:])
                last.then_inc(picks_turned, 1)

            def route(c, s):
                pe.wait_ge(hot_ready, c * NS + s + 1)
                for g in range(PS // PB):
                    gi = s * (PS // PB) + g
                    above(pe, routed, c * NG + max(gi - 1, 0))
                    for j in range(PB):
                        i = g * PB + j
                        nc.tensor.matmul(p_route[gi % 2][:, j, :], y_hot[:, s, :, i], x_hi[:, s, :, i],
                                         start=True, stop=False)
                        last = nc.tensor.matmul(p_route[gi % 2][:, j, :], y_hot[:, s, :, i], x_lo[:, s, :, i],
                                                start=False, stop=True)
                    last.then_inc(route_ready, 1)

            def expert_in(c, xp):
                if xp == 0:
                    pe.wait_ge(xt_copied, c + 1)
                if xp % 2 == 0:
                    above(pe, gelu_ready, c * (NX // 2) + xp // 2 - 1)
                bank = p_hid[(xp // 2) % 2]
                for dh in range(DH):
                    last = nc.tensor.matmul(bank[:, xp % 2, :], kin_t[:, dh, xp * P:(xp + 1) * P], xt[:, dh, :],
                                            start=dh == 0, stop=dh == DH - 1)
                if xp % 2 == 1:
                    last.then_inc(hid_ready, 1)

            def expert_out(c, xp):
                if xp == 0:
                    pe.wait_ge(routed, c * NG + NG)
                    above(pe, y_ready, c)
                for u in range(2):
                    last = nc.tensor.matmul(p_out[:, u, :], hidden[:, xp, u * P:(u + 1) * P], kout[:, xp, :],
                                            start=(xp == 0 and u == 0), stop=xp == NX - 1, skip_group_check=True)
                if xp == NX - 1:
                    last.then_inc(out_ready, 1)

            def chunk(c):
                for s in range(NS):
                    route(c, s)
                    if s == NS // 4:
                        sub_scores(c + 1, 0)
                    if s == NS // 2:
                        sub_scores(c + 1, 1)
                for xp in range(NX):
                    expert_out(c, xp)
                    expert_in(c + 1, xp)
                    if xp == 21:
                        turn_picks(c + 1)

            pe.wait_ge(consts_loaded, 16)
            pe.wait_ge(weights_loaded, 48)
            sub_scores(0, 0)
            sub_scores(0, 1)
            for xp in range(NX):
                expert_in(0, xp)
            turn_picks(0)
            with pe.Fori(0, NCH - 1) as c:
                chunk(c)
            for s in range(NS):
                route(NCH - 1, s)
            for xp in range(NX):
                expert_out(NCH - 1, xp)

        @block.scalar
        def _(act):
            def prepare(c):
                act.wait_ge(xt_loaded, c * 16 + 16)
                above(act, sim_ready, 2 * c)
                for dh in range(DH):
                    last = nc.scalar.activation(xn[:, dh, :], xt_in[:, dh, :], ACT.Identity,
                                                bias=shift[:, dh:dh + 1], scale=scale[:, dh:dh + 1])
                last.then_inc(xn_ready, 1)
                above(act, hid_ready, c * (NX // 2))
                nc.scalar.copy(xt[:], xt_in[:]).then_inc(xt_copied, 1)

            def copy_scores(c, u):
                act.wait_ge(sim_ready, 2 * c + u + 1)
                above(act, picks_ready, c)
                nc.scalar.copy(sim[:, u, :], p_sim[:]).then_inc(sim_copied, 1)

            def exponent(c):
                act.wait_ge(best_ready, c + 1)
                nc.scalar.activation(expo[:], expo[:], ACT.Exp).then_inc(exp_ready, 1)

            def copy_picks(c):
                act.wait_ge(picks_turned, c + 1)
                above(act, hot_ready, c * NS)
                nc.scalar.activation(xq[:], p_picks[:, 0, :], ACT.Identity, bias=tile_base[:])
                nc.scalar.copy(yq[:], p_picks[:, 1, :])
                nc.scalar.mul(p_hi[:], p_picks[:, 2, :], P_SCALE).then_inc(picks_copied, 1)

            def gelu(c, g):
                act.wait_ge(hid_ready, c * (NX // 2) + g + 1)
                nc.scalar.activation(hidden[:, 2 * g:2 * g + 2, :], p_hid[g % 2][:], ACT.Gelu).then_inc(gelu_ready, 1)

            def chunk(c):
                prepare(c)
                copy_scores(c, 0)
                copy_scores(c, 1)
                for g in range(NX // 2):
                    gelu(c, g)
                    if g == 8:
                        exponent(c)
                    if g == 10:
                        copy_picks(c)

            act.wait_ge(base_ready, 1)
            prepare(0)
            copy_scores(0, 0)
            copy_scores(0, 1)
            for g in range(NX // 2):
                gelu(0, g)
            exponent(0)
            copy_picks(0)
            with act.Fori(1, NCH) as c:
                chunk(c)

        @block.vector
        def _(dve):
            PICK_STEPS = 12

            def pick(c):
                chain = Chain(dve, steps, c * PICK_STEPS)
                for u in range(2):
                    dve.wait_ge(sim_copied, c * 2 + u + 1)
                    nc.vector.memset(junk[:, u:u + 1], 0.0)
                    for side in range(2):
                        for h in range(NH):
                            k0 = (side * NH + h) * NK
                            last = nc.vector.max(top[:, side, u, h, :], sim[:, u, k0:k0 + NK])
                chain.link(last)
                for u in range(2):
                    a = top[:, 0, u, :, :].unsqueeze(3).to_broadcast([P, NH, TOPK, TOPK])
                    b = top[:, 1, u, :, :].unsqueeze(2).to_broadcast([P, NH, TOPK, TOPK])
                    last = nc.vector.tensor_tensor(cand[:, u, :, :, :], a, b, ALU.add)
                chain.mark(last)
                for side in range(2):
                    for u in range(2):
                        for h in range(NH):
                            k0 = (side * NH + h) * NK
                            nc.vector.max_index(top_key[:, side, u, h, :], top[:, side, u, h, :], sim[:, u, k0:k0 + NK])
                chain.wait()
                nc.vector.memset(junk[:, 2:3], 0.0)
                for u in range(2):
                    for h in range(NH):
                        last = nc.vector.max(best[:, u, h, :], cand[:, u, h, :, :].rearrange("p a b -> p (a b)"))
                chain.link(last)
                flat = best[:].rearrange("p u h k -> p (u h) k")
                nc.vector.tensor_tensor(expo[:], flat, flat[:, :, 0:1].to_broadcast([P, 2 * NH, TOPK]),
                                        ALU.subtract).then_inc(best_ready, 1)
                for u in range(2):
                    for h in range(NH):
                        o = (u * NH + h) * TOPK
                        last = nc.vector.max_index(best_at[:, o:o + TOPK], best[:, u, h, :],
                                                   cand[:, u, h, :, :].rearrange("p a b -> p (a b)"))
                chain.link(last)
                r = rank[:].rearrange("p s g k -> p s (g k)")
                nc.vector.tensor_single_scalar(r[:, 0, :], best_at[:], 3, ALU.logical_shift_right)
                chain.link(nc.vector.tensor_single_scalar(r[:, 1, :], best_at[:], TOPK - 1, ALU.bitwise_and))
                iota = rank_iota[:].unsqueeze(1).to_broadcast([P, 2 * NH, TOPK, TOPK])
                for side in range(2):
                    last = nc.vector.tensor_tensor(picked[:, side, :, :, :], iota, rank[:, side, :, :].unsqueeze(2).to_broadcast([P, 2 * NH, TOPK, TOPK]),
                                                   ALU.is_equal)
                chain.link(last)
                for side in range(2):
                    keys_of = top_key[:, side, :, :, :].rearrange("p u h k -> p (u h) k").unsqueeze(3).to_broadcast([P, 2 * NH, TOPK, TOPK])
                    last = nc.vector.tensor_tensor(picked[:, side, :, :, :], picked[:, side, :, :, :], keys_of, ALU.mult)
                chain.link(last)
                for side in range(2):
                    last = nc.vector.tensor_reduce(key[:, side, :].rearrange("p (g k) -> p g k", k=TOPK),
                                                   picked[:, side, :, :, :].rearrange("p g a k -> p g k a"), AX.X, ALU.add)
                chain.link(last)
                chain.link(nc.vector.tensor_copy(key_u[:], key[:, 0, :]))
                nc.vector.tensor_single_scalar(key_half[:], key_u[:], 1, ALU.logical_shift_right)
                chain.link(nc.vector.tensor_scalar(key_bit[:], key_u[:], 1, 6, ALU.bitwise_and, ALU.logical_shift_left))
                above(dve, picks_turned, c)
                nc.vector.tensor_copy(picks[:, 0, :], key_half[:])
                nc.vector.tensor_tensor(picks[:, 1, :], key_bit[:], key[:, 1, :], ALU.add)
                dve.wait_ge(exp_ready, c + 1)
                chain.link(nc.vector.tensor_reduce(total[:], expo[:], AX.X, ALU.add))
                chain.link(nc.vector.reciprocal(total[:], total[:]))
                nc.vector.tensor_tensor(picks[:, 2, :].rearrange("p (g k) -> p g k", k=TOPK), expo[:],
                                        total[:].unsqueeze(2).to_broadcast([P, 2 * NH, TOPK]), ALU.mult).then_inc(picks_ready, 1)
                dve.wait_ge(picks_copied, c + 1)
                nc.vector.scalar_tensor_tensor(p_lo[:], p_picks[:, 2, :], P_SCALE, p_hi[:], ALU.mult,
                                               ALU.subtract).then_inc(p_lo_ready, 1)
                dve.wait_ge(p_lo_ready, c + 1)

                return chain

            def one_hots(c, hots):
                for s in range(NS):
                    lo, hi = s * PS, (s + 1) * PS
                    hot = x_hot[s % 2]
                    above(dve, hot_ready, c * NS + s - 1)
                    hots.mark(nc.vector.tensor_tensor(hot[:], y_iota[:, 0:2 * NX, :], xq[:, lo:hi].unsqueeze(1).to_broadcast([P, 2 * NX, PS]), ALU.is_equal))
                    nc.vector.tensor_tensor(y_hot[:, s, :, :], y_iota[:], yq[:, lo:hi].unsqueeze(1).to_broadcast([P, P, PS]), ALU.is_equal)
                    hots.wait()
                    nc.vector.tensor_tensor(x_hi[:, s, :, :], hot[:], p_hi[:, lo:hi].unsqueeze(1).to_broadcast([P, 2 * NX, PS]), ALU.mult)
                    nc.vector.tensor_tensor(x_lo[:, s, :, :], hot[:], p_lo[:, lo:hi].unsqueeze(1).to_broadcast([P, 2 * NX, PS]), ALU.mult).then_inc(hot_ready, 1)

            def weigh(c):
                dve.wait_ge(gelu_ready, c * (NX // 2) + NX // 2)
                for g in range(NG):
                    dve.wait_ge(route_ready, c * NG + g + 1)
                    h = hidden[:].rearrange("p x (u t) -> p x u t", u=2)[:, :, :, g * PB:(g + 1) * PB]
                    nc.vector.tensor_tensor(h, h, p_route[g % 2][:].rearrange("p t (u x) -> p x u t", u=2),
                                            ALU.mult).then_inc(routed, 1)

            def add_residual(c):
                dve.wait_ge(out_ready, c + 1)
                dve.wait_ge(x_loaded, c * 16 + 16)
                nc.vector.scalar_tensor_tensor(xres[:].rearrange("p u d -> p (u d)"), p_out[:].rearrange("p u d -> p (u d)"),
                                               1.0 / P_SCALE, xres[:].rearrange("p u d -> p (u d)"), ALU.mult, ALU.add).then_inc(y_ready, 1)

            def prepare(c):
                chain = pick(c)
                hots = Chain(dve, hot_steps, c * NS)
                one_hots(c, hots)
                PICKED.append(chain.n)

            PICKED = []
            hot_steps = sem(tag + "hot_steps")
            nc.vector.memset(tile_base[0:HK, :], 0.0)
            nc.vector.memset(tile_base[HK:P, :], float(NX)).then_inc(base_ready, 1)
            dve.wait_ge(iota_ready, 2)
            prepare(0)
            with dve.Fori(0, NCH - 1) as c:
                weigh(c)
                prepare(c + 1)
                add_residual(c)
            weigh(NCH - 1)
            add_residual(NCH - 1)
            assert set(PICKED) == {PICK_STEPS}, PICKED


ERR_CLIP, GRAD_CLIP = 5.0, 1.0
ERR_SCALE = 2.0 / 1024.0
NT = T // P


def memory_prepare(nc, sem, ident_dram, Wk, Wv, Wout, W0, W1, w):
    with ExitStack() as ctx:
        def sb(name, shape, dt=F32):
            return ctx.enter_context(nc.sbuf_tensor(name, shape, dt))

        ident = sb("mp_ident", [P, P])
        order = ("W0", "Wk", "Wv", "W1", "Wout")
        natural = {"W0": sb("mp_W0", [P, DH, D]), "Wk": w["Wk"], "Wv": sb("mp_Wv", [P, DH, D]), "W1": w["W1"],
                   "Wout": sb("mp_Wout", [P, DH, D])}
        dram = {"W0": W0, "Wk": Wk, "Wv": Wv, "W1": W1, "Wout": Wout}
        pt = [ctx.enter_context(nc.psum_tensor(f"mp_pt{i}", [P, DH, D], F32)) for i in range(len(order))]
        pw = ctx.enter_context(nc.psum_tensor("mp_pw", [P, DH, D], F32))
        loaded = sem("mp_loaded")
        turned, copied, product = sem("mp_turned"), sem("mp_copied"), sem("mp_product")
        block = ctx.enter_context(nc.Block())

        @block.sync
        def _(sp):
            sp.dma_start(ident[:], ident_dram).then_inc(loaded, 16)
            for name in order:
                sp.dma_start(natural[name][:], dram[name].rearrange("(h p) d -> p h d", p=P)).then_inc(loaded, 16)

        @block.tensor
        def _(pe):
            pe.wait_ge(loaded, 16 * (len(order) + 1))
            for i, name in enumerate(order):
                for a in range(DH):
                    for b in range(DH):
                        last = nc.tensor.transpose(pt[i][:, b, a * P:(a + 1) * P],
                                                   natural[name][:, a, b * P:(b + 1) * P], ident[:])
                last.then_inc(turned, 1)
            pe.wait_ge(copied, 1)
            for dh in range(DH):
                for mh in range(DH):
                    last = nc.tensor.matmul(pw[:, dh, :], w["Wk"][:, mh, dh * P:(dh + 1) * P], w["W0T"][:, mh, :],
                                            start=mh == 0, stop=mh == DH - 1)
            last.then_inc(product, 1)

        @block.vector
        def _(dve):
            for i, (name, sign) in enumerate((("W0T", 1.0), ("WkT", 1.0), ("minusWvT", -1.0), ("W1T", 1.0), ("WoutT", 1.0))):
                dve.wait_ge(turned, i + 1)
                nc.vector.tensor_scalar_mul(w[name][:], pt[i][:], sign).then_inc(copied, 1)
            dve.wait_ge(product, 1)
            nc.vector.tensor_copy(w["W0WkT"][:], pw[:])


def memory_gradients(nc, sem, xln_dram, xt_dram, ident_dram, w, grad1, grad0t):
    RING = 4
    with ExitStack() as ctx:
        def ring(name, shape, n=RING):
            return [ctx.enter_context(nc.sbuf_tensor(f"mg_{name}{i}", shape, F32)) for i in range(n)]

        def pb(name):
            return ctx.enter_context(nc.psum_tensor("mg_" + name, [P, DH * P * 2], F32))

        ident = ctx.enter_context(nc.sbuf_tensor("mg_ident", [P, P], F32))
        xt, xln = ring("xt", [P, DH, P]), ring("xln", [P, D])
        sig, a1, dsilu, err, d1 = ring("sig", [P, D]), ring("a1", [P, D]), ring("dsilu", [P, D]), ring("err", [P, D]), ring("d1", [P, D])
        tmp = ring("tmp", [P, D])
        a1t, errt = ring("a1t", [P, DH, P]), ring("errt", [P, DH, P])
        p_pre, p_a1t, p_err, p_errt, p_back = pb("pre"), pb("a1t"), pb("err"), pb("errt"), pb("back")
        p_grad1, p_grad0t = pb("grad1"), pb("grad0t")
        names = ("xt_loaded", "xln_loaded", "pre_ready", "sig_ready", "a1_ready", "dsilu_ready", "a1t_turned", "a1t_ready",
                 "err_summed", "err_ready", "errt_turned", "errt_ready", "back_ready", "d1_ready", "grads_added")
        s = {n: sem("mg_" + n) for n in names}
        for n in ("xt_loaded", "xln_loaded"):
            s[n] = [sem(f"mg_{n}{i}") for i in range(RING)]
        ident_loaded, steps = sem("mg_ident_loaded"), sem("mg_steps")
        block = ctx.enter_context(nc.Block())

        def above(eng, what, value):
            if not isinstance(value, int) or value > 0:
                eng.wait_ge(what, value)

        def valid(n):
            return not isinstance(n, int) or 0 <= n < NT

        def pipeline(eng, step):
            for n in range(RING):
                step(n, n)
            with eng.Fori(1, NT // RING) as i:
                for m in range(RING):
                    step(i * RING + m, m)
            for n in range(NT, NT + 3):
                step(n, n % RING)

        @block.sync
        def _(sp):
            sp.dma_start(ident[:], ident_dram).then_inc(ident_loaded, 16)

            def load(i, m):
                above(sp, s["grads_added"], (i - 1) * RING + m + 1)
                for h in range(DH):
                    sp.dma_start(xt[m][:, h, :], xt_dram[bass.ds(i * (RING // 2) + m // 2, 1), :, h, (m % 2) * P:(m % 2 + 1) * P]
                                 .rearrange("c p t -> (c p) t")).then_inc(s["xt_loaded"][m], 16)
                sp.dma_start(xln[m][:], xln_dram.rearrange("(n p) d -> n p d", p=P)[bass.ds(i * RING + m, 1), :, :]
                             .rearrange("n p d -> (n p) d")).then_inc(s["xln_loaded"][m], 16)

            for m in range(RING):
                load(0, m)
            with sp.Fori(1, NT // RING) as i:
                for m in range(RING):
                    load(i, m)

        @block.tensor
        def _(pe):
            pe.wait_ge(ident_loaded, 16)

            def step(n, m, it):
                m1, m2, m3 = (m - 1) % RING, (m - 2) % RING, (m - 3) % RING
                if valid(n - 1):
                    pe.wait_ge(s["a1_ready"], n)
                    above(pe, s["a1t_ready"], n - 1)
                    for h in range(DH):
                        last = nc.tensor.transpose(p_a1t[:, h * P:(h + 1) * P], a1[m1][:, h * P:(h + 1) * P], ident[:])
                    last.then_inc(s["a1t_turned"], 1)
                if valid(n - 2):
                    pe.wait_ge(s["err_ready"], n - 1)
                    above(pe, s["errt_ready"], n - 2)
                    for h in range(DH):
                        last = nc.tensor.transpose(p_errt[:, h * P:(h + 1) * P], err[m2][:, h * P:(h + 1) * P], ident[:])
                    last.then_inc(s["errt_turned"], 1)
                if valid(n):
                    pe.wait_ge(s["xt_loaded"][m], it * 32 + 32)
                    above(pe, s["a1_ready"], n)
                    for h in range(DH):
                        last = nc.tensor.matmul(p_pre[:, 0:D], xt[m][:, h, :], w["W0WkT"][:, h, :], start=h == 0, stop=h == DH - 1)
                    last.then_inc(s["pre_ready"], 1)
                if valid(n - 2):
                    pe.wait_ge(s["errt_ready"], n - 1)
                    above(pe, s["d1_ready"], n - 2)
                    for h in range(DH):
                        last = nc.tensor.matmul(p_back[:, 0:D], errt[m2][:, h, :], w["W1"][:, h, :], start=h == 0, stop=h == DH - 1)
                    last.then_inc(s["back_ready"], 1)
                if valid(n - 1):
                    pe.wait_ge(s["a1t_ready"], n)
                    above(pe, s["err_ready"], n - 1)
                    for h in range(DH):
                        nc.tensor.matmul(p_err[:, 0:D], a1t[m1][:, h, :], w["W1T"][:, h, :], start=h == 0, stop=False)
                    for h in range(DH):
                        last = nc.tensor.matmul(p_err[:, 0:D], xt[m1][:, h, :], w["minusWvT"][:, h, :], start=False, stop=h == DH - 1)
                    last.then_inc(s["err_summed"], 1)
                if valid(n - 3):
                    first, end = isinstance(n, int) and n == 3, isinstance(n, int) and n == NT + 2
                    pe.wait_ge(s["xln_loaded"][m3], (it if m == 3 else it - 1) * 16 + 16)
                    pe.wait_ge(s["d1_ready"], n - 2)
                    for h in range(DH):
                        nc.tensor.matmul(p_grad1[:, h * D:(h + 1) * D], err[m3][:, h * P:(h + 1) * P], a1[m3][:],
                                         start=first and h == 0, stop=end, skip_group_check=True)
                    for h in range(DH):
                        last = nc.tensor.matmul(p_grad0t[:, h * D:(h + 1) * D], xln[m3][:, h * P:(h + 1) * P], d1[m3][:],
                                                start=first and h == 0, stop=end, skip_group_check=True)
                    last.then_inc(s["grads_added"], 1)

            for n in range(RING):
                step(n, n, 0)
            with pe.Fori(1, NT // RING) as i:
                for m in range(RING):
                    step(i * RING + m, m, i)
            for n in range(NT, NT + 3):
                step(n, n % RING, NT // RING)

        @block.scalar
        def _(act):
            def step(n, m):
                m1, m2 = (m - 1) % RING, (m - 2) % RING
                if valid(n - 1):
                    act.wait_ge(s["a1t_turned"], n)
                    nc.scalar.copy(a1t[m1][:].rearrange("p h t -> p (h t)"), p_a1t[:, 0:D]).then_inc(s["a1t_ready"], 1)
                if valid(n - 2):
                    act.wait_ge(s["errt_turned"], n - 1)
                    nc.scalar.copy(errt[m2][:].rearrange("p h t -> p (h t)"), p_errt[:, 0:D]).then_inc(s["errt_ready"], 1)
                if valid(n):
                    act.wait_ge(s["pre_ready"], n + 1)
                    nc.scalar.activation(sig[m][:], p_pre[:, 0:D], ACT.Sigmoid).then_inc(s["sig_ready"], 1)

            pipeline(act, step)

        @block.vector
        def _(dve):
            def step(n, m):
                m1, m2 = (m - 1) % RING, (m - 2) % RING
                if valid(n):
                    dve.wait_ge(s["sig_ready"], n + 1)
                    above(dve, s["grads_added"], n - RING + 1)
                    nc.vector.tensor_tensor(a1[m][:], p_pre[:, 0:D], sig[m][:], ALU.mult).then_inc(s["a1_ready"], 1)
                if valid(n - 2):
                    dve.wait_ge(s["back_ready"], n - 1)
                    nc.vector.tensor_tensor(d1[m2][:], p_back[:, 0:D], dsilu[m2][:], ALU.mult).then_inc(s["d1_ready"], 1)
                if valid(n):
                    dve.wait_ge(s["a1_ready"], n + 1)
                    nc.vector.scalar_tensor_tensor(tmp[m][:], sig[m][:], 1.0, a1[m][:], ALU.subtract, ALU.mult).then_inc(steps, 1)
                    dve.wait_ge(steps, n + 1)
                    nc.vector.tensor_tensor(dsilu[m][:], sig[m][:], tmp[m][:], ALU.subtract).then_inc(s["dsilu_ready"], 1)
                if valid(n - 1):
                    dve.wait_ge(s["err_summed"], n)
                    nc.vector.tensor_scalar(err[m1][:], p_err[:, 0:D], -ERR_CLIP, ERR_CLIP, ALU.max, ALU.min).then_inc(s["err_ready"], 1)

            pipeline(dve, step)
            dve.wait_ge(s["grads_added"], NT)
            nc.vector.tensor_copy(grad1[:].rearrange("p h e -> p (h e)"), p_grad1[:])
            nc.vector.tensor_copy(grad0t[:].rearrange("p h e -> p (h e)"), p_grad0t[:])


def memory_update(nc, sem, ident_dram, feature_stats, gate_w, gate_b, W0_t, Wq, w, grad1, grad0t, first_w, second_w):
    with ExitStack() as ctx:
        def sb(name, shape, dt=F32):
            return ctx.enter_context(nc.sbuf_tensor("mu_" + name, shape, dt))

        NGATE = 3
        ones, wg, weighted, bias = sb("ones", [P, P]), sb("wg", [P, NGATE, DH]), sb("weighted", [P, NGATE, DH]), sb("bias", [P, NGATE])
        wq, mean = sb("wq", [P, DH, D]), sb("mean", [P, DH, 2])
        gates, minus_lr, keep = sb("gates", [P, NGATE]), sb("minus_lr", [P, 1]), sb("keep", [P, 1])
        zero, mom = sb("zero", [P, DH, D]), sb("mom", [P, DH, D])
        g0, g1, w0n, w1n = sb("g0", [P, DH, D]), sb("g1", [P, DH, D]), sb("w0n", [P, DH, D]), sb("w1n", [P, DH, D])
        p_gate = ctx.enter_context(nc.psum_tensor("mu_p_gate", [P, 512], F32))
        p_g0, p_first, p_second = (ctx.enter_context(nc.psum_tensor("mu_" + n, [P, DH, D], F32)) for n in ("p_g0", "p_first", "p_second"))
        loaded, bias_zero, bias_loaded, gate_in, gate_sum, gate_ready = (sem("mu_" + n) for n in (
            "loaded", "bias_zero", "bias_loaded", "gate_in", "gate_sum", "gate_ready"))
        g0_ready, w0n_ready, w1n_ready, first_ready, second_ready, steps = (sem("mu_" + n) for n in (
            "g0_ready", "w0n_ready", "w1n_ready", "first_ready", "second_ready", "steps"))
        block = ctx.enter_context(nc.Block())

        @block.sync
        def _(sp):
            sp.dma_start(wq[:], Wq.rearrange("(h p) d -> p h d", p=P)).then_inc(loaded, 16)
            with nc.allow_non_contiguous_dma(reason="768 scalars"):
                for g in range(NGATE):
                    sp.dma_start(wg[:, g, :], gate_w[g].rearrange("o (h p) -> p (o h)", p=P)).then_inc(loaded, 16)
            sp.wait_ge(bias_zero, 1)
            for g in range(NGATE):
                sp.dma_start(bias[0:1, g:g + 1], gate_b[g].rearrange("(o n) -> o n", o=1)).then_inc(bias_loaded, 16)

        @block.tensor
        def _(pe):
            pe.wait_ge(bias_loaded, 16 * NGATE)
            nc.tensor.matmul(p_gate[:, 0:NGATE], ones[:], bias[:], start=True, stop=False)
            pe.wait_ge(gate_in, 1)
            for h in range(DH):
                last = nc.tensor.matmul(p_gate[:, 0:NGATE], ones[:], weighted[:, :, h], start=False, stop=h == DH - 1)
            last.then_inc(gate_sum, 1)
            for mh in range(DH):
                for h in range(DH):
                    last = nc.tensor.matmul(p_g0[:, mh, :], w["WkT"][:, h, mh * P:(mh + 1) * P], grad0t[:, h, :],
                                            start=h == 0, stop=h == DH - 1)
            last.then_inc(g0_ready, 1)
            pe.wait_ge(w1n_ready, 1)
            for eh in range(DH):
                for h in range(DH):
                    last = nc.tensor.matmul(p_second[:, eh, :], w1n[:, h, eh * P:(eh + 1) * P], w["WoutT"][:, h, :],
                                            start=h == 0, stop=h == DH - 1)
            last.then_inc(second_ready, 1)
            pe.wait_ge(w0n_ready, 1)
            for dh in range(DH):
                for mh in range(DH):
                    last = nc.tensor.matmul(p_first[:, dh, :], wq[:, mh, dh * P:(dh + 1) * P], w0n[:, mh, :],
                                            start=mh == 0, stop=mh == DH - 1)
            last.then_inc(first_ready, 1)

        @block.scalar
        def _(act):
            act.wait_ge(gate_sum, 1)
            nc.scalar.activation(gates[:], p_gate[:, 0:NGATE], ACT.Sigmoid).then_inc(gate_ready, 1)

        @block.vector
        def _(dve):
            chain = Chain(dve, steps)
            nc.vector.memset(ones[:], 1.0)
            nc.vector.memset(bias[:], 0.0).then_inc(bias_zero, 1)
            chain.mark(nc.vector.memset(zero[:], 0.0))
            for h in range(DH):
                chain.mark(nc.vector.bn_aggr(mean[:, h, :], feature_stats[:, h, :, :].rearrange("p b s -> p (b s)")))
            dve.wait_ge(loaded, 16 * (NGATE + 1))
            chain.wait()
            nc.vector.tensor_tensor(weighted[:], wg[:], mean[:, :, 0].unsqueeze(1).to_broadcast([P, NGATE, DH]),
                                    ALU.mult).then_inc(gate_in, 1)
            dve.wait_ge(gate_ready, 1)
            chain.mark(nc.vector.tensor_scalar(keep[:], gates[:, 0:1], -1.0, 1.0, ALU.mult, ALU.add))
            chain.mark(nc.vector.tensor_scalar_mul(minus_lr[:], gates[:, 1:2], -1.0))
            chain.mark(nc.vector.tensor_scalar(mom[:], zero[:], gates[:, 2:3], None, ALU.mult))

            def step_layer(grad, g, scale, old, new, done):
                if scale != 1.0:
                    chain.link(nc.vector.tensor_scalar_mul(g, grad, scale))
                    grad = g
                chain.link(nc.vector.tensor_scalar(g, grad, -GRAD_CLIP, GRAD_CLIP, ALU.max, ALU.min))
                chain.link(nc.vector.scalar_tensor_tensor(g, g, minus_lr[:], mom[:].rearrange("p h e -> p (h e)"), ALU.mult, ALU.add))
                nc.vector.scalar_tensor_tensor(new, old, keep[:], g, ALU.mult, ALU.add).then_inc(done, 1)

            def flat(x):
                return x[:].rearrange("p h e -> p (h e)")

            step_layer(flat(grad1), flat(g1), ERR_SCALE, flat(w["W1"]), flat(w1n), w1n_ready)
            dve.wait_ge(g0_ready, 1)
            step_layer(flat(p_g0), flat(g0), ERR_SCALE, flat(W0_t), flat(w0n), w0n_ready)
            dve.wait_ge(second_ready, 1)
            nc.vector.tensor_copy(second_w[:], p_second[:])
            dve.wait_ge(first_ready, 1)
            nc.vector.tensor_copy(first_w[:], p_first[:])


def memory_read(nc, sem, x_dram, y_dram, xt_dram, first_w, second_w):
    with ExitStack() as ctx:
        def pair(name, shape):
            return [ctx.enter_context(nc.sbuf_tensor(f"mr_{name}{u}", shape, F32)) for u in range(2)]

        xt, sig, hid = pair("xt", [P, DH, CH]), pair("sig", [P, DH, CH]), pair("hid", [P, DH, CH])
        x, y = pair("x", [P, 2, D]), pair("y", [P, 2, D])
        p_pre = [ctx.enter_context(nc.psum_tensor(f"mr_p_pre{u}", [P, DH, CH], F32)) for u in range(2)]
        p_out = [ctx.enter_context(nc.psum_tensor(f"mr_p_out{u}", [P, 2, D], F32)) for u in range(2)]
        xt_loaded, x_loaded, pre_ready, sig_ready, hid_ready, out_ready, y_ready, y_stored = (
            [sem(f"mr_{n}{u}") for u in range(2)] for n in (
                "xt_loaded", "x_loaded", "pre_ready", "sig_ready", "hid_ready", "out_ready", "y_ready", "y_stored"))
        n_it = NCH // 2
        rows = x_dram.rearrange("(n p) d -> p n d", p=P)
        out_rows = y_dram.rearrange("(n p) d -> p n d", p=P)
        block = ctx.enter_context(nc.Block())

        @block.sync
        def _(sp):
            with sp.Fori(0, n_it) as i:
                for u in range(2):
                    sp.wait_ge(pre_ready[u], i)
                    sp.dma_start(xt[u][:], xt_dram[bass.ds(i * 2 + u, 1), :, :, :].rearrange("c p h t -> (c p) h t")).then_inc(xt_loaded[u], 16)
                    sp.wait_ge(y_ready[u], i)
                    sp.dma_start(x[u][:], rows[:, bass.ds((i * 2 + u) * 2, 2), :]).then_inc(x_loaded[u], 16)

        @block.gpsimd
        def _(pool):
            with pool.Fori(0, n_it) as i:
                for u in range(2):
                    pool.wait_ge(y_ready[u], i + 1)
                    pool.dma_start(out_rows[:, bass.ds((i * 2 + u) * 2, 2), :], y[u][:]).then_inc(y_stored[u], 16)
            for u in range(2):
                pool.wait_ge(y_stored[u], 16 * n_it)

        @block.tensor
        def _(pe):
            def pre(u, i):
                pe.wait_ge(xt_loaded[u], i * 16 + 16)
                pe.wait_ge(hid_ready[u], i)
                for eh in range(DH):
                    for h in range(DH):
                        last = nc.tensor.matmul(p_pre[u][:, eh, :], first_w[:, h, eh * P:(eh + 1) * P], xt[u][:, h, :],
                                                start=h == 0, stop=h == DH - 1)
                last.then_inc(pre_ready[u], 1)

            def out(u, i):
                pe.wait_ge(hid_ready[u], i + 1)
                pe.wait_ge(y_ready[u], i)
                for t in range(2):
                    for eh in range(DH):
                        last = nc.tensor.matmul(p_out[u][:, t, :], hid[u][:, eh, t * P:(t + 1) * P], second_w[:, eh, :],
                                                start=eh == 0, stop=eh == DH - 1)
                last.then_inc(out_ready[u], 1)

            pre(0, 0)
            with pe.Fori(0, n_it - 1) as i:
                pre(1, i)
                out(0, i)
                pre(0, i + 1)
                out(1, i)
            pre(1, n_it - 1)
            out(0, n_it - 1)
            out(1, n_it - 1)

        @block.scalar
        def _(act):
            with act.Fori(0, n_it) as i:
                for u in range(2):
                    act.wait_ge(pre_ready[u], i + 1)
                    nc.scalar.activation(sig[u][:], p_pre[u][:], ACT.Sigmoid).then_inc(sig_ready[u], 1)

        @block.vector
        def _(dve):
            def hidden(u, i):
                dve.wait_ge(sig_ready[u], i + 1)
                dve.wait_ge(out_ready[u], i)
                nc.vector.tensor_tensor(hid[u][:], p_pre[u][:], sig[u][:], ALU.mult).then_inc(hid_ready[u], 1)

            def residual(u, i):
                dve.wait_ge(out_ready[u], i + 1)
                dve.wait_ge(x_loaded[u], i * 16 + 16)
                dve.wait_ge(y_stored[u], i * 16)
                nc.vector.tensor_tensor(y[u][:], p_out[u][:], x[u][:], ALU.add).then_inc(y_ready[u], 1)

            hidden(0, 0)
            with dve.Fori(0, n_it - 1) as i:
                hidden(1, i)
                residual(0, i)
                hidden(0, i + 1)
                residual(1, i)
            hidden(1, n_it - 1)
            residual(0, n_it - 1)
            residual(1, n_it - 1)


def neural_memory(nc, sem, x_dram, y_dram, xln_dram, xt_dram, ident_dram, Wk, Wv, Wq, Wout, W0, W1, gate_w, gate_b):
    with ExitStack() as ctx:
        def sb(name, shape=(P, DH, D)):
            return ctx.enter_context(nc.sbuf_tensor("nm_" + name, list(shape), F32))

        w = {n: sb(n) for n in ("Wk", "W1", "W0T", "WkT", "minusWvT", "W1T", "WoutT", "W0WkT")}
        grad1, grad0t, first_w, second_w = sb("grad1"), sb("grad0t"), sb("first_w"), sb("second_w")
        feature_stats = sb("feature_stats", (P, DH, NBLK, 6))
        memory_prepare(nc, sem, ident_dram, Wk, Wv, Wout, W0, W1, w)
        layer_norm_pass(nc, sem, "nm_ln_", x_dram, xt_dram, ident_dram, feature_stats, xln_dram=xln_dram)
        memory_gradients(nc, sem, xln_dram, xt_dram, ident_dram, w, grad1, grad0t)
        memory_update(nc, sem, ident_dram, feature_stats, gate_w, gate_b, w["W0T"], Wq, w, grad1, grad0t, first_w, second_w)
        memory_read(nc, sem, x_dram, y_dram, xt_dram, first_w, second_w)


AH, DK, DC = 16, 16, 64
HG = 4
NU = BATCH * AH // HG
GD = HG * DK
QT, QB, STEP = SEQ // P, SEQ // BLK, BLK // P
PAIRS = ((0, 0), (0, 1), (1, 0), (0, 2), (2, 0), (1, 1))
KS_ROWS = len(PAIRS) * DK
M_ROWS = 3
NEG = -1e30


def attention_project(nc, sem, xt_dram, qk_dram, v_dram, W_dq, W_dkv, W_uq, W_uk, W_uv):
    with ExitStack() as ctx:
        def sb(name, shape, dt=F32):
            return ctx.enter_context(nc.sbuf_tensor("ap_" + name, shape, dt))

        def pair(name, shape, dt=F32):
            return [sb(f"{name}{u}", shape, dt) for u in range(2)]

        down, up = sb("down", [P, DH, 2 * DC]), {n: sb("up_" + n, [P, D]) for n in "qkv"}
        xt, ct = pair("xt", [P, DH, CH]), pair("ct", [P, CH])
        parts = {n: pair("parts_" + n, [P, 3, DH, CH], BF16) for n in "qk"}
        rest = {n: pair("rest_" + n, [P, DH, CH]) for n in "qk"}
        v = pair("v", [P, AH // HG, 2, HG, 32])
        p_c = ctx.enter_context(nc.psum_tensor("ap_p_c", [P, 512], F32))
        p_up = {n: [ctx.enter_context(nc.psum_tensor(f"ap_p_{n}{u}", [P, DH, CH], F32)) for u in range(2)] for n in "qkv"}
        up_zero, weights = sem("ap_up_zero"), sem("ap_weights")
        s = {n: [sem(f"ap_{n}{u}") for u in range(2)] for n in (
            "xt_loaded", "c_ready", "c_copied", "q_ready", "k_ready", "v_ready", "first_q", "first_k", "rest_q",
            "rest_k", "second_q", "second_k", "third_q", "third_k", "v_copied", "stored", "v_zero")}
        n_it = SEQ // CH // 2
        scale = {"q": 0.25, "k": 1.0}
        block = ctx.enter_context(nc.Block())

        @block.sync
        def _(sp):
            for i, w in enumerate((W_dq, W_dkv)):
                sp.dma_start(down[:, :, i * DC:(i + 1) * DC], w.rearrange("(h p) c -> p h c", p=P)).then_inc(weights, 16)
            sp.wait_ge(up_zero, 3)
            sp.dma_start(up["q"][0:DC, :], W_uq).then_inc(weights, 16)
            sp.dma_start(up["k"][DC:P, :], W_uk).then_inc(weights, 16)
            sp.dma_start(up["v"][DC:P, :], W_uv).then_inc(weights, 16)
            with sp.Fori(0, BATCH * n_it) as i:
                for u in range(2):
                    sp.wait_ge(s["c_ready"][u], i)
                    sp.dma_start(xt[u][:], xt_dram[bass.ds(i * 2 + u, 1), :, :, :].rearrange("c p h t -> (c p) h t")).then_inc(s["xt_loaded"][u], 16)

        @block.gpsimd
        def _(pool):
            for n in "qkv":
                nc.gpsimd.memset(up[n][:], 0.0).then_inc(up_zero, 1)
            with pool.Fori(0, BATCH) as b:
                with pool.Fori(0, n_it) as j:
                    for u in range(2):
                        n = b * n_it + j
                        for k, name in enumerate("qk"):
                            pool.wait_ge(s["third_" + name][u], n + 1)
                            for h in range(DH):
                                dst = qk_dram[k, :, bass.ds(b * D + h * P, P), bass.ds((j * 2 + u) * CH, CH)].rearrange("a r t -> r a t")
                                pool.dma_start(dst, parts[name][u][:, :, h, :]).then_inc(s["stored"][u], 16)
                        pool.wait_ge(s["v_copied"][u], n + 1)
                        dst = v_dram[bass.ds(b * (NU // BATCH), NU // BATCH), :, bass.ds((j * 2 + u) * 2 * P, 2 * P)].rearrange("g p c -> p g c")
                        pool.dma_start(dst, v[u][:].rearrange("p g t h c -> p g (t h c)")).then_inc(s["stored"][u], 16)
            for u in range(2):
                pool.wait_ge(s["stored"][u], 80 * BATCH * n_it)

        @block.tensor
        def _(pe):
            pe.wait_ge(weights, 80)
            with pe.Fori(0, BATCH * n_it) as i:
                for u in range(2):
                    pe.wait_ge(s["xt_loaded"][u], i * 16 + 16)
                    if u:
                        pe.wait_ge(s["c_copied"][0], i + 1)
                    else:
                        pe.wait_ge(s["c_copied"][1], i)
                    for h in range(DH):
                        last = nc.tensor.matmul(p_c[:, 0:CH], down[:, h, :], xt[u][:, h, :], start=h == 0, stop=h == DH - 1)
                    last.then_inc(s["c_ready"][u], 1)
                    pe.wait_ge(s["c_copied"][u], i + 1)
                    for name in "qk":
                        pe.wait_ge(s["rest_" + name][u], i)
                        for h in range(DH):
                            last = nc.tensor.matmul(p_up[name][u][:, h, :], up[name][:, h * P:(h + 1) * P], ct[u][:], start=True, stop=True)
                        last.then_inc(s[name + "_ready"][u], 1)
                    pe.wait_ge(s["v_copied"][u], i)
                    for t in range(2):
                        last = nc.tensor.matmul(p_up["v"][u][:, t, :], ct[u][:, t * P:(t + 1) * P], up["v"][:], start=True, stop=True)
                    last.then_inc(s["v_ready"][u], 1)

        @block.scalar
        def _(act):
            for u in range(2):
                act.wait_ge(s["v_zero"][u], 2)
            with act.Fori(0, BATCH * n_it) as i:
                for u in range(2):
                    act.wait_ge(s["c_ready"][u], i + 1)
                    act.wait_ge(s["v_ready"][u], i)
                    nc.scalar.copy(ct[u][:], p_c[:, 0:CH]).then_inc(s["c_copied"][u], 1)
                    act.wait_ge(s["stored"][u], i * 80)
                    for name in "qk":
                        act.wait_ge(s[name + "_ready"][u], i + 1)
                        nc.scalar.mul(parts[name][u][:, 0, :, :], p_up[name][u][:], scale[name]).then_inc(s["first_" + name][u], 1)
                    act.wait_ge(s["v_ready"][u], i + 1)
                    for t in range(2):
                        last = nc.scalar.copy(v[u][:, :, t, :, 0:DK], p_up["v"][u][:, t, :].rearrange("p (g h c) -> p g h c", h=HG, c=DK))
                    last.then_inc(s["v_copied"][u], 1)
                    for name in "qk":
                        act.wait_ge(s["rest_" + name][u], i + 1)
                        nc.scalar.copy(parts[name][u][:, 1, :, :], rest[name][u][:]).then_inc(s["second_" + name][u], 1)

        @block.vector
        def _(dve):
            for u in range(2):
                nc.vector.memset(v[u][:], 0.0).then_inc(s["v_zero"][u], 1)
                dve.wait_ge(s["v_zero"][u], 1)
                nc.vector.memset(v[u][:, :, :, :, DK:DK + 1].rearrange("p g t h c -> p (g t h) c"), 1.0).then_inc(s["v_zero"][u], 1)
            with dve.Fori(0, BATCH * n_it) as i:
                for u in range(2):
                    for name in "qk":
                        dve.wait_ge(s["first_" + name][u], i + 1)
                        dve.wait_ge(s["third_" + name][u], i)
                        nc.vector.scalar_tensor_tensor(rest[name][u][:], p_up[name][u][:], scale[name], parts[name][u][:, 0, :, :],
                                                       ALU.mult, ALU.subtract).then_inc(s["rest_" + name][u], 1)
                    for name in "qk":
                        dve.wait_ge(s["second_" + name][u], i + 1)
                        nc.vector.tensor_tensor(parts[name][u][:, 2, :, :], rest[name][u][:], parts[name][u][:, 1, :, :],
                                                ALU.subtract).then_inc(s["third_" + name][u], 1)


def attention_plan():
    steps = [(qb, kt) for qb in range(QB) for kt in range(STEP * qb + STEP)]
    weight = [2 * 2 * (BLK - P * max(0, kt - STEP * qb)) + 400 for qb, kt in steps]
    pieces = [("max", h, qt, kb) for h in range(HG) for qt in range(QT) for kb in range(qt // STEP + 1)]
    cost = [min(BLK, (qt + 1) * P - kb * BLK) + 120 for _, h, qt, kb in pieces]
    until = len(steps) - 3
    share, done, k, turns = sum(cost) / sum(weight[:until]), 0.0, 0, []
    passed = 0.0
    for i in range(len(steps)):
        passed += weight[i] * share
        here = []
        while k < len(pieces) and (done + cost[k] / 2 < passed or i == until - 1):
            here.append(pieces[k])
            done += cost[k]
            k += 1
        if i == until:
            here.append(("m",))
        turns.append(here)
    ends = [i for i, (qb, kt) in enumerate(steps) if kt == STEP * qb + STEP - 1]
    for qb, e in enumerate(ends[:-1]):
        turns[e + 2].append(("o", qb))
    return steps, turns, ends, pieces


def attention_units(nc, sem, qk_dram, v_dram, ao_dram, ident_dram):
    steps, turns, ends, pieces = attention_plan()
    NST, RING, SLOTS = len(steps), 3, 3
    TURNS = sum(map(len, turns)) + 1
    FIRST = len(pieces) + 1
    assert TURNS % RING == 0
    with ExitStack() as ctx:
        def sb(name, shape, dt=F32):
            return ctx.enter_context(nc.sbuf_tensor("at_" + name, shape, dt))

        def pb(name, shape):
            return ctx.enter_context(nc.psum_tensor("at_" + name, shape, F32))

        ident, identb = sb("ident", [P, P]), sb("identb", [P, P], BF16)
        mask_rows, mask_cols = sb("mask_rows", [P, P], BF16), sb("mask_cols", [P, P], BF16)
        q = [sb(f"q{i}", [P, HG, SEQ], BF16) for i in range(SLOTS)]
        k = [sb(f"k{i}", [P, HG, SEQ], BF16) for i in range(SLOTS)]
        v = [sb(f"v{i}", [P, QT, HG, 32]) for i in range(SLOTS)]
        prob = [sb(f"prob{i}", [P, HG, BLK]) for i in range(2)]
        part_max, row_max = sb("part_max", [P, HG * QT, QB]), sb("row_max", [P, P])
        m_rows, m_rest = sb("m_rows", [HG * QT, M_ROWS, P], BF16), sb("m_rest", [HG * QT, P])
        out_t, ao, recip = sb("out_t", [P, BLK]), sb("ao", [P, STEP, GD]), sb("recip", [P, STEP, HG])
        p_s = [pb(f"p_s{i}", [P, 2, BLK]) for i in range(2)]
        p_o = pb("p_o", [P, BLK])
        p_ring = [pb(f"p_ring{i}", [P, BLK]) for i in range(RING)]
        names = ("ident_loaded", "made", "mask_zero", "turn_ready", "turn_taken", "row_max_ready", "m_first", "m_steps", "m_ready",
                 "m_loaded", "s_ready", "prob_ready", "pv_done", "out_done", "out_copied", "ao_steps", "ao_ready", "ao_stored",
                 "floor_set")
        s = {n: sem("at_" + n) for n in names}
        loaded = [sem(f"at_loaded{i}") for i in range(SLOTS)]
        N_LOADS = 2 * len(PAIRS) + 1
        block = ctx.enter_context(nc.Block())

        def above(eng, what, value):
            if not isinstance(value, int) or value > 0:
                eng.wait_ge(what, value)

        def units(eng, unit):
            with eng.Fori(0, NU // SLOTS) as i:
                for slot in range(SLOTS):
                    unit(i * SLOTS + slot, slot, i)
            for n in range(NU // SLOTS * SLOTS, NU):
                unit(n, n % SLOTS, n // SLOTS)

        @block.gpsimd
        def _(pool):
            nc.gpsimd.memset(mask_rows[:], 0.0).then_inc(s["mask_zero"], 1)
            nc.gpsimd.memset(mask_cols[:], 0.0).then_inc(s["mask_zero"], 1)
            pool.wait_ge(s["mask_zero"], 2)
            nc.gpsimd.affine_select(out=mask_rows[:], in_=mask_rows[:], compare_op=ALU.is_ge, fill=NEG, base=0,
                                    pattern=[[-1, P]], channel_multiplier=1).then_inc(s["made"], 1)
            nc.gpsimd.affine_select(out=mask_cols[:], in_=mask_cols[:], compare_op=ALU.is_ge, fill=NEG, base=0,
                                    pattern=[[1, P]], channel_multiplier=-1).then_inc(s["made"], 1)

            def store(n, slot, it):
                for qb in range(QB):
                    pool.wait_ge(s["ao_ready"], n * QB + qb + 1)
                    pool.dma_start(ao_dram[bass.ds(n, 1), qb * BLK:(qb + 1) * BLK, :].rearrange("n (t p) c -> p (n t) c", p=P),
                                   ao[:]).then_inc(s["ao_stored"], 16)

            units(pool, store)
            pool.wait_ge(s["ao_stored"], 16 * NU * QB)

        @block.sync
        def _(sp):
            sp.dma_start(ident[:], ident_dram).then_inc(s["ident_loaded"], 16)

            def load(n, slot):
                for r, (pq, pk) in enumerate(PAIRS):
                    for which, tile, part in ((0, q, pq), (1, k, pk)):
                        src = qk_dram[which, part, bass.ds(n * GD, GD), :].rearrange("(h d) t -> d h t", d=DK)
                        sp.dma_start(tile[slot][r * DK:(r + 1) * DK, :, :], src).then_inc(loaded[slot], 16)
                sp.dma_start(v[slot][:].rearrange("p t h c -> p (t h c)"), v_dram[bass.ds(n, 1), :, :].rearrange("n p c -> (n p) c")).then_inc(loaded[slot], 16)

            def rows(n, slot):
                sp.wait_ge(s["m_ready"], n + 1)
                for a in range(M_ROWS):
                    dst = q[slot][KS_ROWS + a:KS_ROWS + a + 1, :, :].rearrange("o h t -> o (h t)").rearrange("o (x p) -> o x p", p=P)
                    sp.dma_start(dst, m_rows[:, a, :]).then_inc(s["m_loaded"], 16)

            for n in range(2):
                load(n, n)
            rows(0, 0)
            with sp.Fori(0, NU // SLOTS) as i:
                for slot in range(SLOTS):
                    n = i * SLOTS + slot
                    sp.wait_ge(s["pv_done"], n * NST)
                    load(n + 2, (slot + 2) % SLOTS)
                    rows(n + 1, (slot + 1) % SLOTS)
            rows(NU - 1, (NU - 1) % SLOTS)

        def turn_base(n):
            return n * TURNS + FIRST

        @block.tensor
        def _(pe):
            def ring(number, index):
                above(pe, s["turn_taken"], number - (RING - 1))
                return p_ring[index % RING]

            def take_max(number, index, piece, slot):
                _, h, qt, kb = piece
                bank = ring(number, index)
                n = min(BLK, (qt + 1) * P - kb * BLK)
                diagonal = kb == qt // STEP
                last = nc.tensor.matmul(bank[:, 0:n], q[slot][0:KS_ROWS, h, qt * P:(qt + 1) * P],
                                        k[slot][0:KS_ROWS, h, kb * BLK:kb * BLK + n], start=True, stop=not diagonal)
                if diagonal:
                    last = nc.tensor.matmul(bank[:, n - P:n], identb[:], mask_rows[:], start=False, stop=True)
                last.then_inc(s["turn_ready"], 1)

            def turn_maxima(number, index, n):
                bank = ring(number, index)
                pe.wait_ge(s["row_max_ready"], n + 1)
                nc.tensor.transpose(bank[:, 0:P], row_max[:], ident[:]).then_inc(s["turn_ready"], 1)

            def turn_output(number, index, n, qb):
                bank = ring(number, index)
                pe.wait_ge(s["out_copied"], n * QB + qb + 1)
                for t in range(STEP):
                    last = nc.tensor.transpose(bank[:, t * P:(t + 1) * P], out_t[:, t * P:(t + 1) * P], ident[:])
                last.then_inc(s["turn_ready"], 1)

            def scores(n, slot, i):
                qb, kt = steps[i]
                off = P * max(0, kt - STEP * qb)
                for pair in range(2):
                    above(pe, s["prob_ready"], n * 2 * NST + max(2 * i + pair - 1, 0))
                    for j in range(2):
                        h = 2 * pair + j
                        diagonal = kt >= STEP * qb
                        last = nc.tensor.matmul(p_s[pair][:, j, off:BLK], k[slot][0:KS_ROWS + M_ROWS, h, kt * P:(kt + 1) * P],
                                                q[slot][0:KS_ROWS + M_ROWS, h, qb * BLK + off:(qb + 1) * BLK],
                                                start=True, stop=not diagonal)
                        if diagonal:
                            last = nc.tensor.matmul(p_s[pair][:, j, off:off + P], identb[:], mask_cols[:], start=False, stop=True)
                    last.then_inc(s["s_ready"], 1)

            def weigh_values(n, slot, i):
                qb, kt = steps[i]
                off = P * max(0, kt - STEP * qb)
                pe.wait_ge(s["prob_ready"], n * 2 * NST + 2 * i + 2)
                if kt == 0:
                    above(pe, s["out_copied"], n * QB + qb)
                for h in range(HG):
                    last = nc.tensor.matmul(p_o[32 * h:32 * h + 32, off:BLK], v[slot][:, kt, h, :], prob[i % 2][:, h, off:BLK],
                                            start=kt == 0, stop=kt == STEP * qb + STEP - 1)
                last.then_inc(s["pv_done"], 1)
                return kt == STEP * qb + STEP - 1

            def unit(n, slot, it):
                last_unit = isinstance(n, int) and n == NU - 1
                nxt = (slot + 1) % SLOTS
                if not last_unit:
                    pe.wait_ge(loaded[nxt], (it + (nxt == 0)) * 16 * N_LOADS + 16 * N_LOADS)
                pe.wait_ge(s["m_loaded"], n * 16 * M_ROWS + 16 * M_ROWS)
                base, count = turn_base(n), 0
                for i in range(NST):
                    scores(n, slot, i)
                    for turn in turns[i]:
                        if turn[0] == "o":
                            turn_output(base + count, FIRST + count, n, turn[1])
                        elif last_unit:
                            continue
                        elif turn[0] == "m":
                            turn_maxima(base + count, FIRST + count, n + 1)
                        else:
                            take_max(base + count, FIRST + count, turn, nxt)
                        count += 1
                    if i:
                        weigh_values(n, slot, i - 1)
                weigh_values(n, slot, NST - 1)
                turn_output(base + count, FIRST + count, n, QB - 1)

            pe.wait_ge(s["ident_loaded"], 16)
            pe.wait_ge(s["made"], 6)
            pe.wait_ge(loaded[0], 16 * N_LOADS)
            for c, piece in enumerate(pieces):
                take_max(c, c, piece, 0)
            turn_maxima(FIRST - 1, FIRST - 1, 0)
            units(pe, unit)

        @block.scalar
        def _(act):
            def first_part(n):
                act.wait_ge(s["turn_ready"], M_TURN[0] if isinstance(n, int) and n == 0 else turn_base(n - 1) + M_TURN[1] + 1)
                act.wait_ge(s["m_loaded"], n * 16 * M_ROWS) if not (isinstance(n, int) and n == 0) else None
                b = (FIRST - 1 if isinstance(n, int) and n == 0 else FIRST + M_TURN[1]) % RING
                nc.scalar.mul(m_rows[:, 0, :], p_ring[b][0:HG * QT, 0:P], -1.0).then_inc(s["m_first"], 1)

            flat_turns = [t for ts in turns for t in ts]
            M_TURN = (FIRST, flat_turns.index(("m",)))

            def copy_out(n, qb, i):
                act.wait_ge(s["pv_done"], n * NST + i + 1)
                above(act, s["ao_ready"], n * QB + qb)
                nc.scalar.copy(out_t[:], p_o[:]).then_inc(s["out_copied"], 1)

            def unit(n, slot, it):
                last_unit = isinstance(n, int) and n == NU - 1
                for i, (qb, kt) in enumerate(steps):
                    off = P * max(0, kt - STEP * qb)
                    for pair in range(2):
                        act.wait_ge(s["s_ready"], n * 2 * NST + 2 * i + pair + 1)
                        above(act, s["pv_done"], n * NST + max(i - 1, 0))
                        nc.scalar.activation(prob[i % 2][:, 2 * pair:2 * pair + 2, off:BLK], p_s[pair][:, :, off:BLK],
                                             ACT.Exp).then_inc(s["prob_ready"], 1)
                    if i - 1 in ends:
                        copy_out(n, ends.index(i - 1), i - 1)
                    if ("m",) in turns[i] and not last_unit:
                        first_part(n + 1)
                copy_out(n, QB - 1, NST - 1)

            first_part(0)
            units(act, unit)

        @block.vector
        def _(dve):
            def take_max(number, index, piece):
                _, h, qt, kb = piece
                n = min(BLK, (qt + 1) * P - kb * BLK)
                dve.wait_ge(s["turn_ready"], number + 1)
                nc.vector.reduce_max(part_max[:, h * QT + qt, kb:kb + 1], p_ring[index % RING][:, 0:n], axis=AX.X).then_inc(s["turn_taken"], 1)

            def maxima(number, n):
                dve.wait_ge(s["turn_taken"], number)
                nc.vector.reduce_max(row_max[:, 0:HG * QT], part_max[:], axis=AX.X).then_inc(s["row_max_ready"], 1)

            def split_maxima(number, index, n):
                dve.wait_ge(s["m_first"], n + 1)
                bank = p_ring[index % RING][0:HG * QT, 0:P]
                nc.vector.scalar_tensor_tensor(m_rest[:], bank, -1.0, m_rows[:, 0, :], ALU.mult, ALU.subtract).then_inc(s["turn_taken"], 1)
                dve.wait_ge(s["turn_taken"], number + 1)
                nc.vector.tensor_copy(m_rows[:, 1, :], m_rest[:]).then_inc(s["m_steps"], 1)
                dve.wait_ge(s["m_steps"], n + 1)
                nc.vector.tensor_tensor(m_rows[:, 2, :], m_rest[:], m_rows[:, 1, :], ALU.subtract).then_inc(s["m_ready"], 1)

            def normalise(number, index, n, qb):
                dve.wait_ge(s["turn_ready"], number + 1)
                bank = p_ring[index % RING][:].rearrange("p (t h c) -> p t h c", t=STEP, h=HG)
                nc.vector.reciprocal(recip[:], bank[:, :, :, DK]).then_inc(s["ao_steps"], 1)
                above(dve, s["ao_stored"], (n * QB + qb) * 16)
                dve.wait_ge(s["ao_steps"], n * QB + qb + 1)
                nc.vector.tensor_tensor(ao[:].rearrange("p t (h c) -> p t h c", h=HG), bank[:, :, :, 0:DK],
                                        recip[:].unsqueeze(3).to_broadcast([P, STEP, HG, DK]), ALU.mult).then_inc(s["turn_taken"], 1)
                dve.wait_ge(s["turn_taken"], number + 1)
                nc.vector.memset(junk[:], 0.0).then_inc(s["ao_ready"], 1)

            def unit(n, slot, it):
                last_unit = isinstance(n, int) and n == NU - 1
                base, count = turn_base(n), 0
                for i in range(NST):
                    for turn in turns[i]:
                        if turn[0] == "o":
                            normalise(base + count, FIRST + count, n, turn[1])
                        elif last_unit:
                            continue
                        elif turn[0] == "m":
                            maxima(base + count, n + 1)
                            split_maxima(base + count, FIRST + count, n + 1)
                        else:
                            take_max(base + count, FIRST + count, turn)
                        count += 1
                normalise(base + count, FIRST + count, n, QB - 1)

            junk = sb("junk", [P, 1])
            dve.wait_ge(s["ident_loaded"], 16)
            nc.vector.tensor_copy(identb[:], ident[:]).then_inc(s["made"], 1)
            for i in range(SLOTS):
                nc.vector.memset(k[i][KS_ROWS:KS_ROWS + M_ROWS, :, :], 1.0).then_inc(s["made"], 1)
            nc.vector.memset(row_max[:], 0.0)
            nc.vector.memset(part_max[:], NEG).then_inc(s["floor_set"], 1)
            dve.wait_ge(s["floor_set"], 1)
            for c, piece in enumerate(pieces):
                take_max(c, c, piece)
            maxima(FIRST - 1, 0)
            split_maxima(FIRST - 1, FIRST - 1, 0)
            units(dve, unit)


def attention_output(nc, sem, x_dram, y_dram, ao_dram, ident_dram, W_o):
    with ExitStack() as ctx:
        def pair(name, shape):
            return [ctx.enter_context(nc.sbuf_tensor(f"ao_{name}{u}", shape, F32)) for u in range(2)]

        NG_ = AH // HG
        ident, wo = (ctx.enter_context(nc.sbuf_tensor("ao_" + n, sh, F32)) for n, sh in (("ident", [P, P]), ("wo", [P, DH, D])))
        rows, rows_t, x, y = pair("rows", [P, 2, NG_, GD]), pair("rows_t", [P, DH, CH]), pair("x", [P, 2, D]), pair("y", [P, 2, D])
        p_t = [ctx.enter_context(nc.psum_tensor(f"ao_p_t{u}", [P, DH, CH], F32)) for u in range(2)]
        p_y = [ctx.enter_context(nc.psum_tensor(f"ao_p_y{u}", [P, 2, D], F32)) for u in range(2)]
        consts = sem("ao_consts")
        rows_loaded, x_loaded, turned, copied, summed, y_ready, y_stored = (
            [sem(f"ao_{n}{u}") for u in range(2)] for n in ("rows_loaded", "x_loaded", "turned", "copied", "summed", "y_ready", "y_stored"))
        n_it = SEQ // CH // 2
        xin, yout = (d.rearrange("(n p) d -> p n d", p=P) for d in (x_dram, y_dram))
        block = ctx.enter_context(nc.Block())

        @block.sync
        def _(sp):
            sp.dma_start(ident[:], ident_dram).then_inc(consts, 16)
            sp.dma_start(wo[:], W_o.rearrange("(h p) d -> p h d", p=P)).then_inc(consts, 16)
            with sp.Fori(0, BATCH) as b:
                with sp.Fori(0, n_it) as j:
                    for u in range(2):
                        sp.wait_ge(turned[u], b * n_it + j)
                        for t in range(2):
                            src = ao_dram[bass.ds(b * NG_, NG_), bass.ds(((j * 2 + u) * 2 + t) * P, P), :].rearrange("g p c -> p g c")
                            sp.dma_start(rows[u][:, t, :, :], src).then_inc(rows_loaded[u], 16)
                        sp.wait_ge(y_ready[u], b * n_it + j)
                        sp.dma_start(x[u][:], xin[:, bass.ds((b * n_it + j) * 4 + u * 2, 2), :]).then_inc(x_loaded[u], 16)

        @block.gpsimd
        def _(pool):
            with pool.Fori(0, BATCH * n_it) as i:
                for u in range(2):
                    pool.wait_ge(y_ready[u], i + 1)
                    pool.dma_start(yout[:, bass.ds(i * 4 + u * 2, 2), :], y[u][:]).then_inc(y_stored[u], 16)
            for u in range(2):
                pool.wait_ge(y_stored[u], 16 * BATCH * n_it)

        @block.tensor
        def _(pe):
            pe.wait_ge(consts, 32)
            with pe.Fori(0, BATCH * n_it) as i:
                for u in range(2):
                    pe.wait_ge(rows_loaded[u], i * 32 + 32)
                    pe.wait_ge(copied[u], i)
                    for h in range(DH):
                        for t in range(2):
                            last = nc.tensor.transpose(p_t[u][:, h, t * P:(t + 1) * P],
                                                       rows[u][:, t, :, :].rearrange("p g c -> p (g c)")[:, h * P:(h + 1) * P], ident[:])
                    last.then_inc(turned[u], 1)
                    pe.wait_ge(copied[u], i + 1)
                    pe.wait_ge(y_ready[u], i)
                    for t in range(2):
                        for h in range(DH):
                            last = nc.tensor.matmul(p_y[u][:, t, :], rows_t[u][:, h, t * P:(t + 1) * P], wo[:, h, :],
                                                    start=h == 0, stop=h == DH - 1)
                    last.then_inc(summed[u], 1)

        @block.scalar
        def _(act):
            with act.Fori(0, BATCH * n_it) as i:
                for u in range(2):
                    act.wait_ge(turned[u], i + 1)
                    act.wait_ge(summed[u], i)
                    nc.scalar.copy(rows_t[u][:], p_t[u][:]).then_inc(copied[u], 1)

        @block.vector
        def _(dve):
            with dve.Fori(0, BATCH * n_it) as i:
                for u in range(2):
                    dve.wait_ge(summed[u], i + 1)
                    dve.wait_ge(x_loaded[u], i * 16 + 16)
                    dve.wait_ge(y_stored[u], i * 16)
                    nc.vector.tensor_tensor(y[u][:], p_y[u][:], x[u][:], ALU.add).then_inc(y_ready[u], 1)


def attention(nc, sem, x_dram, y_dram, xt_dram, qk_dram, v_dram, ao_dram, ident_dram, W_dq, W_uq, W_dkv, W_uk, W_uv, W_o):
    with ExitStack() as ctx:
        feature_stats = ctx.enter_context(nc.sbuf_tensor("aa_feature_stats", [P, DH, NBLK, 6], F32))
        layer_norm_pass(nc, sem, "aa_ln_", x_dram, xt_dram, ident_dram, feature_stats)
        attention_project(nc, sem, xt_dram, qk_dram, v_dram, W_dq, W_dkv, W_uq, W_uk, W_uv)
        attention_units(nc, sem, qk_dram, v_dram, ao_dram, ident_dram)
        attention_output(nc, sem, x_dram, y_dram, ao_dram, ident_dram, W_o)


class StageSemaphores:

    def __init__(self, nc):
        self.nc, self.sems = nc, []

    def __enter__(self):
        return self.sem

    def sem(self, name):
        self.sems.append(self.nc.alloc_semaphore(name=name))
        return self.sems[-1]

    def __exit__(self, kind, value, trace):
        if kind is None:
            self.nc.all_engine_barrier()
            self.nc.clear_and_free_semaphores(self.sems)
            self.nc.all_engine_barrier()


def hybrid_block(nc, a, out):
    def scratch(name, shape, dt=F32):
        return nc.dram_tensor(name, shape, dt, kind="Internal").ap()

    x = a["L0_attn_a_x"].rearrange("b s d -> (b s) d")
    y = out.rearrange("b s d -> (b s) d")
    x1, x2, x3, xln = (scratch(n, (T, D)) for n in ("x1", "x2", "x3", "xln"))
    xt = scratch("xt", (NCH, P, DH, CH))
    ident = scratch("ident", (P, P))
    wct, kin = scratch("wct", (P, DH, NSUB)), scratch("kin_t", (P, DH, NE))
    qk = scratch("qk", (2, 3, BATCH * D, SEQ), BF16)
    v = scratch("v", (NU, P, QT * HG * 32))
    ao = scratch("attn_rows", (NU, SEQ, GD))

    def m(name):
        return a["L0_attn_a_" + name]

    def b(name):
        return a["L0_attn_b_" + name]

    def f(name):
        return a["L0_ffn_" + name]

    with StageSemaphores(nc) as sem:
        product_key_prepare(nc, sem, ident, f("w_q"), f("keys"), f("key_in"), wct, kin)
    with StageSemaphores(nc) as sem:
        neural_memory(nc, sem, x, x1, xln, xt, ident, m("Wk"), m("Wv"), m("Wq"), m("Wout"), m("W0"), m("W1"),
                      [m("Wg_decay"), m("Wg_lr"), m("Wg_mom")], [m("bg_decay"), m("bg_lr"), m("bg_mom")])
    with StageSemaphores(nc) as sem:
        product_key_memory(nc, sem, "f1_", x1, x2, xt, ident, wct, kin, f("key_out"), f("gamma"), f("beta"))
    with StageSemaphores(nc) as sem:
        attention(nc, sem, x2, x3, xt, qk, v, ao, ident, b("W_dq"), b("W_uq"), b("W_dkv"), b("W_uk"), b("W_uv"), b("W_o"))
    with StageSemaphores(nc) as sem:
        product_key_memory(nc, sem, "f2_", x3, y, xt, ident, wct, kin, f("key_out"), f("gamma"), f("beta"))


def kernel(**inputs):
    import numpy as _np
    import concourse.bacc as _bacc
    from concourse import mybir as _mybir
    from concourse.bass_utils import run_bass_kernel_spmd as _run

    nc = _bacc.Bacc("TRN2", target_bir_lowering=False, num_devices=1)
    arrays, aps = {}, {}
    for name, value in inputs.items():
        a = _np.ascontiguousarray(value)
        arrays[f"in_{name}"] = a
        aps[name] = nc.dram_tensor(f"in_{name}", a.shape, _mybir.dt.from_np(a.dtype), kind="ExternalInput").ap()
    out = nc.dram_tensor("out", (BATCH, SEQ, D), F32, kind="ExternalOutput").ap()
    hybrid_block(nc, aps, out)
    r = _run(nc, [arrays], core_ids=[0])
    return r.results[0]["out"]
```

```python
from contextlib import ExitStack

import concourse.bass as bass
from concourse import mybir

F32, F16, BF16 = mybir.dt.float32, mybir.dt.float16, mybir.dt.bfloat16
U16 = mybir.dt.uint16
ALU, ACT, AX = mybir.AluOpType, mybir.ActivationFunctionType, mybir.AxisListType

P = 128
D = 256
DH = D // P
BATCH, SEQ = 2, 2048
T = BATCH * SEQ
BLK = 512
BT = BLK // P
NBLK = T // BLK
CH = 256
NCH = T // CH
LN_EPS = 1e-5
ONE = 1


class Chain:

    def __init__(self, eng, sem, base=0):
        self.eng, self.sem, self.base, self.n = eng, sem, base, 0

    def mark(self, ins):
        self.n += 1
        return ins.then_inc(self.sem, 1)

    def wait(self):
        self.eng.wait_ge(self.sem, ONE + self.base + self.n)

    def link(self, ins):
        self.mark(ins)
        self.wait()


def newton_reciprocal(nc, chain, out, root, var_eps, tmp):
    chain.link(nc.vector.reciprocal(out, root))
    chain.link(nc.vector.tensor_tensor(tmp[:], out, out, ALU.mult))
    chain.link(nc.vector.tensor_tensor(tmp[:], tmp[:], var_eps, ALU.mult))
    chain.link(nc.vector.tensor_scalar(tmp[:], tmp[:], -0.5, 1.5, ALU.mult, ALU.add))
    return nc.vector.tensor_tensor(out, out, tmp[:], ALU.mult)


LNB = 4
LN_LINKS = LNB * (BT + BT + 5)


def layer_norm_pass(nc, sem, tag, x_dram, xt_dram, ident_dram, feature_stats=None, xln_dram=None,
                    prefetch=None):
    with ExitStack() as ctx:
        def sb(name, shape, dt=F32):
            return ctx.enter_context(nc.sbuf_tensor(tag + name, shape, dt))

        ident = sb("ident", [P, P])
        xin = [sb(f"xin{u}", [P, BT, D]) for u in range(LNB)]
        xln = [sb(f"xln{u}", [P, BT, D]) for u in range(2)]
        xt = [sb(f"xt{u}", [P, DH, BLK]) for u in range(2)]
        ln_stats, mv, gate = sb("ln_stats", [P, LNB, BT, 6]), sb("mv", [P, LNB, BT, 2]), sb("gate", [P, LNB])
        var_eps, rstd, ln_tmp = sb("var_eps", [P, LNB, BT]), sb("rstd", [P, LNB, BT]), sb("ln_tmp", [P, BT])
        pxt = [ctx.enter_context(nc.psum_tensor(f"{tag}pxt{u}", [P, DH, BLK], F32)) for u in range(2)]

        ident_loaded = sem(tag + "ident_loaded")
        x_loaded = [sem(f"{tag}x_loaded{u}") for u in range(LNB)]
        xln_stored = [sem(f"{tag}xln_stored{u}") for u in range(2)]
        xt_stored = [sem(f"{tag}xt_stored{u}") for u in range(2)]
        var_ready, root_ready = sem(tag + "var_ready"), sem(tag + "root_ready")
        xln_ready, xt_ready, xt_copied = sem(tag + "xln_ready"), sem(tag + "xt_ready"), sem(tag + "xt_copied")
        counted, steps = sem(tag + "counted"), sem(tag + "ln_steps")
        rows = x_dram.rearrange("(n p) d -> p n d", p=P)
        n_it = NBLK // LNB
        assert n_it == 2
        NK = BLK // CH
        block = ctx.enter_context(nc.Block())

        def blocks(eng, do):
            with eng.Fori(0, n_it) as i:
                for u in range(LNB):
                    do(i * LNB + u, u, i * (LNB // 2) + u // 2)

        def two_before(eng, what, b, u):
            eng.wait_ge(what, ONE + (b - 1 if u >= 1 else b))

        @block.sync
        def _(sp):
            def load(i, u):
                sp.dma_start(xin[u][:], rows[:, bass.ds((i * LNB + u) * BT, BT), :]).then_inc(x_loaded[u], 16)

            def stores(b, u):
                if xln_dram is not None:
                    sp.dma_start(xln_dram.rearrange("(n p) d -> p n d", p=P)[:, bass.ds(b * BT, BT), :],
                                 xln[u % 2][:]).then_inc(xln_stored[u % 2], 16)
                sp.wait_ge(xt_copied, ONE + b + 1)
                for k in range(NK):
                    sp.dma_start(xt_dram[bass.ds(b * NK + k, 1), :, :, :].rearrange("c p h t -> (c p) h t"),
                                 xt[u % 2][:, :, k * CH:(k + 1) * CH]).then_inc(xt_stored[u % 2], 16)

            for u in range(LNB):
                load(0, u)
            sp.dma_start(ident[:], ident_dram).then_inc(ident_loaded, 16)
            with sp.Fori(0, n_it - 1) as i:
                for u in range(LNB):
                    sp.wait_ge(xln_ready, ONE + i * LNB + u + 1)
                    load(i + 1, u)
                    stores(i * LNB + u, u)
                    if prefetch is not None:
                        prefetch(sp, 0, u)
            for u in range(LNB):
                sp.wait_ge(xln_ready, ONE + NBLK - LNB + u + 1)
                stores(NBLK - LNB + u, u)
                if prefetch is not None:
                    prefetch(sp, 1, u)
            for u in range(2):
                sp.wait_ge(xt_stored[u], ONE + 16 * NBLK // 2 * NK)
                if xln_dram is not None:
                    sp.wait_ge(xln_stored[u], ONE + 16 * NBLK // 2)

        @block.tensor
        def _(pe):
            def transpose(b, u, k):
                pe.wait_ge(xln_ready, ONE + b + 1)
                two_before(pe, xt_copied, b, u)
                for t in range(BT):
                    for dh in range(DH):
                        last = nc.tensor.transpose(pxt[u % 2][:, dh, t * P:(t + 1) * P],
                                                   xln[u % 2][:, t, dh * P:(dh + 1) * P], ident[:])
                last.then_inc(xt_ready, 1)

            pe.wait_ge(ident_loaded, ONE + 16)
            blocks(pe, transpose)

        @block.scalar
        def _(act):
            def root(b, u):
                act.wait_ge(var_ready, ONE + b + 1)
                nc.scalar.activation(rstd[:, u, :], var_eps[:, u, :], ACT.Sqrt).then_inc(root_ready, 1)

            def copy_xt(b, u, k):
                act.wait_ge(xt_ready, ONE + b + 1)
                act.wait_ge(xt_stored[u % 2], ONE + k * 16 * NK)
                if feature_stats is not None:
                    two_before(act, counted, b, u)
                nc.scalar.copy(xt[u % 2][:], pxt[u % 2][:]).then_inc(xt_copied, 1)

            with act.Fori(0, n_it) as i:
                root(i * LNB, 0)
                for u in range(LNB):
                    if u + 1 < LNB:
                        root(i * LNB + u + 1, u + 1)
                    copy_xt(i * LNB + u, u, i * (LNB // 2) + u // 2)

        @block.vector
        def _(dve):
            def statistics(b, u, chain):
                for t in range(BT):
                    chain.mark(nc.vector.bn_stats(ln_stats[:, u, t, :], xin[u][:, t, :]))
                chain.wait()
                nc.vector.memset(gate[:, u:u + 1], 0.0)
                for t in range(BT):
                    chain.mark(nc.vector.bn_aggr(mv[:, u, t, :], ln_stats[:, u, t, :]))
                chain.wait()
                nc.vector.tensor_scalar_add(var_eps[:, u, :], mv[:, u, :, 1], LN_EPS).then_inc(var_ready, 1)

            def deviations(b, u, chain):
                dve.wait_ge(root_ready, ONE + b + 1)
                chain.link(newton_reciprocal(nc, chain, rstd[:, u, :], rstd[:, u, :], var_eps[:, u, :], ln_tmp))

            def normalise(b, u, k):
                two_before(dve, xt_ready, b, u)
                if xln_dram is not None:
                    dve.wait_ge(xln_stored[u % 2], ONE + k * 16)
                for t in range(BT):
                    last = nc.vector.tensor_scalar(xln[u % 2][:, t, :], xin[u][:, t, :], mv[:, u, t, 0:1], rstd[:, u, t:t + 1],
                                                   ALU.subtract, ALU.mult)
                last.then_inc(xln_ready, 1)

            def count_features(b, u):
                dve.wait_ge(xt_copied, ONE + b + 1)
                for dh in range(DH):
                    last = nc.vector.bn_stats(feature_stats[:, dh, bass.ds(b, 1), :], xt[u % 2][:, dh, :])
                last.then_inc(counted, 1)

            with dve.Fori(0, n_it) as i:
                chain = Chain(dve, steps, i * LN_LINKS)
                for u in range(LNB + 2):
                    b = i * LNB + u
                    if 1 <= u <= LNB:
                        deviations(b - 1, u - 1, chain)
                        normalise(b - 1, u - 1, i * (LNB // 2) + (u - 1) // 2)
                    if u < LNB:
                        dve.wait_ge(x_loaded[u], ONE + i * 16 + 16)
                        if u == 0:
                            dve.wait_ge(xln_ready, ONE + i * LNB)
                        statistics(b, u, chain)
                    if u >= 2 and feature_stats is not None:
                        count_features(b - 2, u - 2)
                assert chain.n == LN_LINKS


NH, NK, KD, TOPK = 8, 64, 128, 8
NE = NK * NK
NSUB = 2 * NH * NK
HK = NH * TOPK
BN_EPS = 1e-5
NX = NE // P
PS = 16
NS = P // PS
PB = 8
NG = P // PB
VS = 4
E_SCALE = 16.0


def product_key_prepare(nc, sem, ident_dram, w_q, keys, key_in, wct_dram, kin_dram):
    with ExitStack() as ctx:
        def sb(name, shape, dt=F32):
            return ctx.enter_context(nc.sbuf_tensor(name, shape, dt))

        ident = sb("pp_ident", [P, P])
        kin = sb("pp_kin", [P, NX, D])
        kin_t = sb("pp_kin_t", [P, 2, DH, NE], F16)
        wq = sb("pp_wq", [P, 2 * NH, D])
        keyrows = sb("pp_keyrows", [P, NH, KD])
        keys_t = sb("pp_keys_t", [P, NH, NK, 2])
        wct = sb("pp_wct", [P, DH, NSUB])
        pt = [ctx.enter_context(nc.psum_tensor(f"pp_pt{i}", [P, 4, P], F32)) for i in range(2)]
        pw = [ctx.enter_context(nc.psum_tensor(f"pp_pw{i}", [P, 512], F32)) for i in range(4)]

        ident_zero, ident_ready = sem("pp_ident_zero"), sem("pp_ident_ready")
        kin_loaded, small_loaded = sem("pp_kin_loaded"), sem("pp_small_loaded")
        transposed, copied = sem("pp_transposed"), sem("pp_copied")
        product_ready, product_copied = sem("pp_product_ready"), sem("pp_product_copied")
        stored, kin_hi = sem("pp_stored"), sem("pp_kin_hi")
        KIN_STORES = 4 * DH
        n_keyt, n_kint = NH // 4, DH * NX // 4
        block = ctx.enter_context(nc.Block())

        @block.gpsimd
        def _(pool):
            nc.gpsimd.memset(ident[:], 0.0).then_inc(ident_zero, 1)
            pool.wait_ge(ident_zero, ONE + 1)
            nc.gpsimd.affine_select(out=ident[:], in_=ident[:], compare_op=ALU.not_equal, fill=1.0, base=0,
                                    pattern=[[-1, P]], channel_multiplier=1).then_inc(ident_ready, 1)

        @block.sync
        def _(sp):
            sp.dma_start(keyrows[:], keys.rearrange("h k s d -> (k s) h d")).then_inc(small_loaded, 16)
            sp.dma_start(wq[:], w_q.rearrange("(b k) d -> k b d", k=P)).then_inc(small_loaded, 16)
            for i in range(4):
                x = slice(i * NX // 4, (i + 1) * NX // 4)
                sp.dma_start(kin[:, x, :], key_in.rearrange("(x y) d -> y x d", y=P)[:, x, :]).then_inc(kin_loaded, 16)
            sp.wait_ge(ident_ready, ONE + 1)
            sp.dma_start(ident_dram, ident[:]).then_inc(stored, 16)
            sp.wait_ge(product_copied, ONE + 4)
            sp.dma_start(wct_dram, wct[:]).then_inc(stored, 16)
            for i in range(KIN_STORES):
                sp.wait_ge(copied, ONE + n_keyt + (i + 1) * n_kint // KIN_STORES)
                dh, k = i // 4, slice(i % 4 * (NE // 4), (i % 4 + 1) * (NE // 4))
                sp.dma_start(kin_dram[:, :, dh, k], kin_t[:, :, dh, k]).then_inc(stored, 16)
            sp.wait_ge(stored, ONE + 16 * (2 + KIN_STORES))

        @block.tensor
        def _(pe):
            pe.wait_ge(ident_ready, ONE + 1)
            pe.wait_ge(small_loaded, ONE + 32)
            for g in range(n_keyt):
                for j in range(4):
                    last = nc.tensor.transpose(pt[g % 2][:, j, :], keyrows[:, 4 * g + j, :], ident[:])
                last.then_inc(transposed, 1)
            pe.wait_ge(copied, ONE + n_keyt)
            for dh in range(DH):
                for side in range(2):
                    for h in range(NH):
                        last = nc.tensor.matmul(pw[2 * dh + side][:, h * NK:(h + 1) * NK],
                                                wq[:, side * NH + h, dh * P:(dh + 1) * P],
                                                keys_t[:, h, :, side], start=True, stop=True)
                    last.then_inc(product_ready, 1)
            pe.wait_ge(kin_loaded, ONE + 64)
            for g in range(n_kint):
                pe.wait_ge(copied, ONE + n_keyt + g - 1)
                dh, x0 = g // (NX // 4), 4 * (g % (NX // 4))
                for j in range(4):
                    last = nc.tensor.transpose(pt[g % 2][:, j, :], kin[:, x0 + j, dh * P:(dh + 1) * P], ident[:])
                last.then_inc(transposed, 1)

        @block.vector
        def _(dve):
            for g in range(n_keyt):
                dve.wait_ge(transposed, ONE + g + 1)
                nc.vector.tensor_copy(keys_t[:, 4 * g:4 * g + 4, :, :].rearrange("p h k s -> p (h k s)"),
                                      pt[g % 2][:].rearrange("p h k -> p (h k)")).then_inc(copied, 1)
            for g in range(n_kint):
                dve.wait_ge(transposed, ONE + n_keyt + g + 1)
                dh, x0 = g // (NX // 4), 4 * (g % (NX // 4))
                dve.wait_ge(kin_hi, ONE + g + 1)
                nc.vector.scalar_tensor_tensor(kin_t[:, 1, dh, x0 * P:(x0 + 4) * P],
                                               pt[g % 2][:].rearrange("p h k -> p (h k)"), E_SCALE,
                                               kin_t[:, 0, dh, x0 * P:(x0 + 4) * P], ALU.mult, ALU.subtract).then_inc(copied, 1)

        @block.scalar
        def _(act):
            for g in range(4):
                act.wait_ge(product_ready, ONE + g + 1)
                nc.scalar.copy(wct[:, g // 2, (g % 2) * 512:(g % 2 + 1) * 512], pw[g][:]).then_inc(product_copied, 1)
            for g in range(n_kint):
                act.wait_ge(transposed, ONE + n_keyt + g + 1)
                dh, x0 = g // (NX // 4), 4 * (g % (NX // 4))
                nc.scalar.mul(kin_t[:, 0, dh, x0 * P:(x0 + 4) * P], pt[g % 2][:].rearrange("p h k -> p (h k)"),
                              E_SCALE).then_inc(kin_hi, 1)


def product_key_memory(nc, sem, tag, x_dram, y_dram, xt_dram, ident_dram, wct_dram, kin_dram, key_out, gamma, beta):
    with ExitStack() as ctx:
        def sb(name, shape, dt=F32):
            return ctx.enter_context(nc.sbuf_tensor(tag + name, shape, dt))

        wct = sb("wct", [P, DH, NSUB])
        kin_t = sb("kin_t", [P, 2, DH, NE], F16)
        kout = sb("kout", [P, 2, NX, D], F16)
        scale = sb("scale", [P, DH])
        shift = sb("shift", [P, DH])
        y_hot = sb("y_hot", [P, NS, P, PS], F16)
        kout_rows = y_hot[:].rearrange("p s x t -> p (s x t)").bitcast(F32).rearrange("p (x d) -> p x d", d=D)
        weights_loaded, kout_loaded = sem(tag + "weights_loaded"), sem(tag + "kout_loaded")

        def load_weights(sp, turn, u):
            if turn == 0:
                k = slice(u * NE // LNB, (u + 1) * NE // LNB)
                sp.dma_start(kin_t[:, :, :, k].rearrange("p a h e -> p (a h) e"),
                             kin_dram[:, :, :, k].rearrange("p a h e -> p (a h) e")).then_inc(weights_loaded, 16)
            else:
                k = slice(u * NX // LNB, (u + 1) * NX // LNB)
                sp.dma_start(kout_rows[:, k, :], key_out.rearrange("(x y) d -> y x d", y=P)[:, k, :]).then_inc(kout_loaded, 16)
                if u == 0:
                    sp.dma_start(wct[:], wct_dram).then_inc(weights_loaded, 16)

        with ExitStack() as first:
            def fb(name, shape, dt=F32):
                return first.enter_context(nc.sbuf_tensor(tag + name, shape, dt))

            bn_st, bn_mv = fb("bn_st", [P, DH, NBLK, 6]), fb("bn_mv", [P, DH, 2])
            bn_var, bn_tmp, gb = fb("bn_var", [P, DH]), fb("bn_tmp", [P, DH]), fb("gb", [P, 2, DH])
            layer_norm_pass(nc, sem, tag + "ln_", x_dram, xt_dram, ident_dram, bn_st, prefetch=load_weights)

            gb_loaded, bn_steps = sem(tag + "gb_loaded"), sem(tag + "bn_steps")
            bn_var_ready, bn_root_ready = sem(tag + "bn_var_ready"), sem(tag + "bn_root_ready")
            block = first.enter_context(nc.Block())

            @block.sync
            def _(sp):
                with nc.allow_non_contiguous_dma(reason="512 scalars"):
                    sp.dma_start(gb[:, 0, :], gamma.rearrange("(h p) -> p h", p=P)).then_inc(gb_loaded, 16)
                    sp.dma_start(gb[:, 1, :], beta.rearrange("(h p) -> p h", p=P)).then_inc(gb_loaded, 16)

            @block.scalar
            def _(act):
                act.wait_ge(bn_var_ready, ONE + 1)
                nc.scalar.activation(scale[:], bn_var[:], ACT.Sqrt).then_inc(bn_root_ready, 1)

            @block.vector
            def _(dve):
                chain = Chain(dve, bn_steps)
                for dh in range(DH):
                    chain.mark(nc.vector.bn_aggr(bn_mv[:, dh, :], bn_st[:, dh, :, :].rearrange("p b s -> p (b s)")))
                chain.wait()
                nc.vector.tensor_scalar_add(bn_var[:], bn_mv[:, :, 1], BN_EPS).then_inc(bn_var_ready, 1)
                dve.wait_ge(bn_root_ready, ONE + 1)
                chain.link(newton_reciprocal(nc, chain, scale[:], scale[:], bn_var[:], bn_tmp))
                dve.wait_ge(gb_loaded, ONE + 32)
                chain.link(nc.vector.tensor_tensor(scale[:], scale[:], gb[:, 0, :], ALU.mult))
                chain.link(nc.vector.tensor_tensor(bn_tmp[:], bn_mv[:, :, 0], scale[:], ALU.mult))
                chain.link(nc.vector.tensor_tensor(shift[:], gb[:, 1, :], bn_tmp[:], ALU.subtract))

        routed_experts(nc, sem, tag, x_dram, y_dram, xt_dram, ident_dram, wct, kin_t, kout, scale, shift,
                       weights_loaded, kout_loaded, kout_rows, y_hot)


def routed_experts(nc, sem, tag, x_dram, y_dram, xt_dram, ident_dram, wct, kin_t, kout, scale, shift, weights_loaded,
                   kout_loaded, kout_rows, y_hot):
    with ExitStack() as ctx:
        def sb(name, shape, dt=F32):
            return ctx.enter_context(nc.sbuf_tensor(tag + name, shape, dt))

        def pb(name, shape):
            return ctx.enter_context(nc.psum_tensor(tag + name, shape, F32))

        ident = sb("ident2", [P, P])
        hidden = sb("hidden", [P, NX, CH])
        parts = hidden[:].rearrange("p x t -> p (x t)").bitcast(F16).rearrange("p (x t k) -> p x t k", x=NX, k=2)
        xt_in = sb("xt_in", [P, DH, CH])
        xt = sb("xtc", [P, 2, DH, CH], F16)
        xn = sb("xn", [P, DH, CH])
        sim = sb("sim", [P, 2, NSUB])
        top = sb("top", [P, 2, 2, NH, TOPK])
        top_key = sb("top_key", [P, 2, 2, NH, TOPK], U16)
        cand = sb("cand", [P, 2, NH, TOPK, TOPK])
        picked = cand[:].rearrange("p u h a b -> p (u h a b)").bitcast(F16).rearrange(
            "p (s g a k) -> p s g a k", s=2, g=2 * NH, a=TOPK)
        best = sb("best", [P, 2, NH, TOPK])
        best_at = sb("best_at", [P, 2 * NH * TOPK], U16)
        rank = sb("rank", [P, 2, 2 * NH, TOPK], U16)
        key = sb("key", [P, 2, 2 * HK])
        key_u = sb("key_u", [P, 2 * HK], U16)
        key_bit = sb("key_bit", [P, 2 * HK], U16)
        key_half = sb("key_half", [P, 2 * HK], U16)
        total = sb("total", [P, 2 * NH])
        expo = sb("expo", [P, 2 * NH, TOPK])
        picks = sb("picks", [P, 3, 2 * HK])
        xq, yq = sb("xq", [P, P], F16), sb("yq", [P, P], F16)
        p_hi, p_lo = sb("p_hi", [P, P], F16), sb("p_lo", [P, P], F16)
        rank_iota = sb("rank_iota", [P, TOPK, TOPK], U16)
        y_iota = sb("y_iota", [P, P, PS], F16)
        tile_base = sb("tile_base", [P, 1])
        x_hot = [sb(f"x_hot{i}", [P, 2 * NX, PS], F16) for i in range(2)]
        ring = [cand[:, u].rearrange("p h a b -> p (h a b)") for u in range(2)] + [
            x_hot[i][:].rearrange("p x t -> p (x t)").bitcast(F32) for i in range(2)]
        weighted = [r.rearrange("p (x u t) -> p x u t", x=NX, u=2) for r in ring]
        x_hi = sb("x_hi", [P, NS, 2 * NX, PS], F16)
        x_lo = sb("x_lo", [P, NS, 2 * NX, PS], F16)
        xres = sb("xres", [P, 2, D])
        gate = sb("gate", [P, 3])

        p_sim = pb("p_sim", [P, NSUB])
        p_route = [pb(f"p_route{i}", [P, PB, 2 * NX]) for i in range(2)]
        p_hid = [pb(f"p_hid{i}", [P, 2, CH]) for i in range(2)]
        p_out = pb("p_out", [P, 2, D])
        p_picks = pb("p_picks", [P, 3, P])

        consts_loaded, iota_ready = sem(tag + "consts_loaded"), sem(tag + "iota_ready")
        xt_loaded, xn_ready, xt_copied = sem(tag + "xt2_loaded"), sem(tag + "xn_ready"), sem(tag + "xt2_copied")
        sim_ready, sim_copied = sem(tag + "sim_ready"), sem(tag + "sim_copied")
        best_ready, exp_ready = sem(tag + "best_ready"), sem(tag + "exp_ready")
        picks_ready, picks_turned, picks_copied = sem(tag + "picks_ready"), sem(tag + "picks_turned"), sem(tag + "picks_copied")
        p_lo_ready, hot_ready = sem(tag + "p_lo_ready"), sem(tag + "hot_ready")
        route_ready, routed = sem(tag + "route_ready"), sem(tag + "routed")
        hid_ready, gelu_ready = sem(tag + "hid_ready"), sem(tag + "gelu_ready")
        xt_lo_ready, out_read = sem(tag + "xt_lo_ready"), sem(tag + "out_read")
        hi_ready, lo_ready, lo_ready_v = sem(tag + "hi_ready"), sem(tag + "lo_ready"), sem(tag + "lo_ready_v")
        x_loaded, y_ready, y_stored = sem(tag + "xres_loaded"), sem(tag + "y_ready"), sem(tag + "y_stored")
        hot_steps, x_lo_ready = sem(tag + "hot_steps"), sem(tag + "x_lo_ready")
        kout_scaled, kout_hi, kout_ready = sem(tag + "kout_scaled"), sem(tag + "kout_hi"), sem(tag + "kout_ready")
        steps, base_ready = sem(tag + "steps"), sem(tag + "base_ready")

        PAIRS = ((0, 0), (0, 1), (1, 0))

        def above(eng, s, value):
            if not isinstance(value, int) or value > 0:
                eng.wait_ge(s, ONE + value)

        SHARES = 8

        def share(b):
            return slice(b * NX // SHARES, (b + 1) * NX // SHARES)

        def split_ready(eng, c, g):
            eng.wait_ge(lo_ready, ONE + c * (NG - NG // VS) + g + 1 - (g + 1) // VS)
            if g + 1 >= VS:
                eng.wait_ge(lo_ready_v, ONE + c * (NG // VS) + (g + 1) // VS)

        def group_parts(g):
            v = parts.rearrange("p x (u t) k -> p x u t k", u=2)[:, :, :, g * PB:(g + 1) * PB, :]
            return v[:, :, :, :, 0], v[:, :, :, :, 1]

        block = ctx.enter_context(nc.Block())

        @block.gpsimd
        def _(pool):
            nc.gpsimd.iota(rank_iota[:], pattern=[[1, TOPK], [0, TOPK]], base=0, channel_multiplier=0,
                           allow_small_or_imprecise_dtypes=True).then_inc(iota_ready, 1)
            nc.gpsimd.iota(y_iota[:], pattern=[[1, P], [0, PS]], base=0, channel_multiplier=0,
                           allow_small_or_imprecise_dtypes=True).then_inc(iota_ready, 1)

            def split_xt(c):
                pool.wait_ge(xt_copied, ONE + c + 1)
                nc.gpsimd.tensor_tensor(xt[:, 1, :, :], xt_in[:], xt[:, 0, :, :], ALU.subtract).then_inc(xt_lo_ready, 1)

            def split_weighted(c):
                for g in range(NG):
                    if g % VS == VS - 1:
                        continue
                    pool.wait_ge(hi_ready, ONE + c * NG + g + 1)
                    hi, lo = group_parts(g)
                    nc.gpsimd.tensor_tensor(lo, weighted[g % 4], hi, ALU.subtract).then_inc(lo_ready, 1)

            def low_hots(c):
                pool.wait_ge(p_lo_ready, ONE + c + 1)
                for s in range(NS):
                    lo, hi = s * PS, (s + 1) * PS
                    pool.wait_ge(hot_steps, ONE + c * NS + s + 1)
                    above(pool, route_ready, (c - 1) * NG + (s + 1) * (PS // PB) if not isinstance(c, int) or c else 0)
                    nc.gpsimd.tensor_tensor(x_lo[:, s, :, :], x_hot[s % 2][:], p_lo[:, lo:hi].unsqueeze(1).to_broadcast([P, 2 * NX, PS]),
                                            ALU.mult).then_inc(x_lo_ready, 1)

            split_xt(0)
            for b in range(SHARES):
                pool.wait_ge(kout_hi, ONE + b + 1)
                x = share(b)
                nc.gpsimd.tensor_tensor(kout[:, 1, x, :], kout_rows[:, x, :], kout[:, 0, x, :], ALU.subtract).then_inc(kout_ready, 1)
            low_hots(0)
            with pool.Fori(0, NCH - 1) as c:
                split_xt(c + 1)
                split_weighted(c)
                low_hots(c + 1)
            split_weighted(NCH - 1)

        x_view = x_dram.rearrange("(n p) d -> p n d", p=P)
        y_view = y_dram.rearrange("(n p) d -> p n d", p=P)

        @block.sync
        def _(sp):
            def load_xt(c):
                above(sp, xt_lo_ready, c)
                sp.dma_start(xt_in[:], xt_dram[bass.ds(c, 1), :, :, :].rearrange("c p h t -> (c p) h t")).then_inc(xt_loaded, 16)

            def chunk(c, last=False):
                above(sp, y_stored, c * 16)
                sp.dma_start(xres[:], x_view[:, bass.ds(c * 2, 2), :]).then_inc(x_loaded, 16)
                if not last:
                    load_xt(c + 2)
                sp.wait_ge(y_ready, ONE + c + 1)
                sp.dma_start(y_view[:, bass.ds(c * 2, 2), :], xres[:]).then_inc(y_stored, 16)

            sp.dma_start(ident[:], ident_dram).then_inc(consts_loaded, 16)
            load_xt(0)
            load_xt(1)
            with sp.Fori(0, NCH - 2) as c:
                chunk(c)
            chunk(NCH - 2, True)
            chunk(NCH - 1, True)
            sp.wait_ge(y_stored, ONE + 16 * NCH)

        @block.tensor
        def _(pe):
            SS_STEPS = NSUB // 512 * DH

            def sub_scores_step(c, u, i):
                if i == 0:
                    if u == 0:
                        pe.wait_ge(xn_ready, ONE + c + 1)
                    above(pe, sim_copied, 2 * c + u)
                cb, dh = i // DH, i % DH
                last = nc.tensor.matmul(p_sim[:, cb * 512:(cb + 1) * 512], xn[:, dh, u * P:(u + 1) * P],
                                        wct[:, dh, cb * 512:(cb + 1) * 512], start=dh == 0, stop=dh == DH - 1)
                if i == SS_STEPS - 1:
                    last.then_inc(sim_ready, 1)

            def sub_scores(c, u):
                for i in range(SS_STEPS):
                    sub_scores_step(c, u, i)

            def turn_picks(c):
                pe.wait_ge(picks_ready, ONE + c + 1)
                above(pe, p_lo_ready, c)
                for k in range(3):
                    last = nc.tensor.transpose(p_picks[:, k, :], picks[:, k, :], ident[:])
                last.then_inc(picks_turned, 1)

            def route(c, s):
                pe.wait_ge(hot_ready, ONE + c * NS + s + 1)
                pe.wait_ge(x_lo_ready, ONE + c * NS + s + 1)
                for g in range(PS // PB):
                    gi = s * (PS // PB) + g
                    above(pe, routed, c * NG + max(gi - 1, 0))
                    for j in range(PB):
                        i = g * PB + j
                        nc.tensor.matmul(p_route[gi % 2][:, j, :], y_hot[:, s, :, i], x_hi[:, s, :, i],
                                         start=True, stop=False)
                        last = nc.tensor.matmul(p_route[gi % 2][:, j, :], y_hot[:, s, :, i], x_lo[:, s, :, i],
                                                start=False, stop=True)
                    last.then_inc(route_ready, 1)

            def expert_in(c, xp):
                if xp == 0:
                    pe.wait_ge(xt_lo_ready, ONE + c + 1)
                if xp % 2 == 0:
                    above(pe, gelu_ready, c * (NX // 2) + xp // 2 - 1)
                bank = p_hid[(xp // 2) % 2]
                for dh in range(DH):
                    for i, (a, b) in enumerate(PAIRS):
                        last = nc.tensor.matmul(bank[:, xp % 2, :], kin_t[:, a, dh, xp * P:(xp + 1) * P], xt[:, b, dh, :],
                                                start=dh == 0 and i == 0, stop=dh == DH - 1 and i == 2)
                if xp % 2 == 1:
                    last.then_inc(hid_ready, 1)

            def expert_out(c, xp):
                if xp == 0:
                    split_ready(pe, c, NG - 1)
                    above(pe, y_ready, c)
                for u in range(2):
                    for i, (a, b) in enumerate(PAIRS):
                        last = nc.tensor.matmul(p_out[:, u, :], parts[:, xp, u * P:(u + 1) * P, a], kout[:, b, xp, :],
                                                start=(xp == 0 and u == 0 and i == 0), stop=xp == NX - 1 and i == 2,
                                                skip_group_check=True)
                if xp % 2 == 1:
                    last.then_inc(out_read, 1)

            def chunk(c, last=False):
                for s in range(NS):
                    route(c, s)
                    if s < SS_STEPS:
                        sub_scores_step(c + 1, 1, s)
                    elif s - SS_STEPS < 2:
                        expert_in(c + 1, s - SS_STEPS)
                for xp in range(2, 4):
                    expert_in(c + 1, xp)
                for xp in range(0, NX, 2):
                    if xp >= 4:
                        expert_in(c + 1, xp)
                        expert_in(c + 1, xp + 1)
                    expert_out(c, xp)
                    expert_out(c, xp + 1)
                    if xp == 18:
                        turn_picks(c + 1)
                    if xp == 22 and not last:
                        sub_scores(c + 2, 0)

            pe.wait_ge(consts_loaded, ONE + 16)
            pe.wait_ge(weights_loaded, ONE + 16 * (LNB + 1))
            sub_scores(0, 0)
            sub_scores(0, 1)
            for xp in range(NX):
                expert_in(0, xp)
                if xp == 18:
                    turn_picks(0)
            sub_scores(1, 0)
            pe.wait_ge(kout_ready, ONE + SHARES)
            with pe.Fori(0, NCH - 2) as c:
                chunk(c)
            chunk(NCH - 2, True)
            for s in range(NS):
                route(NCH - 1, s)
            for xp in range(NX):
                expert_out(NCH - 1, xp)

        @block.scalar
        def _(act):
            def normalise(c):
                act.wait_ge(xt_loaded, ONE + c * 16 + 16)
                above(act, sim_ready, 2 * c)
                for dh in range(DH):
                    last = nc.scalar.activation(xn[:, dh, :], xt_in[:, dh, :], ACT.Identity,
                                                bias=shift[:, dh:dh + 1], scale=scale[:, dh:dh + 1])
                last.then_inc(xn_ready, 1)

            def copy_xt(c):
                above(act, hid_ready, c * (NX // 2))
                nc.scalar.copy(xt[:, 0, :, :], xt_in[:]).then_inc(xt_copied, 1)

            def copy_scores(c, u):
                act.wait_ge(sim_ready, ONE + 2 * c + u + 1)
                above(act, picks_ready, c)
                nc.scalar.copy(sim[:, u, :], p_sim[:]).then_inc(sim_copied, 1)

            def exponent(c):
                act.wait_ge(best_ready, ONE + c + 1)
                nc.scalar.activation(expo[:], expo[:], ACT.Exp).then_inc(exp_ready, 1)

            def copy_picks(c):
                act.wait_ge(picks_turned, ONE + c + 1)
                above(act, hot_ready, c * NS)
                nc.scalar.activation(xq[:], p_picks[:, 0, :], ACT.Identity, bias=tile_base[:])
                nc.scalar.copy(yq[:], p_picks[:, 1, :])
                nc.scalar.mul(p_hi[:], p_picks[:, 2, :], E_SCALE).then_inc(picks_copied, 1)

            def gelu(c, g):
                act.wait_ge(hid_ready, ONE + c * (NX // 2) + g + 1)
                above(act, out_read, (c - 1) * (NX // 2) + g + 1 if not isinstance(c, int) or c else 0)
                nc.scalar.activation(hidden[:, 2 * g:2 * g + 2, :], p_hid[g % 2][:], ACT.Gelu, scale=1.0 / E_SCALE).then_inc(gelu_ready, 1)

            def expert_phase(c, last=False):
                for g in range(NX // 2):
                    gelu(c, g)
                    if g == 5:
                        exponent(c)
                    if g == 8:
                        copy_picks(c)
                    if g == 10 and not last:
                        normalise(c + 1)
                    if g == 13 and not last:
                        copy_scores(c + 1, 0)

            def round_weighted(c):
                for g in range(NG):
                    act.wait_ge(routed, ONE + c * NG + g + 1)
                    hi, lo = group_parts(g)
                    nc.scalar.copy(hi, weighted[g % 4]).then_inc(hi_ready, 1)

            def chunk(c, last=False):
                copy_xt(c)
                round_weighted(c - 1)
                copy_scores(c, 1)
                expert_phase(c, last)

            act.wait_ge(base_ready, ONE + 1)
            normalise(0)
            copy_xt(0)
            act.wait_ge(kout_loaded, ONE + 16 * LNB)
            for b in range(SHARES):
                x = share(b)
                nc.scalar.mul(kout_rows[:, x, :], kout_rows[:, x, :], E_SCALE).then_inc(kout_scaled, 1)
                act.wait_ge(kout_scaled, ONE + b + 1)
                nc.scalar.copy(kout[:, 0, x, :], kout_rows[:, x, :]).then_inc(kout_hi, 1)
                if b == 1:
                    copy_scores(0, 0)
                if b == 3:
                    copy_scores(0, 1)
            expert_phase(0)
            with act.Fori(1, NCH - 1) as c:
                chunk(c)
            chunk(NCH - 1, True)
            round_weighted(NCH - 1)

        @block.vector
        def _(dve):
            PICK_STEPS = 14

            def pick(c):
                chain = Chain(dve, steps, c * PICK_STEPS)
                for u in range(2):
                    dve.wait_ge(sim_copied, ONE + c * 2 + u + 1)
                    nc.vector.memset(gate[:, u:u + 1], 0.0)
                    for side in range(2):
                        for h in range(NH):
                            k0 = (side * NH + h) * NK
                            last = nc.vector.max(top[:, side, u, h, :], sim[:, u, k0:k0 + NK])
                chain.link(last)
                if not isinstance(c, int) or c:
                    split_ready(dve, c - 1, NG - 1)
                for u in range(2):
                    a = top[:, 0, u, :, :].unsqueeze(3).to_broadcast([P, NH, TOPK, TOPK])
                    b = top[:, 1, u, :, :].unsqueeze(2).to_broadcast([P, NH, TOPK, TOPK])
                    last = nc.vector.tensor_tensor(cand[:, u, :, :, :], a, b, ALU.add)
                chain.mark(last)
                for side in range(2):
                    for u in range(2):
                        for h in range(NH):
                            k0 = (side * NH + h) * NK
                            nc.vector.max_index(top_key[:, side, u, h, :], top[:, side, u, h, :], sim[:, u, k0:k0 + NK])
                chain.wait()
                nc.vector.memset(gate[:, 2:3], 0.0)
                for u in range(2):
                    for h in range(NH):
                        last = nc.vector.max(best[:, u, h, :], cand[:, u, h, :, :].rearrange("p a b -> p (a b)"))
                chain.link(last)
                flat = best[:].rearrange("p u h k -> p (u h) k")
                nc.vector.tensor_tensor(expo[:], flat, flat[:, :, 0:1].to_broadcast([P, 2 * NH, TOPK]),
                                        ALU.subtract).then_inc(best_ready, 1)
                for u in range(2):
                    for h in range(NH):
                        o = (u * NH + h) * TOPK
                        last = nc.vector.max_index(best_at[:, o:o + TOPK], best[:, u, h, :],
                                                   cand[:, u, h, :, :].rearrange("p a b -> p (a b)"))
                chain.link(last)
                r = rank[:].rearrange("p s g k -> p s (g k)")
                nc.vector.tensor_single_scalar(r[:, 0, :], best_at[:], 3, ALU.logical_shift_right)
                chain.link(nc.vector.tensor_single_scalar(r[:, 1, :], best_at[:], TOPK - 1, ALU.bitwise_and))
                iota = rank_iota[:].unsqueeze(1).to_broadcast([P, 2 * NH, TOPK, TOPK])
                for side in range(2):
                    last = nc.vector.tensor_tensor(picked[:, side, :, :, :], iota, rank[:, side, :, :].unsqueeze(2).to_broadcast([P, 2 * NH, TOPK, TOPK]),
                                                   ALU.is_equal)
                chain.link(last)
                for side in range(2):
                    keys_of = top_key[:, side, :, :, :].rearrange("p u h k -> p (u h) k").unsqueeze(3).to_broadcast([P, 2 * NH, TOPK, TOPK])
                    last = nc.vector.tensor_tensor(picked[:, side, :, :, :], picked[:, side, :, :, :], keys_of, ALU.mult)
                chain.link(last)
                flat_picked = picked.rearrange("p s g a k -> p (s g) (a k)")
                for n in (TOPK // 2 * TOPK, TOPK // 4 * TOPK):
                    chain.link(nc.vector.tensor_tensor(flat_picked[:, :, 0:n], flat_picked[:, :, 0:n], flat_picked[:, :, n:2 * n], ALU.add))
                chain.link(nc.vector.tensor_tensor(key[:].rearrange("p s (g k) -> p (s g) k", k=TOPK), flat_picked[:, :, 0:TOPK],
                                                   flat_picked[:, :, TOPK:2 * TOPK], ALU.add))
                chain.link(nc.vector.tensor_copy(key_u[:], key[:, 0, :]))
                nc.vector.tensor_single_scalar(key_half[:], key_u[:], 1, ALU.logical_shift_right)
                chain.link(nc.vector.tensor_scalar(key_bit[:], key_u[:], 1, 6, ALU.bitwise_and, ALU.logical_shift_left))
                above(dve, picks_turned, c)
                nc.vector.tensor_copy(picks[:, 0, :], key_half[:])
                nc.vector.tensor_tensor(picks[:, 1, :], key_bit[:], key[:, 1, :], ALU.add)
                dve.wait_ge(exp_ready, ONE + c + 1)
                chain.link(nc.vector.tensor_reduce(total[:], expo[:], AX.X, ALU.add))
                chain.link(nc.vector.reciprocal(total[:], total[:]))
                nc.vector.tensor_tensor(picks[:, 2, :].rearrange("p (g k) -> p g k", k=TOPK), expo[:],
                                        total[:].unsqueeze(2).to_broadcast([P, 2 * NH, TOPK]), ALU.mult).then_inc(picks_ready, 1)
                dve.wait_ge(picks_copied, ONE + c + 1)
                nc.vector.scalar_tensor_tensor(p_lo[:], p_picks[:, 2, :], E_SCALE, p_hi[:], ALU.mult,
                                               ALU.subtract).then_inc(p_lo_ready, 1)
                return chain

            def one_hots(c, hots):
                if isinstance(c, int) and c == 0:
                    dve.wait_ge(kout_ready, ONE + SHARES)
                for s in range(NS):
                    lo, hi = s * PS, (s + 1) * PS
                    hot = x_hot[s % 2]
                    if s >= 2:
                        dve.wait_ge(hot_ready, ONE + c * NS + s - 1)
                        dve.wait_ge(x_lo_ready, ONE + c * NS + s - 1)
                    hots.mark(nc.vector.tensor_tensor(hot[:], y_iota[:, 0:2 * NX, :], xq[:, lo:hi].unsqueeze(1).to_broadcast([P, 2 * NX, PS]), ALU.is_equal))
                    nc.vector.tensor_tensor(y_hot[:, s, :, :], y_iota[:], yq[:, lo:hi].unsqueeze(1).to_broadcast([P, P, PS]), ALU.is_equal)
                    hots.wait()
                    nc.vector.tensor_tensor(x_hi[:, s, :, :], hot[:], p_hi[:, lo:hi].unsqueeze(1).to_broadcast([P, 2 * NX, PS]), ALU.mult).then_inc(hot_ready, 1)

            def split(c, g):
                dve.wait_ge(hi_ready, ONE + c * NG + g + 1)
                hi, lo = group_parts(g)
                nc.vector.tensor_tensor(lo, weighted[g % 4], hi, ALU.subtract).then_inc(lo_ready_v, 1)

            def weigh(c):
                dve.wait_ge(gelu_ready, ONE + c * (NX // 2) + NX // 2)
                for g in range(NG):
                    dve.wait_ge(route_ready, ONE + c * NG + g + 1)
                    if g == 2:
                        dve.wait_ge(hot_ready, ONE + c * NS + NS)
                        dve.wait_ge(x_lo_ready, ONE + c * NS + NS)
                    if g >= 4:
                        split_ready(dve, c, g - 4)
                    h = hidden[:].rearrange("p x (u t) -> p x u t", u=2)[:, :, :, g * PB:(g + 1) * PB]
                    nc.vector.tensor_tensor(weighted[g % 4], h, p_route[g % 2][:].rearrange("p t (u x) -> p x u t", u=2),
                                            ALU.mult).then_inc(routed, 1)
                    if g % VS == 0 and g:
                        split(c, g - 1)
                split(c, NG - 1)

            def add_residual(c):
                dve.wait_ge(out_read, ONE + (c + 1) * (NX // 2))
                dve.wait_ge(x_loaded, ONE + c * 16 + 16)
                nc.vector.scalar_tensor_tensor(xres[:].rearrange("p u d -> p (u d)"), p_out[:].rearrange("p u d -> p (u d)"),
                                               1.0 / E_SCALE ** 2, xres[:].rearrange("p u d -> p (u d)"), ALU.mult, ALU.add).then_inc(y_ready, 1)

            def prepare(c):
                chain = pick(c)
                hots = Chain(dve, hot_steps, c * NS)
                one_hots(c, hots)
                PICKED.append(chain.n)

            PICKED = []
            nc.vector.memset(tile_base[0:HK, :], 0.0)
            nc.vector.memset(tile_base[HK:P, :], float(NX)).then_inc(base_ready, 1)
            dve.wait_ge(iota_ready, ONE + 2)
            prepare(0)
            with dve.Fori(0, NCH - 1) as c:
                weigh(c)
                prepare(c + 1)
                add_residual(c)
            weigh(NCH - 1)
            add_residual(NCH - 1)
            assert set(PICKED) == {PICK_STEPS}, PICKED


ERR_CLIP, GRAD_CLIP = 5.0, 1.0
ERR_SCALE = 2.0 / 1024.0
NT = T // P


def memory_prepare(nc, sem, ident_dram, Wk, Wv, Wout, W0, W1, w):
    with ExitStack() as ctx:
        def sb(name, shape, dt=F32):
            return ctx.enter_context(nc.sbuf_tensor(name, shape, dt))

        ident = sb("mp_ident", [P, P])
        order = ("W0", "Wk", "Wv", "W1", "Wout")
        natural = {"W0": sb("mp_W0", [P, DH, D]), "Wk": w["Wk"], "Wv": sb("mp_Wv", [P, DH, D]), "W1": w["W1"],
                   "Wout": sb("mp_Wout", [P, DH, D])}
        dram = {"W0": W0, "Wk": Wk, "Wv": Wv, "W1": W1, "Wout": Wout}
        pt = [ctx.enter_context(nc.psum_tensor(f"mp_pt{i}", [P, DH, D], F32)) for i in range(len(order))]
        pw = ctx.enter_context(nc.psum_tensor("mp_pw", [P, DH, D], F32))
        loaded = sem("mp_loaded")
        turned, copied, product = sem("mp_turned"), sem("mp_copied"), sem("mp_product")
        block = ctx.enter_context(nc.Block())

        @block.sync
        def _(sp):
            sp.dma_start(ident[:], ident_dram).then_inc(loaded, 16)
            for name in order:
                sp.dma_start(natural[name][:], dram[name].rearrange("(h p) d -> p h d", p=P)).then_inc(loaded, 16)

        @block.tensor
        def _(pe):
            pe.wait_ge(loaded, ONE + 16 * (len(order) + 1))
            for i, name in enumerate(order):
                for a in range(DH):
                    for b in range(DH):
                        last = nc.tensor.transpose(pt[i][:, b, a * P:(a + 1) * P],
                                                   natural[name][:, a, b * P:(b + 1) * P], ident[:])
                last.then_inc(turned, 1)
            pe.wait_ge(copied, ONE + 1)
            for dh in range(DH):
                for mh in range(DH):
                    last = nc.tensor.matmul(pw[:, dh, :], w["Wk"][:, mh, dh * P:(dh + 1) * P], w["W0T"][:, mh, :],
                                            start=mh == 0, stop=mh == DH - 1)
            last.then_inc(product, 1)

        @block.vector
        def _(dve):
            for i, (name, sign) in enumerate((("W0T", 1.0), ("WkT", 1.0), ("minusWvT", -1.0), ("W1T", 1.0), ("WoutT", 1.0))):
                dve.wait_ge(turned, ONE + i + 1)
                nc.vector.tensor_scalar_mul(w[name][:], pt[i][:], sign).then_inc(copied, 1)
            dve.wait_ge(product, ONE + 1)
            nc.vector.tensor_copy(w["W0WkT"][:], pw[:])


def memory_gradients(nc, sem, xln_dram, xt_dram, ident_dram, w, grad1, grad0t):
    RING = 8
    with ExitStack() as ctx:
        def ring(name, shape, n=RING):
            return [ctx.enter_context(nc.sbuf_tensor(f"mg_{name}{i}", shape, F32)) for i in range(n)]

        def pb(name):
            return ctx.enter_context(nc.psum_tensor("mg_" + name, [P, DH * P * 2], F32))

        ident = ctx.enter_context(nc.sbuf_tensor("mg_ident", [P, P], F32))
        xt, xln = ring("xt", [P, DH, P]), ring("xln", [P, D])
        sig, a1, dsilu, err, d1 = ring("sig", [P, D]), ring("a1", [P, D]), ring("dsilu", [P, D]), ring("err", [P, D]), ring("d1", [P, D])
        tmp = ring("tmp", [P, D])
        a1t, errt = ring("a1t", [P, DH, P]), ring("errt", [P, DH, P])
        p_pre, p_a1t, p_err, p_errt, p_back = pb("pre"), pb("a1t"), pb("err"), pb("errt"), pb("back")
        p_grad1, p_grad0t = pb("grad1"), pb("grad0t")
        names = ("xt_loaded", "xln_loaded", "pre_ready", "sig_ready", "a1_ready", "dsilu_ready", "a1t_turned", "a1t_ready",
                 "err_summed", "err_ready", "errt_turned", "errt_ready", "back_ready", "d1_ready", "grads_added")
        s = {n: sem("mg_" + n) for n in names}
        for n in ("xt_loaded", "xln_loaded"):
            s[n] = [sem(f"mg_{n}{i}") for i in range(RING)]
        ident_loaded, steps = sem("mg_ident_loaded"), sem("mg_steps")
        block = ctx.enter_context(nc.Block())

        def above(eng, what, value):
            if not isinstance(value, int) or value > 0:
                eng.wait_ge(what, ONE + value)

        def valid(n):
            return not isinstance(n, int) or 0 <= n < NT

        def pipeline(eng, step):
            for n in range(RING):
                step(n, n)
            with eng.Fori(1, NT // RING) as i:
                for m in range(RING):
                    step(i * RING + m, m)
            for n in range(NT, NT + 3):
                step(n, n % RING)

        @block.sync
        def _(sp):
            sp.dma_start(ident[:], ident_dram).then_inc(ident_loaded, 16)

            def load(i, m):
                above(sp, s["grads_added"], (i - 1) * RING + m + 1)
                for h in range(DH):
                    sp.dma_start(xt[m][:, h, :], xt_dram[bass.ds(i * (RING // 2) + m // 2, 1), :, h, (m % 2) * P:(m % 2 + 1) * P]
                                 .rearrange("c p t -> (c p) t")).then_inc(s["xt_loaded"][m], 16)
                sp.dma_start(xln[m][:], xln_dram.rearrange("(n p) d -> n p d", p=P)[bass.ds(i * RING + m, 1), :, :]
                             .rearrange("n p d -> (n p) d")).then_inc(s["xln_loaded"][m], 16)

            for m in range(RING):
                load(0, m)
            with sp.Fori(1, NT // RING) as i:
                for m in range(RING):
                    load(i, m)

        @block.tensor
        def _(pe):
            pe.wait_ge(ident_loaded, ONE + 16)

            def step(n, m, it):
                m1, m2, m3 = (m - 1) % RING, (m - 2) % RING, (m - 3) % RING
                if valid(n - 1):
                    pe.wait_ge(s["a1_ready"], ONE + n)
                    above(pe, s["a1t_ready"], n - 1)
                    for h in range(DH):
                        last = nc.tensor.transpose(p_a1t[:, h * P:(h + 1) * P], a1[m1][:, h * P:(h + 1) * P], ident[:])
                    last.then_inc(s["a1t_turned"], 1)
                if valid(n - 2):
                    pe.wait_ge(s["err_ready"], ONE + n - 1)
                    above(pe, s["errt_ready"], n - 2)
                    for h in range(DH):
                        last = nc.tensor.transpose(p_errt[:, h * P:(h + 1) * P], err[m2][:, h * P:(h + 1) * P], ident[:])
                    last.then_inc(s["errt_turned"], 1)
                if valid(n):
                    pe.wait_ge(s["xt_loaded"][m], ONE + it * 32 + 32)
                    above(pe, s["a1_ready"], n)
                    for h in range(DH):
                        last = nc.tensor.matmul(p_pre[:, 0:D], xt[m][:, h, :], w["W0WkT"][:, h, :], start=h == 0, stop=h == DH - 1)
                    last.then_inc(s["pre_ready"], 1)
                if valid(n - 2):
                    pe.wait_ge(s["errt_ready"], ONE + n - 1)
                    above(pe, s["d1_ready"], n - 2)
                    for h in range(DH):
                        last = nc.tensor.matmul(p_back[:, 0:D], errt[m2][:, h, :], w["W1"][:, h, :], start=h == 0, stop=h == DH - 1)
                    last.then_inc(s["back_ready"], 1)
                if valid(n - 1):
                    pe.wait_ge(s["a1t_ready"], ONE + n)
                    above(pe, s["err_ready"], n - 1)
                    for h in range(DH):
                        nc.tensor.matmul(p_err[:, 0:D], a1t[m1][:, h, :], w["W1T"][:, h, :], start=h == 0, stop=False)
                    for h in range(DH):
                        last = nc.tensor.matmul(p_err[:, 0:D], xt[m1][:, h, :], w["minusWvT"][:, h, :], start=False, stop=h == DH - 1)
                    last.then_inc(s["err_summed"], 1)
                if valid(n - 3):
                    first, end = isinstance(n, int) and n == 3, isinstance(n, int) and n == NT + 2
                    pe.wait_ge(s["xln_loaded"][m3], ONE + ((it if m >= 3 else it - 1) * 16 + 16))
                    pe.wait_ge(s["d1_ready"], ONE + n - 2)
                    for h in range(DH):
                        nc.tensor.matmul(p_grad1[:, h * D:(h + 1) * D], err[m3][:, h * P:(h + 1) * P], a1[m3][:],
                                         start=first and h == 0, stop=end, skip_group_check=True)
                    for h in range(DH):
                        last = nc.tensor.matmul(p_grad0t[:, h * D:(h + 1) * D], xln[m3][:, h * P:(h + 1) * P], d1[m3][:],
                                                start=first and h == 0, stop=end, skip_group_check=True)
                    last.then_inc(s["grads_added"], 1)

            for n in range(RING):
                step(n, n, 0)
            with pe.Fori(1, NT // RING) as i:
                for m in range(RING):
                    step(i * RING + m, m, i)
            for n in range(NT, NT + 3):
                step(n, n % RING, NT // RING)

        @block.scalar
        def _(act):
            def step(n, m):
                m1, m2 = (m - 1) % RING, (m - 2) % RING
                if valid(n - 1):
                    act.wait_ge(s["a1t_turned"], ONE + n)
                    nc.scalar.copy(a1t[m1][:].rearrange("p h t -> p (h t)"), p_a1t[:, 0:D]).then_inc(s["a1t_ready"], 1)
                if valid(n - 2):
                    act.wait_ge(s["errt_turned"], ONE + n - 1)
                    nc.scalar.copy(errt[m2][:].rearrange("p h t -> p (h t)"), p_errt[:, 0:D]).then_inc(s["errt_ready"], 1)
                if valid(n):
                    act.wait_ge(s["pre_ready"], ONE + n + 1)
                    nc.scalar.activation(sig[m][:], p_pre[:, 0:D], ACT.Sigmoid).then_inc(s["sig_ready"], 1)

            pipeline(act, step)

        @block.vector
        def _(dve):
            def step(n, m):
                m1, m2 = (m - 1) % RING, (m - 2) % RING
                if valid(n):
                    dve.wait_ge(s["sig_ready"], ONE + n + 1)
                    above(dve, s["grads_added"], n - RING + 1)
                    nc.vector.tensor_tensor(a1[m][:], p_pre[:, 0:D], sig[m][:], ALU.mult).then_inc(s["a1_ready"], 1)
                if valid(n - 2):
                    dve.wait_ge(s["back_ready"], ONE + n - 1)
                    nc.vector.tensor_tensor(d1[m2][:], p_back[:, 0:D], dsilu[m2][:], ALU.mult).then_inc(s["d1_ready"], 1)
                if valid(n):
                    dve.wait_ge(s["a1_ready"], ONE + n + 1)
                    nc.vector.scalar_tensor_tensor(tmp[m][:], sig[m][:], 1.0, a1[m][:], ALU.subtract, ALU.mult).then_inc(steps, 1)
                    dve.wait_ge(steps, ONE + n + 1)
                    nc.vector.tensor_tensor(dsilu[m][:], sig[m][:], tmp[m][:], ALU.subtract).then_inc(s["dsilu_ready"], 1)
                if valid(n - 1):
                    dve.wait_ge(s["err_summed"], ONE + n)
                    nc.vector.tensor_scalar(err[m1][:], p_err[:, 0:D], -ERR_CLIP, ERR_CLIP, ALU.max, ALU.min).then_inc(s["err_ready"], 1)

            pipeline(dve, step)
            dve.wait_ge(s["grads_added"], ONE + NT)
            nc.vector.tensor_copy(grad1[:].rearrange("p h e -> p (h e)"), p_grad1[:])
            nc.vector.tensor_copy(grad0t[:].rearrange("p h e -> p (h e)"), p_grad0t[:])


def memory_update(nc, sem, ident_dram, feature_stats, gate_w, gate_b, W0_t, Wq, w, grad1, grad0t, first_w, second_w):
    with ExitStack() as ctx:
        def sb(name, shape, dt=F32):
            return ctx.enter_context(nc.sbuf_tensor("mu_" + name, shape, dt))

        NGATE = 3
        ones, wg, weighted, bias = sb("ones", [P, P]), sb("wg", [P, NGATE, DH]), sb("weighted", [P, NGATE, DH]), sb("bias", [P, NGATE])
        wq, mean = sb("wq", [P, DH, D]), sb("mean", [P, DH, 2])
        gates, minus_lr, keep = sb("gates", [P, NGATE]), sb("minus_lr", [P, 1]), sb("keep", [P, 1])
        zero, mom = sb("zero", [P, DH, D]), sb("mom", [P, DH, D])
        g0, g1, w0n, w1n = sb("g0", [P, DH, D]), sb("g1", [P, DH, D]), sb("w0n", [P, DH, D]), sb("w1n", [P, DH, D])
        p_gate = ctx.enter_context(nc.psum_tensor("mu_p_gate", [P, 512], F32))
        p_g0, p_first, p_second = (ctx.enter_context(nc.psum_tensor("mu_" + n, [P, DH, D], F32)) for n in ("p_g0", "p_first", "p_second"))
        loaded, bias_zero, bias_loaded, gate_in, gate_sum, gate_ready = (sem("mu_" + n) for n in (
            "loaded", "bias_zero", "bias_loaded", "gate_in", "gate_sum", "gate_ready"))
        g0_ready, w0n_ready, w1n_ready, first_ready, second_ready, steps = (sem("mu_" + n) for n in (
            "g0_ready", "w0n_ready", "w1n_ready", "first_ready", "second_ready", "steps"))
        block = ctx.enter_context(nc.Block())

        @block.sync
        def _(sp):
            sp.dma_start(wq[:], Wq.rearrange("(h p) d -> p h d", p=P)).then_inc(loaded, 16)
            with nc.allow_non_contiguous_dma(reason="768 scalars"):
                for g in range(NGATE):
                    sp.dma_start(wg[:, g, :], gate_w[g].rearrange("o (h p) -> p (o h)", p=P)).then_inc(loaded, 16)
            sp.wait_ge(bias_zero, ONE + 1)
            for g in range(NGATE):
                sp.dma_start(bias[0:1, g:g + 1], gate_b[g].rearrange("(o n) -> o n", o=1)).then_inc(bias_loaded, 16)

        @block.tensor
        def _(pe):
            pe.wait_ge(bias_loaded, ONE + 16 * NGATE)
            nc.tensor.matmul(p_gate[:, 0:NGATE], ones[:], bias[:], start=True, stop=False)
            pe.wait_ge(gate_in, ONE + 1)
            for h in range(DH):
                last = nc.tensor.matmul(p_gate[:, 0:NGATE], ones[:], weighted[:, :, h], start=False, stop=h == DH - 1)
            last.then_inc(gate_sum, 1)
            for mh in range(DH):
                for h in range(DH):
                    last = nc.tensor.matmul(p_g0[:, mh, :], w["WkT"][:, h, mh * P:(mh + 1) * P], grad0t[:, h, :],
                                            start=h == 0, stop=h == DH - 1)
            last.then_inc(g0_ready, 1)
            pe.wait_ge(w1n_ready, ONE + 1)
            for eh in range(DH):
                for h in range(DH):
                    last = nc.tensor.matmul(p_second[:, eh, :], w1n[:, h, eh * P:(eh + 1) * P], w["WoutT"][:, h, :],
                                            start=h == 0, stop=h == DH - 1)
            last.then_inc(second_ready, 1)
            pe.wait_ge(w0n_ready, ONE + 1)
            for dh in range(DH):
                for mh in range(DH):
                    last = nc.tensor.matmul(p_first[:, dh, :], wq[:, mh, dh * P:(dh + 1) * P], w0n[:, mh, :],
                                            start=mh == 0, stop=mh == DH - 1)
            last.then_inc(first_ready, 1)

        @block.scalar
        def _(act):
            act.wait_ge(gate_sum, ONE + 1)
            nc.scalar.activation(gates[:], p_gate[:, 0:NGATE], ACT.Sigmoid).then_inc(gate_ready, 1)

        @block.vector
        def _(dve):
            chain = Chain(dve, steps)
            nc.vector.memset(ones[:], 1.0)
            nc.vector.memset(bias[:], 0.0).then_inc(bias_zero, 1)
            chain.mark(nc.vector.memset(zero[:], 0.0))
            for h in range(DH):
                chain.mark(nc.vector.bn_aggr(mean[:, h, :], feature_stats[:, h, :, :].rearrange("p b s -> p (b s)")))
            dve.wait_ge(loaded, ONE + 16 * (NGATE + 1))
            chain.wait()
            nc.vector.tensor_tensor(weighted[:], wg[:], mean[:, :, 0].unsqueeze(1).to_broadcast([P, NGATE, DH]),
                                    ALU.mult).then_inc(gate_in, 1)
            dve.wait_ge(gate_ready, ONE + 1)
            chain.mark(nc.vector.tensor_scalar(keep[:], gates[:, 0:1], -1.0, 1.0, ALU.mult, ALU.add))
            chain.mark(nc.vector.tensor_scalar_mul(minus_lr[:], gates[:, 1:2], -1.0))
            chain.mark(nc.vector.tensor_scalar(mom[:], zero[:], gates[:, 2:3], None, ALU.mult))

            def step_layer(grad, g, scale, old, new, done):
                if scale != 1.0:
                    chain.link(nc.vector.tensor_scalar_mul(g, grad, scale))
                    grad = g
                chain.link(nc.vector.tensor_scalar(g, grad, -GRAD_CLIP, GRAD_CLIP, ALU.max, ALU.min))
                chain.link(nc.vector.scalar_tensor_tensor(g, g, minus_lr[:], mom[:].rearrange("p h e -> p (h e)"), ALU.mult, ALU.add))
                nc.vector.scalar_tensor_tensor(new, old, keep[:], g, ALU.mult, ALU.add).then_inc(done, 1)

            def flat(x):
                return x[:].rearrange("p h e -> p (h e)")

            step_layer(flat(grad1), flat(g1), ERR_SCALE, flat(w["W1"]), flat(w1n), w1n_ready)
            dve.wait_ge(g0_ready, ONE + 1)
            step_layer(flat(p_g0), flat(g0), ERR_SCALE, flat(W0_t), flat(w0n), w0n_ready)
            dve.wait_ge(second_ready, ONE + 1)
            nc.vector.tensor_copy(second_w[:], p_second[:])
            dve.wait_ge(first_ready, ONE + 1)
            nc.vector.tensor_copy(first_w[:], p_first[:])


def memory_read(nc, sem, x_dram, y_dram, xt_dram, first_w, second_w):
    with ExitStack() as ctx:
        def pair(name, shape):
            return [ctx.enter_context(nc.sbuf_tensor(f"mr_{name}{u}", shape, F32)) for u in range(2)]

        xt, sig, hid = pair("xt", [P, DH, CH]), pair("sig", [P, DH, CH]), pair("hid", [P, DH, CH])
        x, y = pair("x", [P, 2, D]), pair("y", [P, 2, D])
        p_pre = [ctx.enter_context(nc.psum_tensor(f"mr_p_pre{u}", [P, DH, CH], F32)) for u in range(2)]
        p_out = [ctx.enter_context(nc.psum_tensor(f"mr_p_out{u}", [P, 2, D], F32)) for u in range(2)]
        xt_loaded, x_loaded, pre_ready, sig_ready, hid_ready, out_ready, y_ready, y_stored = (
            [sem(f"mr_{n}{u}") for u in range(2)] for n in (
                "xt_loaded", "x_loaded", "pre_ready", "sig_ready", "hid_ready", "out_ready", "y_ready", "y_stored"))
        n_it = NCH // 2
        rows = x_dram.rearrange("(n p) d -> p n d", p=P)
        out_rows = y_dram.rearrange("(n p) d -> p n d", p=P)
        block = ctx.enter_context(nc.Block())

        @block.sync
        def _(sp):
            def load_xt(u, i):
                sp.dma_start(xt[u][:], xt_dram[bass.ds(i * 2 + u, 1), :, :, :].rearrange("c p h t -> (c p) h t")).then_inc(xt_loaded[u], 16)

            def load_x(u, i):
                sp.dma_start(x[u][:], rows[:, bass.ds((i * 2 + u) * 2, 2), :]).then_inc(x_loaded[u], 16)

            def next_xt(u, i):
                sp.wait_ge(pre_ready[u], ONE + i + 1)
                load_xt(u, i + 1)

            def finish(u, i, last=False):
                sp.wait_ge(y_ready[u], ONE + i + 1)
                if not last:
                    load_x(u, i + 1)
                sp.dma_start(out_rows[:, bass.ds((i * 2 + u) * 2, 2), :], y[u][:]).then_inc(y_stored[u], 16)

            for u in range(2):
                load_xt(u, 0)
                load_x(u, 0)
            next_xt(0, 0)
            with sp.Fori(0, n_it - 2) as i:
                next_xt(1, i)
                finish(0, i)
                next_xt(0, i + 1)
                finish(1, i)
            next_xt(1, n_it - 2)
            for u in range(2):
                finish(u, n_it - 2)
            for u in range(2):
                finish(u, n_it - 1, last=True)
            for u in range(2):
                sp.wait_ge(y_stored[u], ONE + 16 * n_it)

        @block.tensor
        def _(pe):
            def pre(u, i):
                pe.wait_ge(xt_loaded[u], ONE + i * 16 + 16)
                pe.wait_ge(hid_ready[u], ONE + i)
                for eh in range(DH):
                    for h in range(DH):
                        last = nc.tensor.matmul(p_pre[u][:, eh, :], first_w[:, h, eh * P:(eh + 1) * P], xt[u][:, h, :],
                                                start=h == 0, stop=h == DH - 1)
                last.then_inc(pre_ready[u], 1)

            def out(u, i):
                pe.wait_ge(hid_ready[u], ONE + i + 1)
                pe.wait_ge(y_ready[u], ONE + i)
                for t in range(2):
                    for eh in range(DH):
                        last = nc.tensor.matmul(p_out[u][:, t, :], hid[u][:, eh, t * P:(t + 1) * P], second_w[:, eh, :],
                                                start=eh == 0, stop=eh == DH - 1)
                last.then_inc(out_ready[u], 1)

            pre(0, 0)
            with pe.Fori(0, n_it - 1) as i:
                pre(1, i)
                out(0, i)
                pre(0, i + 1)
                out(1, i)
            pre(1, n_it - 1)
            out(0, n_it - 1)
            out(1, n_it - 1)

        @block.scalar
        def _(act):
            with act.Fori(0, n_it) as i:
                for u in range(2):
                    act.wait_ge(pre_ready[u], ONE + i + 1)
                    nc.scalar.activation(sig[u][:], p_pre[u][:], ACT.Sigmoid).then_inc(sig_ready[u], 1)

        @block.vector
        def _(dve):
            def hidden(u, i):
                dve.wait_ge(sig_ready[u], ONE + i + 1)
                dve.wait_ge(out_ready[u], ONE + i)
                nc.vector.tensor_tensor(hid[u][:], p_pre[u][:], sig[u][:], ALU.mult).then_inc(hid_ready[u], 1)

            def residual(u, i):
                dve.wait_ge(out_ready[u], ONE + i + 1)
                dve.wait_ge(x_loaded[u], ONE + i * 16 + 16)
                dve.wait_ge(y_stored[u], ONE + i * 16)
                nc.vector.tensor_tensor(y[u][:], p_out[u][:], x[u][:], ALU.add).then_inc(y_ready[u], 1)

            hidden(0, 0)
            with dve.Fori(0, n_it - 1) as i:
                hidden(1, i)
                residual(0, i)
                hidden(0, i + 1)
                residual(1, i)
            hidden(1, n_it - 1)
            residual(0, n_it - 1)
            residual(1, n_it - 1)


def neural_memory(nc, sem, x_dram, y_dram, xln_dram, xt_dram, ident_dram, Wk, Wv, Wq, Wout, W0, W1, gate_w, gate_b):
    with ExitStack() as ctx:
        def sb(name, shape=(P, DH, D)):
            return ctx.enter_context(nc.sbuf_tensor("nm_" + name, list(shape), F32))

        w = {n: sb(n) for n in ("Wk", "W1", "W0T", "WkT", "minusWvT", "W1T", "WoutT", "W0WkT")}
        grad1, grad0t, first_w, second_w = sb("grad1"), sb("grad0t"), sb("first_w"), sb("second_w")
        feature_stats = sb("feature_stats", (P, DH, NBLK, 6))
        memory_prepare(nc, sem, ident_dram, Wk, Wv, Wout, W0, W1, w)
        layer_norm_pass(nc, sem, "nm_ln_", x_dram, xt_dram, ident_dram, feature_stats, xln_dram=xln_dram)
        memory_gradients(nc, sem, xln_dram, xt_dram, ident_dram, w, grad1, grad0t)
        memory_update(nc, sem, ident_dram, feature_stats, gate_w, gate_b, w["W0T"], Wq, w, grad1, grad0t, first_w, second_w)
        memory_read(nc, sem, x_dram, y_dram, xt_dram, first_w, second_w)


AH, DK, DC = 16, 16, 64
HG = 4
NU = BATCH * AH // HG
GD = HG * DK
QT, QB, STEP = SEQ // P, SEQ // BLK, BLK // P
PAIRS = ((0, 0), (0, 1), (1, 0), (0, 2), (2, 0), (1, 1))
KS_ROWS = len(PAIRS) * DK
M_ROWS = 3
NEG = -1e30


def attention_project(nc, sem, xt_dram, qk_dram, v_dram, W_dq, W_dkv, W_uq, W_uk, W_uv):
    with ExitStack() as ctx:
        def sb(name, shape, dt=F32):
            return ctx.enter_context(nc.sbuf_tensor("ap_" + name, shape, dt))

        def pair(name, shape, dt=F32):
            return [sb(f"{name}{u}", shape, dt) for u in range(2)]

        down, up = sb("down", [P, DH, 2 * DC]), {n: sb("up_" + n, [P, D]) for n in "qkv"}
        xt, ct = pair("xt", [P, DH, CH]), pair("ct", [P, CH])
        parts = {n: pair("parts_" + n, [P, 3, DH, CH], BF16) for n in "qk"}
        rest = {n: pair("rest_" + n, [P, DH, CH]) for n in "qk"}
        v = pair("v", [P, AH // HG, 2, HG, 32])
        p_c = ctx.enter_context(nc.psum_tensor("ap_p_c", [P, 512], F32))
        p_up = {n: [ctx.enter_context(nc.psum_tensor(f"ap_p_{n}{u}", [P, DH, CH], F32)) for u in range(2)] for n in "qkv"}
        up_zero, weights = sem("ap_up_zero"), sem("ap_weights")
        s = {n: [sem(f"ap_{n}{u}") for u in range(2)] for n in (
            "xt_loaded", "c_ready", "c_copied", "q_ready", "k_ready", "v_ready", "first_q", "first_k", "rest_q",
            "rest_k", "second_q", "second_k", "third_q", "third_k", "v_copied", "stored", "v_zero")}
        n_it = SEQ // CH // 2
        scale = {"q": 0.25, "k": 1.0}
        block = ctx.enter_context(nc.Block())

        @block.sync
        def _(sp):
            for i, w in enumerate((W_dq, W_dkv)):
                sp.dma_start(down[:, :, i * DC:(i + 1) * DC], w.rearrange("(h p) c -> p h c", p=P)).then_inc(weights, 16)
            sp.wait_ge(up_zero, ONE + 3)
            sp.dma_start(up["q"][0:DC, :], W_uq).then_inc(weights, 16)
            sp.dma_start(up["k"][DC:P, :], W_uk).then_inc(weights, 16)
            sp.dma_start(up["v"][DC:P, :], W_uv).then_inc(weights, 16)
            def load(u, c):
                sp.dma_start(xt[u][:], xt_dram[bass.ds(c, 1), :, :, :].rearrange("c p h t -> (c p) h t")).then_inc(s["xt_loaded"][u], 16)

            def chunk(b, j, u, last=False):
                n = b * n_it + j
                if not last:
                    sp.wait_ge(s["c_ready"][u], ONE + n + 1)
                    load(u, n * 2 + u + 2)
                sp.wait_ge(s["v_copied"][u], ONE + n + 1)
                dst = v_dram[bass.ds(b * (NU // BATCH), NU // BATCH), :, bass.ds((j * 2 + u) * 2 * P, 2 * P)].rearrange("g p c -> p g c")
                sp.dma_start(dst, v[u][:].rearrange("p g t h c -> p g (t h c)")).then_inc(s["stored"][u], 16)
                for k, name in enumerate("qk"):
                    sp.wait_ge(s["third_" + name][u], ONE + n + 1)
                    for h in range(DH):
                        dst = qk_dram[k, :, bass.ds(b * D + h * P, P), bass.ds((j * 2 + u) * CH, CH)].rearrange("a r t -> r a t")
                        sp.dma_start(dst, parts[name][u][:, :, h, :]).then_inc(s["stored"][u], 16)

            for u in range(2):
                load(u, u)
            for b in range(BATCH):
                peeled = b == BATCH - 1
                with sp.Fori(0, n_it - peeled) as j:
                    for u in range(2):
                        chunk(b, j, u)
            for u in range(2):
                chunk(BATCH - 1, n_it - 1, u, last=True)
            for u in range(2):
                sp.wait_ge(s["stored"][u], ONE + 80 * BATCH * n_it)

        @block.gpsimd
        def _(pool):
            for n in "qkv":
                nc.gpsimd.memset(up[n][:], 0.0).then_inc(up_zero, 1)

        @block.tensor
        def _(pe):
            pe.wait_ge(weights, ONE + 80)
            with pe.Fori(0, BATCH * n_it) as i:
                for u in range(2):
                    pe.wait_ge(s["xt_loaded"][u], ONE + i * 16 + 16)
                    if u:
                        pe.wait_ge(s["c_copied"][0], ONE + i + 1)
                    else:
                        pe.wait_ge(s["c_copied"][1], ONE + i)
                    for h in range(DH):
                        last = nc.tensor.matmul(p_c[:, 0:CH], down[:, h, :], xt[u][:, h, :], start=h == 0, stop=h == DH - 1)
                    last.then_inc(s["c_ready"][u], 1)
                    pe.wait_ge(s["c_copied"][u], ONE + i + 1)
                    for name in "qk":
                        pe.wait_ge(s["rest_" + name][u], ONE + i)
                        for h in range(DH):
                            last = nc.tensor.matmul(p_up[name][u][:, h, :], up[name][:, h * P:(h + 1) * P], ct[u][:], start=True, stop=True)
                        last.then_inc(s[name + "_ready"][u], 1)
                    pe.wait_ge(s["v_copied"][u], ONE + i)
                    for t in range(2):
                        last = nc.tensor.matmul(p_up["v"][u][:, t, :], ct[u][:, t * P:(t + 1) * P], up["v"][:], start=True, stop=True)
                    last.then_inc(s["v_ready"][u], 1)

        @block.scalar
        def _(act):
            for u in range(2):
                act.wait_ge(s["v_zero"][u], ONE + 2)
            with act.Fori(0, BATCH * n_it) as i:
                for u in range(2):
                    act.wait_ge(s["c_ready"][u], ONE + i + 1)
                    act.wait_ge(s["v_ready"][u], ONE + i)
                    nc.scalar.copy(ct[u][:], p_c[:, 0:CH]).then_inc(s["c_copied"][u], 1)
                    act.wait_ge(s["stored"][u], ONE + i * 80)
                    for name in "qk":
                        act.wait_ge(s[name + "_ready"][u], ONE + i + 1)
                        nc.scalar.mul(parts[name][u][:, 0, :, :], p_up[name][u][:], scale[name]).then_inc(s["first_" + name][u], 1)
                    act.wait_ge(s["v_ready"][u], ONE + i + 1)
                    for t in range(2):
                        last = nc.scalar.copy(v[u][:, :, t, :, 0:DK], p_up["v"][u][:, t, :].rearrange("p (g h c) -> p g h c", h=HG, c=DK))
                    last.then_inc(s["v_copied"][u], 1)
                    for name in "qk":
                        act.wait_ge(s["rest_" + name][u], ONE + i + 1)
                        nc.scalar.copy(parts[name][u][:, 1, :, :], rest[name][u][:]).then_inc(s["second_" + name][u], 1)

        @block.vector
        def _(dve):
            for u in range(2):
                nc.vector.memset(v[u][:], 0.0).then_inc(s["v_zero"][u], 1)
                dve.wait_ge(s["v_zero"][u], ONE + 1)
                nc.vector.memset(v[u][:, :, :, :, DK:DK + 1].rearrange("p g t h c -> p (g t h) c"), 1.0).then_inc(s["v_zero"][u], 1)
            with dve.Fori(0, BATCH * n_it) as i:
                for u in range(2):
                    for name in "qk":
                        dve.wait_ge(s["first_" + name][u], ONE + i + 1)
                        dve.wait_ge(s["third_" + name][u], ONE + i)
                        nc.vector.scalar_tensor_tensor(rest[name][u][:], p_up[name][u][:], scale[name], parts[name][u][:, 0, :, :],
                                                       ALU.mult, ALU.subtract).then_inc(s["rest_" + name][u], 1)
                    for name in "qk":
                        dve.wait_ge(s["second_" + name][u], ONE + i + 1)
                        nc.vector.tensor_tensor(parts[name][u][:, 2, :, :], rest[name][u][:], parts[name][u][:, 1, :, :],
                                                ALU.subtract).then_inc(s["third_" + name][u], 1)


def attention_plan():
    steps = [(qb, kt) for qb in range(QB) for kt in range(STEP * qb + STEP)]
    weight = [2 * 2 * (BLK - P * max(0, kt - STEP * qb)) + 400 for qb, kt in steps]
    pieces = [("max", h, qt, kb) for h in range(HG) for qt in range(QT) for kb in range(qt // STEP + 1)]
    cost = [min(BLK, (qt + 1) * P - kb * BLK) + 120 for _, h, qt, kb in pieces]
    until = len(steps) - 3
    share, done, k, turns = sum(cost) / sum(weight[:until]), 0.0, 0, []
    passed = 0.0
    for i in range(len(steps)):
        passed += weight[i] * share
        here = []
        while k < len(pieces) and (done + cost[k] / 2 < passed or i == until - 1):
            here.append(pieces[k])
            done += cost[k]
            k += 1
        if i == until:
            here.append(("m",))
        turns.append(here)
    ends = [i for i, (qb, kt) in enumerate(steps) if kt == STEP * qb + STEP - 1]
    for qb, e in enumerate(ends[:-1]):
        turns[e + 2].append(("o", qb))
    return steps, turns, ends, pieces


def attention_units(nc, sem, qk_dram, v_dram, ao_dram, ident_dram):
    steps, turns, ends, pieces = attention_plan()
    NST, RING, SLOTS = len(steps), 3, 3
    TURNS = sum(map(len, turns)) + 1
    FIRST = len(pieces) + 1
    assert TURNS % RING == 0
    with ExitStack() as ctx:
        def sb(name, shape, dt=F32):
            return ctx.enter_context(nc.sbuf_tensor("at_" + name, shape, dt))

        def pb(name, shape):
            return ctx.enter_context(nc.psum_tensor("at_" + name, shape, F32))

        ident, identb = sb("ident", [P, P]), sb("identb", [P, P], BF16)
        mask_rows, mask_cols = sb("mask_rows", [P, P], BF16), sb("mask_cols", [P, P], BF16)
        q = [sb(f"q{i}", [P, HG, SEQ], BF16) for i in range(SLOTS)]
        k = [sb(f"k{i}", [P, HG, SEQ], BF16) for i in range(SLOTS)]
        v = [sb(f"v{i}", [P, QT, HG, 32]) for i in range(SLOTS)]
        prob = [sb(f"prob{i}", [P, HG, BLK]) for i in range(2)]
        part_max, row_max = sb("part_max", [P, HG * QT, QB]), sb("row_max", [P, P])
        m_rows, m_rest = sb("m_rows", [HG * QT, M_ROWS, P], BF16), sb("m_rest", [HG * QT, P])
        out_t, ao, recip = sb("out_t", [P, BLK]), sb("ao", [P, STEP, GD]), sb("recip", [P, STEP, HG])
        p_s = [pb(f"p_s{i}", [P, 2, BLK]) for i in range(2)]
        p_o = pb("p_o", [P, BLK])
        p_ring = [pb(f"p_ring{i}", [P, BLK]) for i in range(RING)]
        names = ("ident_loaded", "made", "mask_zero", "turn_ready", "turn_taken", "row_max_ready", "m_first", "m_steps", "m_ready",
                 "m_loaded", "s_ready", "prob_ready", "pv_done", "out_done", "out_copied", "ao_steps", "ao_ready", "ao_stored",
                 "floor_set", "ones_set")
        s = {n: sem("at_" + n) for n in names}
        loaded = [sem(f"at_loaded{i}") for i in range(SLOTS)]
        N_LOADS = 2 * len(PAIRS) + 1
        block = ctx.enter_context(nc.Block())

        def above(eng, what, value):
            if not isinstance(value, int) or value > 0:
                eng.wait_ge(what, ONE + value)

        def units(eng, unit):
            with eng.Fori(0, NU // SLOTS) as i:
                for slot in range(SLOTS):
                    unit(i * SLOTS + slot, slot, i)
            for n in range(NU // SLOTS * SLOTS, NU):
                unit(n, n % SLOTS, n // SLOTS)

        @block.gpsimd
        def _(pool):
            nc.gpsimd.memset(mask_rows[:], 0.0).then_inc(s["mask_zero"], 1)
            nc.gpsimd.memset(mask_cols[:], 0.0).then_inc(s["mask_zero"], 1)
            pool.wait_ge(s["mask_zero"], ONE + 2)
            nc.gpsimd.affine_select(out=mask_rows[:], in_=mask_rows[:], compare_op=ALU.is_ge, fill=NEG, base=0,
                                    pattern=[[-1, P]], channel_multiplier=1).then_inc(s["made"], 1)
            nc.gpsimd.affine_select(out=mask_cols[:], in_=mask_cols[:], compare_op=ALU.is_ge, fill=NEG, base=0,
                                    pattern=[[1, P]], channel_multiplier=-1).then_inc(s["made"], 1)
            for i in range(SLOTS):
                if i:
                    pool.wait_ge(s["ones_set"], ONE + i)
                else:
                    pool.wait_ge(s["made"], ONE + 3)
                nc.gpsimd.memset(k[i][KS_ROWS:KS_ROWS + M_ROWS, :, :], 1.0).then_inc(s["ones_set"], 1)

        @block.sync
        def _(sp):
            sp.dma_start(ident[:], ident_dram).then_inc(s["ident_loaded"], 16)

            def load(n, slot):
                for r, (pq, pk) in enumerate(PAIRS):
                    for which, tile, part in ((0, q, pq), (1, k, pk)):
                        src = qk_dram[which, part, bass.ds(n * GD, GD), :].rearrange("(h d) t -> d h t", d=DK)
                        sp.dma_start(tile[slot][r * DK:(r + 1) * DK, :, :], src).then_inc(loaded[slot], 16)
                sp.dma_start(v[slot][:].rearrange("p t h c -> p (t h c)"), v_dram[bass.ds(n, 1), :, :].rearrange("n p c -> (n p) c")).then_inc(loaded[slot], 16)

            def rows(n, slot):
                sp.wait_ge(s["m_ready"], ONE + n + 1)
                for a in range(M_ROWS):
                    dst = q[slot][KS_ROWS + a:KS_ROWS + a + 1, :, :].rearrange("o h t -> o (h t)").rearrange("o (x p) -> o x p", p=P)
                    sp.dma_start(dst, m_rows[:, a, :]).then_inc(s["m_loaded"], 16)

            def store(n, qb):
                sp.wait_ge(s["ao_ready"], ONE + n * QB + qb + 1)
                sp.dma_start(ao_dram[bass.ds(n, 1), qb * BLK:(qb + 1) * BLK, :].rearrange("n (t p) c -> p (n t) c", p=P),
                             ao[:]).then_inc(s["ao_stored"], 16)

            def unit(n, slot, it):
                static = isinstance(n, int)
                if not static or n + 2 < NU:
                    sp.wait_ge(s["pv_done"], ONE + n * NST)
                    load(n + 2, (slot + 2) % SLOTS)
                for qb in range(QB - 1):
                    store(n, qb)
                if not static or n + 1 < NU:
                    rows(n + 1, (slot + 1) % SLOTS)
                store(n, QB - 1)

            for n in range(2):
                load(n, n)
            rows(0, 0)
            units(sp, unit)
            sp.wait_ge(s["ao_stored"], ONE + 16 * NU * QB)

        def turn_base(n):
            return n * TURNS + FIRST

        @block.tensor
        def _(pe):
            def ring(number, index):
                above(pe, s["turn_taken"], number - (RING - 1))
                return p_ring[index % RING]

            def take_max(number, index, piece, slot):
                _, h, qt, kb = piece
                bank = ring(number, index)
                n = min(BLK, (qt + 1) * P - kb * BLK)
                diagonal = kb == qt // STEP
                last = nc.tensor.matmul(bank[:, 0:n], q[slot][0:KS_ROWS, h, qt * P:(qt + 1) * P],
                                        k[slot][0:KS_ROWS, h, kb * BLK:kb * BLK + n], start=True, stop=not diagonal)
                if diagonal:
                    last = nc.tensor.matmul(bank[:, n - P:n], identb[:], mask_rows[:], start=False, stop=True)
                last.then_inc(s["turn_ready"], 1)

            def turn_maxima(number, index, n):
                bank = ring(number, index)
                pe.wait_ge(s["row_max_ready"], ONE + n + 1)
                nc.tensor.transpose(bank[:, 0:P], row_max[:], ident[:]).then_inc(s["turn_ready"], 1)

            def turn_output(number, index, n, qb):
                bank = ring(number, index)
                pe.wait_ge(s["out_copied"], ONE + n * QB + qb + 1)
                for t in range(STEP):
                    last = nc.tensor.transpose(bank[:, t * P:(t + 1) * P], out_t[:, t * P:(t + 1) * P], ident[:])
                last.then_inc(s["turn_ready"], 1)

            def scores(n, slot, i, between):
                qb, kt = steps[i]
                off = P * max(0, kt - STEP * qb)
                for pair in range(2):
                    if pair:
                        between()
                    above(pe, s["prob_ready"], n * 2 * NST + max(2 * i + pair - 1, 0))
                    for j in range(2):
                        h = 2 * pair + j
                        diagonal = kt >= STEP * qb
                        last = nc.tensor.matmul(p_s[pair][:, j, off:BLK], k[slot][0:KS_ROWS + M_ROWS, h, kt * P:(kt + 1) * P],
                                                q[slot][0:KS_ROWS + M_ROWS, h, qb * BLK + off:(qb + 1) * BLK],
                                                start=True, stop=not diagonal)
                        if diagonal:
                            last = nc.tensor.matmul(p_s[pair][:, j, off:off + P], identb[:], mask_cols[:], start=False, stop=True)
                    last.then_inc(s["s_ready"], 1)

            def weigh_values(n, slot, i):
                qb, kt = steps[i]
                off = P * max(0, kt - STEP * qb)
                pe.wait_ge(s["prob_ready"], ONE + n * 2 * NST + 2 * i + 2)
                if kt == 0:
                    above(pe, s["out_copied"], n * QB + qb)
                for h in range(HG):
                    last = nc.tensor.matmul(p_o[32 * h:32 * h + 32, off:BLK], v[slot][:, kt, h, :], prob[i % 2][:, h, off:BLK],
                                            start=kt == 0, stop=kt == STEP * qb + STEP - 1)
                last.then_inc(s["pv_done"], 1)
                return kt == STEP * qb + STEP - 1

            def unit(n, slot, it):
                last_unit = isinstance(n, int) and n == NU - 1
                nxt = (slot + 1) % SLOTS
                if not last_unit:
                    pe.wait_ge(loaded[nxt], ONE + (it + (nxt == 0)) * 16 * N_LOADS + 16 * N_LOADS)
                pe.wait_ge(s["m_loaded"], ONE + n * 16 * M_ROWS + 16 * M_ROWS)
                base, count = turn_base(n), 0
                def take_turns(of_step):
                    nonlocal count
                    for turn in of_step:
                        if turn[0] == "o":
                            turn_output(base + count, FIRST + count, n, turn[1])
                        elif last_unit:
                            continue
                        elif turn[0] == "m":
                            turn_maxima(base + count, FIRST + count, n + 1)
                        else:
                            take_max(base + count, FIRST + count, turn, nxt)
                        count += 1

                for i in range(NST):
                    a, b = (len(turns[i]) + 1) // 3, (2 * len(turns[i]) + 1) // 3
                    scores(n, slot, i, lambda: take_turns(turns[i][:a]))
                    take_turns(turns[i][a:b])
                    if i:
                        weigh_values(n, slot, i - 1)
                    take_turns(turns[i][b:])
                weigh_values(n, slot, NST - 1)
                turn_output(base + count, FIRST + count, n, QB - 1)

            pe.wait_ge(s["ident_loaded"], ONE + 16)
            pe.wait_ge(s["made"], ONE + 3)
            pe.wait_ge(loaded[0], ONE + 16 * N_LOADS)
            for c, piece in enumerate(pieces):
                take_max(c, c, piece, 0)
            turn_maxima(FIRST - 1, FIRST - 1, 0)
            pe.wait_ge(s["ones_set"], ONE + SLOTS)
            units(pe, unit)

        @block.scalar
        def _(act):
            def first_part(n):
                if isinstance(n, int) and n == 0:
                    act.wait_ge(s["turn_ready"], ONE + FIRST)
                    b = (FIRST - 1) % RING
                else:
                    act.wait_ge(s["turn_ready"], ONE + turn_base(n - 1) + M_TURN + 1)
                    act.wait_ge(s["m_loaded"], ONE + n * 16 * M_ROWS)
                    b = (FIRST + M_TURN) % RING
                nc.scalar.mul(m_rows[:, 0, :], p_ring[b][0:HG * QT, 0:P], -1.0).then_inc(s["m_first"], 1)

            flat_turns = [t for ts in turns for t in ts]
            M_TURN = flat_turns.index(("m",))

            def copy_out(n, qb, i):
                act.wait_ge(s["pv_done"], ONE + n * NST + i + 1)
                above(act, s["ao_ready"], n * QB + qb)
                nc.scalar.copy(out_t[:], p_o[:]).then_inc(s["out_copied"], 1)

            def unit(n, slot, it):
                last_unit = isinstance(n, int) and n == NU - 1
                for i, (qb, kt) in enumerate(steps):
                    off = P * max(0, kt - STEP * qb)
                    for pair in range(2):
                        act.wait_ge(s["s_ready"], ONE + n * 2 * NST + 2 * i + pair + 1)
                        above(act, s["pv_done"], n * NST + max(i - 1, 0))
                        nc.scalar.activation(prob[i % 2][:, 2 * pair:2 * pair + 2, off:BLK], p_s[pair][:, :, off:BLK],
                                             ACT.Exp).then_inc(s["prob_ready"], 1)
                    if i - 1 in ends:
                        copy_out(n, ends.index(i - 1), i - 1)
                    if ("m",) in turns[i] and not last_unit:
                        first_part(n + 1)
                copy_out(n, QB - 1, NST - 1)

            first_part(0)
            units(act, unit)

        @block.vector
        def _(dve):
            def take_max(number, index, piece):
                _, h, qt, kb = piece
                n = min(BLK, (qt + 1) * P - kb * BLK)
                dve.wait_ge(s["turn_ready"], ONE + number + 1)
                nc.vector.reduce_max(part_max[:, h * QT + qt, kb:kb + 1], p_ring[index % RING][:, 0:n], axis=AX.X).then_inc(s["turn_taken"], 1)

            def maxima(number, n):
                dve.wait_ge(s["turn_taken"], ONE + number)
                nc.vector.reduce_max(row_max[:, 0:HG * QT], part_max[:], axis=AX.X).then_inc(s["row_max_ready"], 1)

            def split_maxima(number, index, n):
                dve.wait_ge(s["m_first"], ONE + n + 1)
                bank = p_ring[index % RING][0:HG * QT, 0:P]
                nc.vector.scalar_tensor_tensor(m_rest[:], bank, -1.0, m_rows[:, 0, :], ALU.mult, ALU.subtract).then_inc(s["turn_taken"], 1)
                dve.wait_ge(s["turn_taken"], ONE + number + 1)
                nc.vector.tensor_copy(m_rows[:, 1, :], m_rest[:]).then_inc(s["m_steps"], 1)
                dve.wait_ge(s["m_steps"], ONE + n + 1)
                nc.vector.tensor_tensor(m_rows[:, 2, :], m_rest[:], m_rows[:, 1, :], ALU.subtract).then_inc(s["m_ready"], 1)

            def normalise(number, index, n, qb):
                dve.wait_ge(s["turn_ready"], ONE + number + 1)
                bank = p_ring[index % RING][:].rearrange("p (t h c) -> p t h c", t=STEP, h=HG)
                nc.vector.reciprocal(recip[:], bank[:, :, :, DK]).then_inc(s["ao_steps"], 1)
                above(dve, s["ao_stored"], (n * QB + qb) * 16)
                dve.wait_ge(s["ao_steps"], ONE + n * QB + qb + 1)
                nc.vector.tensor_tensor(ao[:].rearrange("p t (h c) -> p t h c", h=HG), bank[:, :, :, 0:DK],
                                        recip[:].unsqueeze(3).to_broadcast([P, STEP, HG, DK]), ALU.mult).then_inc(s["turn_taken"], 1)
                dve.wait_ge(s["turn_taken"], ONE + number + 1)
                nc.vector.memset(gate[:], 0.0).then_inc(s["ao_ready"], 1)

            def unit(n, slot, it):
                last_unit = isinstance(n, int) and n == NU - 1
                base, count = turn_base(n), 0
                for i in range(NST):
                    for turn in turns[i]:
                        if turn[0] == "o":
                            normalise(base + count, FIRST + count, n, turn[1])
                        elif last_unit:
                            continue
                        elif turn[0] == "m":
                            maxima(base + count, n + 1)
                            split_maxima(base + count, FIRST + count, n + 1)
                        else:
                            take_max(base + count, FIRST + count, turn)
                        count += 1
                normalise(base + count, FIRST + count, n, QB - 1)

            gate = sb("gate", [P, 1])
            dve.wait_ge(s["ident_loaded"], ONE + 16)
            nc.vector.tensor_copy(identb[:], ident[:]).then_inc(s["made"], 1)
            nc.vector.memset(row_max[:], 0.0)
            nc.vector.memset(part_max[:], NEG).then_inc(s["floor_set"], 1)
            dve.wait_ge(s["floor_set"], ONE + 1)
            for c, piece in enumerate(pieces):
                take_max(c, c, piece)
            maxima(FIRST - 1, 0)
            split_maxima(FIRST - 1, FIRST - 1, 0)
            units(dve, unit)


def attention_output(nc, sem, x_dram, y_dram, ao_dram, ident_dram, W_o):
    with ExitStack() as ctx:
        def pair(name, shape):
            return [ctx.enter_context(nc.sbuf_tensor(f"ao_{name}{u}", shape, F32)) for u in range(2)]

        NG_ = AH // HG
        ident, wo = (ctx.enter_context(nc.sbuf_tensor("ao_" + n, sh, F32)) for n, sh in (("ident", [P, P]), ("wo", [P, DH, D])))
        rows, rows_t, x, y = pair("rows", [P, 2, NG_, GD]), pair("rows_t", [P, DH, CH]), pair("x", [P, 2, D]), pair("y", [P, 2, D])
        p_t = [ctx.enter_context(nc.psum_tensor(f"ao_p_t{u}", [P, DH, CH], F32)) for u in range(2)]
        p_y = [ctx.enter_context(nc.psum_tensor(f"ao_p_y{u}", [P, 2, D], F32)) for u in range(2)]
        consts = sem("ao_consts")
        rows_loaded, x_loaded, turned, copied, summed, y_ready, y_stored = (
            [sem(f"ao_{n}{u}") for u in range(2)] for n in ("rows_loaded", "x_loaded", "turned", "copied", "summed", "y_ready", "y_stored"))
        n_it = SEQ // CH // 2
        xin, yout = (d.rearrange("(n p) d -> p n d", p=P) for d in (x_dram, y_dram))
        block = ctx.enter_context(nc.Block())

        @block.sync
        def _(sp):
            sp.dma_start(ident[:], ident_dram).then_inc(consts, 16)
            sp.dma_start(wo[:], W_o.rearrange("(h p) d -> p h d", p=P)).then_inc(consts, 16)
            def load_rows(u, b, j):
                for t in range(2):
                    src = ao_dram[bass.ds(b * NG_, NG_), bass.ds(((j * 2 + u) * 2 + t) * P, P), :].rearrange("g p c -> p g c")
                    sp.dma_start(rows[u][:, t, :, :], src).then_inc(rows_loaded[u], 16)

            def load_x(u, i):
                sp.dma_start(x[u][:], xin[:, bass.ds(i * 4 + u * 2, 2), :]).then_inc(x_loaded[u], 16)

            def next_rows(u, i, b, j):
                sp.wait_ge(turned[u], ONE + i + 1)
                load_rows(u, b, j)

            def finish(u, i, last=False):
                sp.wait_ge(y_ready[u], ONE + i + 1)
                if not last:
                    load_x(u, i + 1)
                sp.dma_start(yout[:, bass.ds(i * 4 + u * 2, 2), :], y[u][:]).then_inc(y_stored[u], 16)

            def step(i, first, second):
                next_rows(1, i, *first)
                finish(0, i)
                next_rows(0, i + 1, *second)
                finish(1, i)

            for u in range(2):
                load_rows(u, 0, 0)
                load_x(u, 0)
            next_rows(0, 0, 0, 1)
            for b in range(BATCH):
                with sp.Fori(0, n_it - 2) as j:
                    step(b * n_it + j, (b, j + 1), (b, j + 2))
                if b + 1 < BATCH:
                    step(b * n_it + n_it - 2, (b, n_it - 1), (b + 1, 0))
                    step(b * n_it + n_it - 1, (b + 1, 0), (b + 1, 1))
            next_rows(1, BATCH * n_it - 2, BATCH - 1, n_it - 1)
            for i in (BATCH * n_it - 2, BATCH * n_it - 1):
                for u in range(2):
                    finish(u, i, last=i == BATCH * n_it - 1)
            for u in range(2):
                sp.wait_ge(y_stored[u], ONE + 16 * BATCH * n_it)

        @block.tensor
        def _(pe):
            def turn(u, i):
                pe.wait_ge(rows_loaded[u], ONE + i * 32 + 32)
                pe.wait_ge(copied[u], ONE + i)
                for h in range(DH):
                    for t in range(2):
                        last = nc.tensor.transpose(p_t[u][:, h, t * P:(t + 1) * P],
                                                   rows[u][:, t, :, :].rearrange("p g c -> p (g c)")[:, h * P:(h + 1) * P], ident[:])
                last.then_inc(turned[u], 1)

            def product(u, i):
                pe.wait_ge(copied[u], ONE + i + 1)
                pe.wait_ge(y_ready[u], ONE + i)
                for t in range(2):
                    for h in range(DH):
                        last = nc.tensor.matmul(p_y[u][:, t, :], rows_t[u][:, h, t * P:(t + 1) * P], wo[:, h, :],
                                                start=h == 0, stop=h == DH - 1)
                last.then_inc(summed[u], 1)

            pe.wait_ge(consts, ONE + 32)
            turn(0, 0)
            with pe.Fori(0, BATCH * n_it - 1) as i:
                turn(1, i)
                product(0, i)
                turn(0, i + 1)
                product(1, i)
            turn(1, BATCH * n_it - 1)
            product(0, BATCH * n_it - 1)
            product(1, BATCH * n_it - 1)

        @block.scalar
        def _(act):
            with act.Fori(0, BATCH * n_it) as i:
                for u in range(2):
                    act.wait_ge(turned[u], ONE + i + 1)
                    act.wait_ge(summed[u], ONE + i)
                    nc.scalar.copy(rows_t[u][:], p_t[u][:]).then_inc(copied[u], 1)

        @block.vector
        def _(dve):
            with dve.Fori(0, BATCH * n_it) as i:
                for u in range(2):
                    dve.wait_ge(summed[u], ONE + i + 1)
                    dve.wait_ge(x_loaded[u], ONE + i * 16 + 16)
                    dve.wait_ge(y_stored[u], ONE + i * 16)
                    nc.vector.tensor_tensor(y[u][:], p_y[u][:], x[u][:], ALU.add).then_inc(y_ready[u], 1)


def attention(nc, sem, x_dram, y_dram, xt_dram, qk_dram, v_dram, ao_dram, ident_dram, W_dq, W_uq, W_dkv, W_uk, W_uv, W_o):
    with ExitStack() as ctx:
        layer_norm_pass(nc, sem, "aa_ln_", x_dram, xt_dram, ident_dram)
        attention_project(nc, sem, xt_dram, qk_dram, v_dram, W_dq, W_dkv, W_uq, W_uk, W_uv)
        attention_units(nc, sem, qk_dram, v_dram, ao_dram, ident_dram)
        attention_output(nc, sem, x_dram, y_dram, ao_dram, ident_dram, W_o)


class StageSemaphores:

    def __init__(self, nc):
        self.nc, self.sems = nc, []

    def __enter__(self):
        return self.sem

    def sem(self, name):
        self.sems.append(self.nc.alloc_semaphore(name=name))
        self.nc.sync.sem_inc(self.sems[-1], ONE)
        return self.sems[-1]

    def __exit__(self, kind, value, trace):
        if kind is None:
            self.nc.all_engine_barrier()
            self.nc.clear_and_free_semaphores(self.sems)
            self.nc.all_engine_barrier()


def hybrid_block(nc, a, out):
    def scratch(name, shape, dt=F32):
        return nc.dram_tensor(name, shape, dt, kind="Internal").ap()

    x = a["L0_attn_a_x"].rearrange("b s d -> (b s) d")
    y = out.rearrange("b s d -> (b s) d")
    x1, x2, x3, xln = (scratch(n, (T, D)) for n in ("x1", "x2", "x3", "xln"))
    xt = scratch("xt", (NCH, P, DH, CH))
    ident = scratch("ident", (P, P))
    wct, kin = scratch("wct", (P, DH, NSUB)), scratch("kin_t", (P, 2, DH, NE), F16)
    qk = scratch("qk", (2, 3, BATCH * D, SEQ), BF16)
    v = scratch("v", (NU, P, QT * HG * 32))
    ao = scratch("attn_rows", (NU, SEQ, GD))

    def m(name):
        return a["L0_attn_a_" + name]

    def b(name):
        return a["L0_attn_b_" + name]

    def f(name):
        return a["L0_ffn_" + name]

    with StageSemaphores(nc) as sem:
        product_key_prepare(nc, sem, ident, f("w_q"), f("keys"), f("key_in"), wct, kin)
    with StageSemaphores(nc) as sem:
        neural_memory(nc, sem, x, x1, xln, xt, ident, m("Wk"), m("Wv"), m("Wq"), m("Wout"), m("W0"), m("W1"),
                      [m("Wg_decay"), m("Wg_lr"), m("Wg_mom")], [m("bg_decay"), m("bg_lr"), m("bg_mom")])
    with StageSemaphores(nc) as sem:
        product_key_memory(nc, sem, "f1_", x1, x2, xt, ident, wct, kin, f("key_out"), f("gamma"), f("beta"))
    with StageSemaphores(nc) as sem:
        attention(nc, sem, x2, x3, xt, qk, v, ao, ident, b("W_dq"), b("W_uq"), b("W_dkv"), b("W_uk"), b("W_uv"), b("W_o"))
    with StageSemaphores(nc) as sem:
        product_key_memory(nc, sem, "f2_", x3, y, xt, ident, wct, kin, f("key_out"), f("gamma"), f("beta"))


def kernel(**inputs):
    import numpy as _np
    import concourse.bacc as _bacc
    from concourse import mybir as _mybir
    from concourse.bass_utils import run_bass_kernel_spmd as _run

    nc = _bacc.Bacc("TRN2", target_bir_lowering=False, num_devices=1)
    arrays, aps = {}, {}
    for name, value in inputs.items():
        a = _np.ascontiguousarray(value)
        arrays[f"in_{name}"] = a
        aps[name] = nc.dram_tensor(f"in_{name}", a.shape, _mybir.dt.from_np(a.dtype), kind="ExternalInput").ap()
    out = nc.dram_tensor("out", (BATCH, SEQ, D), F32, kind="ExternalOutput").ap()
    hybrid_block(nc, aps, out)
    r = _run(nc, [arrays], core_ids=[0])
    return r.results[0]["out"]
```
